# Optimizing a Trainium2 kernel written in Bass

```python
import numpy as np
import jax
import jax.numpy as jnp

def _softmax(x, axis=-1):
    return jax.nn.softmax(x, axis=axis)

def _gelu(x):
    return jax.nn.gelu(x, approximate=True)

def _silu(x):
    return jax.nn.silu(x)

def _sigmoid(x):
    return jax.nn.sigmoid(x)

def _layernorm(x, axis=-1, eps=1e-05):
    m = jnp.mean(x, axis=axis, keepdims=True)
    v = jnp.var(x, axis=axis, keepdims=True)
    return (x - m) / jnp.sqrt(v + eps)

def _scatter_add(tgt, idx, src, axis=0):
    return tgt.at[idx].add(src)

def _segment_sum(src, seg, n):
    return jax.ops.segment_sum(src, seg, n)
kernel_name = 'mk_seq_postln_d1_jaxref_r4_cd425a'

def setup_inputs(seed: int=0):
    np.random.seed(seed)
    _w = jnp.asarray

    def _L0_attn_setup():
        import jax, jax.numpy as jnp
        import numpy as np
        D_MODEL = 256
        N_LAYERS = 2
        D_STATE = 64
        D_CONV = 4
        EXPAND = 2
        D_INNER = EXPAND * D_MODEL
        HEADDIM = D_STATE
        NHEADS = D_INNER // HEADDIM
        CONV_DIM = D_INNER + 2 * D_STATE
        D_IN_PROJ = 2 * D_INNER + 2 * D_STATE + NHEADS
        EPS = 1e-05

        def _layernorm(x, w, b):
            m = x.mean(-1, keepdims=True)
            v = ((x - m) ** 2).mean(-1, keepdims=True)
            return (x - m) * jax.lax.rsqrt(v + EPS) * w + b

        def _mamba2(u, in_w, conv_w, conv_b, dt_bias, A_log, Dp, rms_w, out_w):
            b, l, _ = u.shape
            zxbcdt = u @ in_w.T
            z, xBC, dt = jnp.split(zxbcdt, [D_INNER, D_INNER + CONV_DIM], axis=-1)
            dt = jax.nn.softplus(dt + dt_bias)
            xBC = jnp.transpose(xBC, (0, 2, 1))
            xBC = jax.lax.conv_general_dilated(xBC, conv_w[:, None, :], (1,), [(D_CONV - 1, 0)], dimension_numbers=('NCH', 'OIH', 'NCH'), feature_group_count=CONV_DIM)
            xBC = jnp.transpose(xBC, (0, 2, 1)) + conv_b
            xBC = jax.nn.silu(xBC)
            xh, Bm, Cm = jnp.split(xBC, [D_INNER, D_INNER + D_STATE], axis=-1)
            xh = xh.reshape(b, l, NHEADS, HEADDIM)
            A = -jnp.exp(A_log)
            dA = jnp.exp(dt * A)

            def step(state, inputs):
                dA_t, dt_t, x_t, B_t, C_t = inputs
                state = dA_t[:, :, None, None] * state + (dt_t[:, :, None] * x_t)[..., None] * B_t[:, None, None, :]
                y_t = jnp.einsum('bhpn,bn->bhp', state, C_t)
                return (state, y_t)
            xs = (jnp.moveaxis(dA, 1, 0), jnp.moveaxis(dt, 1, 0), jnp.moveaxis(xh, 1, 0), jnp.moveaxis(Bm, 1, 0), jnp.moveaxis(Cm, 1, 0))
            init = jnp.zeros((b, NHEADS, HEADDIM, D_STATE), u.dtype)
            _, ys = jax.lax.scan(step, init, xs)
            y = jnp.moveaxis(ys, 0, 1) + Dp[None, None, :, None] * xh
            y = y.reshape(b, l, D_INNER)
            y = y * jax.nn.silu(z)
            y = y * jax.lax.rsqrt(jnp.mean(y * y, -1, keepdims=True) + EPS) * rms_w
            return y @ out_w.T
        key = jax.random.key(seed)
        ks = jax.random.split(key, 8)
        B, L = (2, 1024)
        return {'x': jax.random.normal(ks[0], (B, L, D_MODEL), jnp.float32), 'ln_w': jnp.ones((N_LAYERS, D_MODEL), jnp.float32), 'ln_b': jnp.zeros((N_LAYERS, D_MODEL), jnp.float32), 'in_proj_w': jax.random.normal(ks[1], (N_LAYERS, D_IN_PROJ, D_MODEL), jnp.float32) * D_MODEL ** (-0.5), 'conv_w': jax.random.normal(ks[2], (N_LAYERS, CONV_DIM, D_CONV), jnp.float32) * D_CONV ** (-0.5), 'conv_b': jnp.zeros((N_LAYERS, CONV_DIM), jnp.float32), 'dt_bias': jax.random.normal(ks[3], (N_LAYERS, NHEADS), jnp.float32) * 0.5, 'A_log': jnp.log(jax.random.uniform(ks[4], (N_LAYERS, NHEADS), jnp.float32, 1.0, 16.0)), 'D': jnp.ones((N_LAYERS, NHEADS), jnp.float32), 'rms_w': jnp.ones((N_LAYERS, D_INNER), jnp.float32), 'out_proj_w': jax.random.normal(ks[5], (N_LAYERS, D_MODEL, D_INNER), jnp.float32) * D_INNER ** (-0.5)}
    _L0_attn_in = _L0_attn_setup()

    def _L0_ffn_setup():
        import jax, jax.numpy as jnp
        import numpy as np
        D_MODEL = 256
        NUM_EXPERTS = 8
        TOP_K = 2
        B, S = (1, 512)
        key = jax.random.key(seed)
        ks = jax.random.split(key, 8)
        sd = 1.0 / np.sqrt(D_MODEL)
        x = jax.random.normal(ks[0], (B, S, D_MODEL), dtype=jnp.float32)
        gate_w = jax.random.normal(ks[1], (D_MODEL, NUM_EXPERTS), dtype=jnp.float32) * sd
        gate_b = jnp.zeros((NUM_EXPERTS,), dtype=jnp.float32)
        w1 = jax.random.normal(ks[2], (NUM_EXPERTS, D_MODEL, 8 * D_MODEL), dtype=jnp.float32) * sd
        b1 = jnp.zeros((NUM_EXPERTS, 8 * D_MODEL), dtype=jnp.float32)
        w2 = jax.random.normal(ks[3], (NUM_EXPERTS, 4 * D_MODEL, D_MODEL), dtype=jnp.float32) * (1.0 / np.sqrt(4 * D_MODEL))
        b2 = jnp.zeros((NUM_EXPERTS, D_MODEL), dtype=jnp.float32)
        return {'x': x, 'gate_w': gate_w, 'gate_b': gate_b, 'w1': w1, 'b1': b1, 'w2': w2, 'b2': b2}
    _L0_ffn_in = _L0_ffn_setup()
    _d = {'L0_attn_x': _L0_attn_in['x'], 'L0_attn_ln_w': _L0_attn_in['ln_w'], 'L0_attn_ln_b': _L0_attn_in['ln_b'], 'L0_attn_in_proj_w': _L0_attn_in['in_proj_w'], 'L0_attn_conv_w': _L0_attn_in['conv_w'], 'L0_attn_conv_b': _L0_attn_in['conv_b'], 'L0_attn_dt_bias': _L0_attn_in['dt_bias'], 'L0_attn_A_log': _L0_attn_in['A_log'], 'L0_attn_D': _L0_attn_in['D'], 'L0_attn_rms_w': _L0_attn_in['rms_w'], 'L0_attn_out_proj_w': _L0_attn_in['out_proj_w'], 'L0_ffn_gate_w': _L0_ffn_in['gate_w'], 'L0_ffn_gate_b': _L0_ffn_in['gate_b'], 'L0_ffn_w1': _L0_ffn_in['w1'], 'L0_ffn_b1': _L0_ffn_in['b1'], 'L0_ffn_w2': _L0_ffn_in['w2'], 'L0_ffn_b2': _L0_ffn_in['b2']}
    _x0 = _d['L0_attn_x']
    _d['L0_attn_x'] = jax.random.normal(jax.random.fold_in(jax.random.key(seed), 1), (8, 512, 256), dtype=_x0.dtype)
    del _x0
    return _d

def reference(L0_attn_x, L0_attn_ln_w, L0_attn_ln_b, L0_attn_in_proj_w, L0_attn_conv_w, L0_attn_conv_b, L0_attn_dt_bias, L0_attn_A_log, L0_attn_D, L0_attn_rms_w, L0_attn_out_proj_w, L0_ffn_gate_w, L0_ffn_gate_b, L0_ffn_w1, L0_ffn_b1, L0_ffn_w2, L0_ffn_b2):

    def _L0_attn_ref(x, ln_w, ln_b, in_proj_w, conv_w, conv_b, dt_bias, A_log, D, rms_w, out_proj_w):
        import jax, jax.numpy as jnp
        import numpy as np
        D_MODEL = 256
        N_LAYERS = 2
        D_STATE = 64
        D_CONV = 4
        EXPAND = 2
        D_INNER = EXPAND * D_MODEL
        HEADDIM = D_STATE
        NHEADS = D_INNER // HEADDIM
        CONV_DIM = D_INNER + 2 * D_STATE
        D_IN_PROJ = 2 * D_INNER + 2 * D_STATE + NHEADS
        EPS = 1e-05

        def _layernorm(x, w, b):
            m = x.mean(-1, keepdims=True)
            v = ((x - m) ** 2).mean(-1, keepdims=True)
            return (x - m) * jax.lax.rsqrt(v + EPS) * w + b

        def _mamba2(u, in_w, conv_w, conv_b, dt_bias, A_log, Dp, rms_w, out_w):
            b, l, _ = u.shape
            zxbcdt = u @ in_w.T
            z, xBC, dt = jnp.split(zxbcdt, [D_INNER, D_INNER + CONV_DIM], axis=-1)
            dt = jax.nn.softplus(dt + dt_bias)
            xBC = jnp.transpose(xBC, (0, 2, 1))
            xBC = jax.lax.conv_general_dilated(xBC, conv_w[:, None, :], (1,), [(D_CONV - 1, 0)], dimension_numbers=('NCH', 'OIH', 'NCH'), feature_group_count=CONV_DIM)
            xBC = jnp.transpose(xBC, (0, 2, 1)) + conv_b
            xBC = jax.nn.silu(xBC)
            xh, Bm, Cm = jnp.split(xBC, [D_INNER, D_INNER + D_STATE], axis=-1)
            xh = xh.reshape(b, l, NHEADS, HEADDIM)
            A = -jnp.exp(A_log)
            dA = jnp.exp(dt * A)

            def step(state, inputs):
                dA_t, dt_t, x_t, B_t, C_t = inputs
                state = dA_t[:, :, None, None] * state + (dt_t[:, :, None] * x_t)[..., None] * B_t[:, None, None, :]
                y_t = jnp.einsum('bhpn,bn->bhp', state, C_t)
                return (state, y_t)
            xs = (jnp.moveaxis(dA, 1, 0), jnp.moveaxis(dt, 1, 0), jnp.moveaxis(xh, 1, 0), jnp.moveaxis(Bm, 1, 0), jnp.moveaxis(Cm, 1, 0))
            init = jnp.zeros((b, NHEADS, HEADDIM, D_STATE), u.dtype)
            _, ys = jax.lax.scan(step, init, xs)
            y = jnp.moveaxis(ys, 0, 1) + Dp[None, None, :, None] * xh
            y = y.reshape(b, l, D_INNER)
            y = y * jax.nn.silu(z)
            y = y * jax.lax.rsqrt(jnp.mean(y * y, -1, keepdims=True) + EPS) * rms_w
            return y @ out_w.T
        h = x
        for i in range(N_LAYERS):
            res = h
            h = _layernorm(h, ln_w[i], ln_b[i])
            h = _mamba2(h, in_proj_w[i], conv_w[i], conv_b[i], dt_bias[i], A_log[i], D[i], rms_w[i], out_proj_w[i])
            h = h + res
        return h

    def _L0_ffn_ref(x, gate_w, gate_b, w1, b1, w2, b2):
        import jax, jax.numpy as jnp
        import numpy as np
        D_MODEL = 256
        NUM_EXPERTS = 8
        TOP_K = 2
        B, S = (1, 512)
        gate_logits = jnp.einsum('bsd,de->bse', x, gate_w) + gate_b
        weights, indices = jax.lax.top_k(gate_logits, TOP_K)
        weights = jax.nn.softmax(weights, axis=-1)
        h = jnp.einsum('bsd,edh->ebsh', x, w1) + b1[:, None, None, :]
        xh, gh = jnp.split(h, 2, axis=-1)
        act = jax.nn.silu(gh) * xh
        out_e = jnp.einsum('ebsf,efd->ebsd', act, w2) + b2[:, None, None, :]
        out_e = jnp.transpose(out_e, (1, 2, 0, 3))
        sel = jnp.take_along_axis(out_e, indices[..., None], axis=2)
        return jnp.sum(sel * weights[..., None], axis=2)
    x = L0_attn_x
    x = _layernorm(x + _L0_attn_ref(x, L0_attn_ln_w, L0_attn_ln_b, L0_attn_in_proj_w, L0_attn_conv_w, L0_attn_conv_b, L0_attn_dt_bias, L0_attn_A_log, L0_attn_D, L0_attn_rms_w, L0_attn_out_proj_w), axis=-1)
    x = _layernorm(x + _L0_ffn_ref(x, L0_ffn_gate_w, L0_ffn_gate_b, L0_ffn_w1, L0_ffn_b1, L0_ffn_w2, L0_ffn_b2), axis=-1)
    return x

_drawn_inputs = setup_inputs


def setup_inputs(seed=0):
    import zlib

    import numpy as np

    out = dict(_drawn_inputs(seed))
    spreads = {'L0_attn_ln_w': (1.0, 0.2),
     'L0_attn_ln_b': (0.0, 0.1),
     'L0_attn_conv_b': (0.0, 0.1),
     'L0_attn_D': (1.0, 0.2),
     'L0_attn_rms_w': (1.0, 0.2),
     'L0_ffn_gate_b': (0.0, 0.1),
     'L0_ffn_b1': (0.0, 0.1),
     'L0_ffn_b2': (0.0, 0.1)}
    factors = {}
    for name, (base, spread) in spreads.items():
        noise = np.random.default_rng([zlib.crc32(name.encode()), seed]).standard_normal(out[name].shape)
        drawn = base * np.exp(spread * noise) if base else spread * noise
        out[name] = jnp.asarray(drawn.astype(out[name].dtype))
    for name, factor in factors.items():
        out[name] = (out[name] * factor).astype(out[name].dtype)
    return out
```

```python
from contextlib import ExitStack

import concourse.bass as bass
from concourse import mybir

F32 = mybir.dt.float32
I32 = mybir.dt.int32
U32 = mybir.dt.uint32
ALU = mybir.AluOpType
ACT = mybir.ActivationFunctionType
AX = mybir.AxisListType

P = 128
NB, T, D = 8, 512, 256
NK = T // P
KD = D // P
NH, HD, DS = 8, 64, 64
DI = NH * HD
NCT = DI // P
NC = NCT + 1
TAPS = 4
DPROJ = 2 * DI + 2 * DS + NH
OX, OBC, ODT = DI, 2 * DI, 2 * DI + 2 * DS
EPS = 1e-5
NE, FF = 8, 1024
NF = FF // P
NTOK = NB * T
NTILE = NTOK // P
WEX = KD * 2 * FF + NF * D + 2 * NF
QROWS = NTOK + P
DUMMY = NE * QROWS
WB = 3
NJ = (2 * NTOK) // P + NE - 1
NJ += -NJ % WB
NJT = NJ + WB
LG = NK

PLAIN = ["ln0", "ln1", "dt", "c4", "c0", "c1", "c2", "c3", "z0", "z1", "z2", "z3"]
WITH3 = ["ln0", "ln1", "dt", "c4", "c0", "t0", "t1", "c1", "c2", "lg", "c3", "z0", "z1", "rk", "z2", "z3"]
ONLY3 = ["t0", "t1", "lg", "rk"]
PAIRS = ["a0", "a1", "o0", "a2", "o1", "a3", "o2", "o3"]
CONV_ORDER = ["c4", "c0", "c1", "c2", "c3"]
MAMBA_UNITS = 2 * NB


def at_least(eng, sem, count):
    if isinstance(count, int) and count <= 0:
        return
    eng.wait_ge(sem, count)


class Chain:

    def __init__(self, eng, sem, per, unit):
        self.eng, self.sem, self.base, self.per, self.n = eng, sem, per * unit, per, 0

    def link(self, ins):
        self.n += 1
        ins.then_inc(self.sem, 1)
        self.eng.wait_ge(self.sem, self.base + self.n)

    def close(self):
        assert self.n == self.per, (self.n, self.per)


class Step:

    def __init__(self, u, half, layer, parity, fills, half_base, first=False, last=False, s3=False):
        self.u, self.h, self.layer, self.q = u, half, layer, parity
        self.fills, self.hb = fills, half_base
        self.first, self.last, self.s3 = first, last, s3
        self.next_layer = 1 if (layer == 1 or (isinstance(u, int) and u == NB - 1)) else 0

    def fill(self, name):
        p = self.fills.index(name)
        return p % 2, self.hb + p // 2


def schedule(eng, body, prologue, epilogue):
    prologue(Step(-1, -1, 0, 1, PLAIN, 0))
    body(Step(0, 0, 0, 0, PLAIN, 6, first=True))
    with eng.Fori(0, 3) as i:
        for r in range(2):
            body(Step(2 * i + (1 + r), i + r, 0, (1 + r) % 2, PLAIN, 6 * (2 * i) + (12 + 6 * r)))
    body(Step(7, 3, 0, 1, PLAIN, 48))
    body(Step(8, 4, 1, 0, PLAIN, 54))
    with eng.Fori(0, 3) as i:
        for r in range(2):
            body(Step(2 * i + (9 + r), i + (4 + r), 1, (1 + r) % 2, WITH3, 16 * i + (60 + 8 * r), s3=True))
    body(Step(15, 7, 1, 1, ONLY3, 108, last=True, s3=True))
    epilogue(Step(16, 8, 1, 0, ONLY3, 110, s3=True))


def build(nc, x, w_in, conv_w, conv_b, ln_w, ln_b, dt_bias, a_log, d_skip, rms_w, w_out,
          gate_w, gate_b, w_exp, b2, out):
    h1 = nc.dram_tensor("h1", [NB, T, D], F32, kind="Internal").ap()
    x1_rows = nc.dram_tensor("x1_rows", [NTOK, D], F32, kind="Internal").ap()
    queue = nc.dram_tensor("queue", [DUMMY + 4 * P, D], F32, kind="Internal").ap()
    answer = nc.dram_tensor("answer", [NJ * P, D], F32, kind="Internal").ap()

    ctx = ExitStack()
    with ctx:
        def sb(name, shape, dt=F32):
            return ctx.enter_context(nc.sbuf_tensor(name, shape, dt))

        def sem(name):
            return ctx.enter_context(nc.semaphore(name))

        ident = sb("ident", [P, P])
        tri_le = sb("tri_le", [P, P])
        tri_gt = sb("tri_gt", [P, P])
        tri_lt = sb("tri_lt", [P, P])
        ones = sb("ones", [P, P])
        zeros = sb("zeros", [P, D])
        half_neg = sb("half_neg", [P, NK])
        iota_e = sb("iota_e", [P, NE])
        qbase = sb("qbase", [P, NE])
        route = sb("route", [P, NTILE, 4])
        count = sb("count", [P, NE])
        jrow = sb("jrow", [P, NJT])
        jdum = sb("jdum", [P, NJT])
        jrow_i = sb("jrow_i", [P, NJT], I32)
        jdum_i = sb("jdum_i", [P, NJT], I32)
        ARENA = 49600
        arena = sb("arena", [P, ARENA])

        def carver():
            at = [0]

            def carve(*shape, dt=F32):
                n = 1
                for s in shape:
                    n *= s
                ap = arena[:, at[0]:at[0] + n]
                at[0] += n
                assert at[0] <= ARENA, at[0]
                if dt is not F32:
                    ap = ap.bitcast(dt)
                if len(shape) == 2:
                    ap = ap.rearrange("p (a b) -> p a b", a=shape[0])
                elif len(shape) == 3:
                    ap = ap.rearrange("p (a b c) -> p a b c", a=shape[0], b=shape[1])
                elif len(shape) == 4:
                    ap = ap.rearrange("p (a b c d) -> p a b c d", a=shape[0], b=shape[1], c=shape[2])
                return ap
            return carve

        carve = carver()
        win = carve(2, KD, DPROJ)
        wout = carve(2, NCT, D)
        cw, cb = carve(2, NC, TAPS), carve(2, NC)
        lnw, lnb = carve(2, KD), carve(2, KD)
        rmsw = carve(2, NCT)
        dtb, aneg, dsk = carve(2, NH), carve(2, NH), carve(2, NH)
        gw, gb = carve(KD, NE), carve(NE)
        hln = carve(2, NK, D)
        hres = carve(2, NK, D)
        xin = carve(2, NK, D)
        uT = carve(2, KD, T)
        acc, th = carve(2, T), carve(2, T)
        xcT = carve(2, NCT, T)
        bT, cT = carve(2, T), carve(2, T)
        zt = carve(2, DI)
        zs = carve(2, NK, DI)
        tri_a = carve(2, NH, P)
        xs, dtx, xw, xd = carve(2, NH, HD), carve(2, NH, HD), carve(2, NH, HD), carve(2, NH, HD)
        decay, mix = carve(2, NH, P), carve(2, NH, P)
        cbm = carve(2, P)
        bs = carve(2, DS)
        ex = carve(2, 3, NH)
        wdt = carve(2, NH)
        y1, y2, g = carve(2, NH, HD), carve(2, NH, HD), carve(2, NH, HD)
        state, state_d = carve(2, NH, HD), carve(NH, HD)
        gT = carve(2, NCT, P)
        junk = carve(DI)
        ob = carve(2, NK, D)
        x1T = carve(KD, T)
        st6, mv, ve, rs = carve(NK, 6), carve(NK, 2), carve(NK), carve(NK)
        rst6, rmv, rve, rrs = carve(NK, 6), carve(NK, 2), carve(NK), carve(NK)
        ss, sve, srs = carve(2, NK), carve(NK), carve(NK)
        dtr, nab, e1, l1 = carve(NK, NH), carve(NK, NH), carve(NK, NH), carve(NK, NH)
        dt_s, a_s = carve(2, NK, NH), carve(2, NK, NH)
        logit, top8 = carve(NK, NE), carve(NK, 8)
        top_i, top_f = carve(NK, 8, dt=U32), carve(NK, 8)
        gap, p2 = carve(NK), carve(NK)
        oh1, oh2, oh = carve(NK, NE), carve(NK, NE), carve(NK, NE)
        pos, pick, base = carve(NK, NE), carve(2, NK, NE), carve(NK, NE)
        pw = carve(NK, 4)
        slot = carve(2, 2 * NK, dt=U32)

        carve = carver()
        wex = carve(WB, WEX)
        b2b = carve(WB, D)
        xq = carve(WB, D)
        xqT = carve(WB, KD, P)
        sg = carve(2, 4, P)
        act = carve(WB, NF, P)
        yt = carve(WB, D)
        cnt, moved = carve(NE), carve(NE - 1)
        behind, shift = carve(NTILE, NE - 1), carve(NTILE)
        rows_u = carve(NTILE, 2)
        nt, end = carve(NE), carve(NE)
        tcmp = carve(NE, NTILE)
        j128 = carve(NTILE)
        cmp_, cmp_nt = carve(NJT, NE), carve(NJT, NE)
        ej, stj, usedj, tmpj = carve(NJT), carve(NJT), carve(NJT), carve(NJT)
        plan_f = carve(3 * NJT + NE)
        plan_i = carve(3 * NJT + NE, dt=I32)
        slot_c = carve(2, 2 * LG, dt=U32)
        wv = carve(2, LG, 4)
        back, got1, got2 = carve(2, LG, D), carve(2, LG, D), carve(2, LG, D)
        fsum, fin = carve(2, LG, D), carve(2, LG, D)
        fst, fmv = carve(2, LG, 6), carve(2, LG, 2)
        fve, fsd, frs = carve(2, LG), carve(2, LG), carve(2, LG)

        pa = [ctx.enter_context(nc.psum_tensor(f"pa{i}", [P, T], F32)) for i in range(2)]
        pe_ = [ctx.enter_context(nc.psum_tensor(f"pe{i}", [P, T], F32)) for i in range(2)]
        pt = ctx.enter_context(nc.psum_tensor("pt", [P, T], F32))
        pm = ctx.enter_context(nc.psum_tensor("pm", [P, T], F32))
        py = ctx.enter_context(nc.psum_tensor("py", [P, T], F32))
        pz = ctx.enter_context(nc.psum_tensor("pz", [P, T], F32))
        CBT, BTR, CS = pm[:, 0:P], pm[:, P:P + DS], pm[:, P + DS:P + DS + 3 * NH]
        OUT = pm[:, T - D:T]

        consts = sem("consts")
        params = sem("params")
        prepared = sem("prepared")
        hln_in = [sem("hln_in0"), sem("hln_in1")]
        hres_in = [sem("hres_in0"), sem("hres_in1")]
        xin_in = [sem("xin_in0"), sem("xin_in1")]
        ln_var = sem("ln_var")
        ln_rs = sem("ln_rs")
        ln_done = sem("ln_done")
        a_full = [sem("a_full0"), sem("a_full1")]
        a_free = [sem("a_free0"), sem("a_free1")]
        sp_in = sem("sp_in")
        sp_ln = sem("sp_ln")
        a_ready = sem("a_ready")
        acc_init = sem("acc_init")
        tanh_ready = sem("tanh_ready")
        xc_done = sem("xc_done")
        zt_ready = sem("zt_ready")
        tri_ready = sem("tri_ready")
        pt_full, pt_free = sem("pt_full"), sem("pt_free")
        pm_full, pm_free = sem("pm_full"), sem("pm_free")
        seg_full, e_free = sem("seg_full"), sem("e_free")
        pm_read = sem("pm_read")
        wdt_ready = sem("wdt_ready")
        m_done = sem("m_done")
        dtx_ready = sem("dtx_ready")
        xw_ready = sem("xw_ready")
        xd_ready = sem("xd_ready")
        y_full, y_free = sem("y_full"), sem("y_free")
        z_full, z_free = sem("z_full"), sem("z_free")
        s_ready = sem("s_ready")
        sd_ready = sem("sd_ready")
        ysum_ready = sem("ysum_ready")
        g_ready = sem("g_ready")
        ss_ready = sem("ss_ready")
        sve_ready, srs_ready = sem("sve_ready"), sem("srs_ready")
        h_ready = sem("h_ready")
        stored = [sem("stored0"), sem("stored1")]
        r_sum = sem("r_sum")
        r_var, r_rs, x1_ready = sem("r_var"), sem("r_rs"), sem("x1_ready")
        gap_ready, p2_ready = sem("gap_ready"), sem("p2_ready")
        oh_ready = sem("oh_ready")
        slot_ready = sem("slot_ready")
        scattered = [sem("scattered0"), sem("scattered1")]
        c_dve1, c_dve2, c_dve3 = sem("c_dve1"), sem("c_dve2"), sem("c_dve3")
        c_act, c_prep, c_pool = sem("c_act"), sem("c_prep"), sem("c_pool")
        hop = sem("hop")
        plan_done = sem("plan_done")
        padded = sem("padded")
        w_in_s = [sem(f"w_in{i}") for i in range(WB)]
        xq_in = [sem(f"xq_in{i}") for i in range(WB)]
        f_t_full, f_t_free = sem("f_t_full"), sem("f_t_free")
        f_full = [sem(f"f_full{i}") for i in range(4)]
        silu_done = [sem("silu_done0"), sem("silu_done1")]
        act_done = sem("act_done")
        o_full, o_ready = sem("o_full"), sem("o_ready")
        ans_out = [sem(f"ans_out{i}") for i in range(WB)]
        c_plan = sem("c_plan")
        idx_ready = sem("idx_ready")
        x1_back = [sem("x1_back0"), sem("x1_back1")]
        got = [sem("got0"), sem("got1")]
        f_sum, f_var, f_rs, f_out = sem("f_sum"), sem("f_var"), sem("f_rs"), sem("f_out")
        out_done = [sem("out_done0"), sem("out_done1")]
        c_fin = sem("c_fin")

        N_PARAMS = 14
        N_CONSTS = 1


        GATE, VALUE = [pe_[0], pe_[1]], [pa[0], pa[1]]

        def rows(dram, b):
            return dram[b].rearrange("(k p) d -> p k d", p=P)

        def over_p(ap, k=None):
            return ap.unsqueeze(2).to_broadcast([ap.shape[0], NH, HD])

        block = ctx.enter_context(nc.Block())

        @block.sync
        def _(sp):
            def fill_base(v):
                return 6 * v if v <= 9 else 60 + 8 * (v - 10)

            def load_hln(w):
                q = w % 2
                if w >= 2:
                    sp.wait_ge(a_full[1], fill_base(w - 2) + 1)
                if w < NB:
                    sp.dma_start(hln[:, q], rows(x, w)).then_inc(hln_in[q], 16)
                else:
                    b = min(w - NB, NB - 1)
                    sp.wait_ge(stored[b % 2], 16 * (b // 2 + 1) + 16)
                    sp.dma_start(hln[:, q], rows(h1, b)).then_inc(hln_in[q], 16)

            load_hln(0)
            n_params = [0]

            def param(dst, src):
                sp.dma_start(dst, src).then_inc(params, 16)
                n_params[0] += 1

            param(lnw, ln_w)
            param(lnb, ln_b)
            param(dtb, dt_bias.unsqueeze(0).to_broadcast([P, 2, NH]))
            param(aneg, a_log.unsqueeze(0).to_broadcast([P, 2, NH]))
            param(dsk, d_skip.unsqueeze(0).to_broadcast([P, 2, NH]))
            param(cw, conv_w)
            param(cb, conv_b)
            param(rmsw, rms_w)
            param(gw, gate_w.rearrange("(k p) e -> p k e", p=P))
            param(gb, gate_b.unsqueeze(0).to_broadcast([P, NE]))
            param(win[:, 0], w_in[0].rearrange("(k p) n -> p k n", p=P))
            load_hln(1)
            param(wout[:, 0], w_out[0].rearrange("(k p) n -> p k n", p=P))
            param(wout[:, 1], w_out[1].rearrange("(k p) n -> p k n", p=P))
            param(win[:, 1], w_in[1].rearrange("(k p) n -> p k n", p=P))
            assert n_params[0] == N_PARAMS
            load_hln(2)
            sp.wait_ge(consts, N_CONSTS)
            for s in range(2):
                row = DUMMY + (2 + s) * P
                sp.dma_start(queue[row:row + P, :], zeros[:, :]).then_inc(stored[s], 16)
            for u in range(MAMBA_UNITS + 1):
                q = u % 2
                if u < MAMBA_UNITS:
                    at_least(sp, h_ready, u - 1)
                    if u < NB:
                        sp.dma_start(hres[:, q], rows(x, u)).then_inc(hres_in[q], 16)
                    else:
                        sp.dma_start(hres[:, q], rows(h1, u - NB)).then_inc(hres_in[q], 16)
                        at_least(sp, r_sum, u - NB - 1)
                        sp.dma_start(xin[:, q], rows(x, u - NB)).then_inc(xin_in[q], 16)
                if 1 <= u <= NB:
                    sp.wait_ge(h_ready, u)
                    sp.dma_start(rows(h1, u - 1), ob[:, 1 - q]).then_inc(stored[1 - q], 16)
                if u > NB:
                    b = u - 1 - NB
                    sp.wait_ge(x1_ready, b + 1)
                    sp.dma_start(x1_rows[b * T:(b + 1) * T, :].rearrange("(k p) d -> p k d", p=P),
                                 ob[:, 1 - q]).then_inc(stored[1 - q], 16)
                if u + 3 <= MAMBA_UNITS:
                    load_hln(u + 3)

            sp.wait_ge(plan_done, 1)
            for e in range(NE):
                end_e = sp.value_load(plan_i[0:1, 3 * NJT + e:3 * NJT + e + 1], min_val=0, max_val=NTOK)
                sp.dma_start(queue[bass.ds(end_e + e * QROWS, P), :], zeros[:, :]).then_inc(padded, 16)
            sp.wait_ge(padded, 16 * NE)
            for s in range(2):
                sp.wait_ge(scattered[s], 16 * 2 * NK * (NB // 2) + 16)
                sp.wait_ge(stored[s], 16 * NB + 16)

            def load_rows(i, r):
                row = sp.value_load(plan_i[0:1, bass.ds(WB * i + r, 1)], min_val=0, max_val=DUMMY + (WB - 1) * P)
                sp.dma_start(xq[:, r % WB], queue[bass.ds(row, P), :]).then_inc(xq_in[r % WB], 16)

            def load_weights(i, r):
                e = sp.value_load(plan_i[0:1, bass.ds(WB * i + (r + NJT), 1)], min_val=0, max_val=NE - 1)
                need = sp.value_load(plan_i[0:1, bass.ds(WB * i + (r + 2 * NJT), 1)], min_val=0, max_val=1)
                sp.dma_start(wex[:, r], w_exp[bass.ds(e, 1)].rearrange("o p n -> (o p) n"),
                             cond=(need > 0)).then_inc(w_in_s[r], 16)
                sp.dma_start(b2b[:, r], b2[bass.ds(e, 1)].to_broadcast([P, D]),
                             cond=(need > 0)).then_inc(w_in_s[r], 16)

            for r in range(WB):
                load_rows(0, r)
                load_weights(0, r)
            with sp.Fori(1, NJ // WB) as i:
                for r in range(WB):
                    sp.wait_ge(o_ready, WB * i + (r + 1 - WB))
                    sp.sem_inc(hop, 1)
                    load_weights(i, r)
                    load_rows(i, r)
            sp.wait_ge(o_ready, NJ + 1 - WB)
            load_rows(NJ // WB, 0)

            for s in range(WB):
                sp.wait_ge(ans_out[s], 16 * (NJ // WB))

            def load_back(i, q):
                sp.dma_start(back[:, q], x1_rows[bass.ds((2 * i + q) * T, T), :].rearrange(
                    "(k p) d -> p k d", p=P)).then_inc(x1_back[q], 16)

            def store_out(i, q):
                sp.wait_ge(f_out, 2 * i + (q + 1))
                sp.sem_inc(hop, 1)
                sp.dma_start(out[bass.ds((2 * i + q) * T, T), :].rearrange("(k p) d -> p k d", p=P),
                             fin[:, q]).then_inc(out_done[q], 16)

            for q in range(2):
                load_back(0, q)
            with sp.Fori(1, NB // 2) as i:
                for q in range(2):
                    sp.wait_ge(f_sum, 2 * i + (q - 1))
                    sp.sem_inc(hop, 1)
                    load_back(i, q)
                    store_out(i - 1, q)
            for q in range(2):
                store_out(NB // 2 - 1, q)
            for q in range(2):
                sp.wait_ge(out_done[q], 16 * (NB // 2))

        @block.tensor
        def _(pe):
            def fill(st, name, product):
                bank, before = st.fill(name)
                at_least(pe, a_free[bank], before)
                product(pa[bank]).then_inc(a_full[bank], 1)

            def s1_fill(st, name):
                l, vq = st.next_layer, 1 - st.q
                v = st.u + 1
                if name in ("ln0", "ln1"):
                    d = int(name[2])
                    if d == 0:
                        pe.wait_ge(ln_done, v + 1)

                    def go(bank):
                        for k in range(NK):
                            ins = pe.transpose(bank[:, k * P:(k + 1) * P], hln[:, vq, k, d * P:(d + 1) * P], ident[:, :])
                        return ins
                elif name == "dt":
                    for n in ("ln0", "ln1"):
                        bank, before = st.fill(n)
                        pe.wait_ge(a_free[bank], before + 1)
                    if isinstance(v, int) and v == 0:
                        pe.wait_ge(params, 16 * N_PARAMS)

                    def go(bank):
                        for k in range(NK):
                            for d in range(KD):
                                ins = pe.matmul(bank[:, k * NH:(k + 1) * NH], uT[:, vq, d, k * P:(k + 1) * P],
                                                win[:, l, d, ODT:ODT + NH], start=(d == 0), stop=(d == KD - 1))
                        return ins
                elif name[0] == "c":
                    c = int(name[1])

                    def go(bank):
                        for d in range(KD):
                            ins = pe.matmul(bank[:, :], win[:, l, d, OX + c * P:OX + (c + 1) * P], uT[:, vq, d, :],
                                            start=(d == 0), stop=(d == KD - 1))
                        return ins
                else:
                    k = int(name[1])

                    def go(bank):
                        for d in range(KD):
                            ins = pe.matmul(bank[:, :], uT[:, vq, d, k * P:(k + 1) * P], win[:, l, d, 0:DI],
                                            start=(d == 0), stop=(d == KD - 1))
                        return ins
                fill(st, name, go)

            def s3_fill(st, name):
                w_q = 1 - st.q
                if name in ("t0", "t1"):
                    d = int(name[1])
                    if d == 0:
                        pe.wait_ge(x1_ready, st.u - NB)

                    def go(bank):
                        for k in range(NK):
                            ins = pe.transpose(bank[:, k * P:(k + 1) * P], ob[:, w_q, k, d * P:(d + 1) * P], ident[:, :])
                        return ins
                elif name == "lg":
                    for n in ("t0", "t1"):
                        bank, before = st.fill(n)
                        pe.wait_ge(a_free[bank], before + 1)

                    def go(bank):
                        for k in range(NK):
                            for d in range(KD):
                                ins = pe.matmul(bank[:, k * NE:(k + 1) * NE], x1T[:, d, k * P:(k + 1) * P],
                                                gw[:, d, :], start=(d == 0), stop=(d == KD - 1))
                        return ins
                else:
                    pe.wait_ge(oh_ready, st.u - NB)

                    def go(bank):
                        pe.matmul(bank[:, 0:NK * NE], tri_lt[:, :], oh.rearrange("p k e -> p (k e)"), start=True, stop=True)
                        return pe.matmul(bank[:, NK * NE:2 * NK * NE], ones[:, :], oh.rearrange("p k e -> p (k e)"),
                                         start=True, stop=True)
                fill(st, name, go)

            def do_fills(st, names):
                for n in names:
                    if n in ONLY3:
                        s3_fill(st, n)
                    else:
                        s1_fill(st, n)

            def chunk_a(st, k):
                q, n, kq, u8 = st.q, 4 * st.u + k, k % 2, 8 * st.u
                p = PAIRS.index(f"a{k}")
                tk = slice(k * P, (k + 1) * P)
                if k == 0:
                    pe.wait_ge(xc_done, 5 * st.u + 5)
                    pe.wait_ge(a_ready, st.u + 1)
                at_least(pe, pt_free, u8 + p)
                for c in range(NCT):
                    ins = pe.transpose(pt[:, c * P:(c + 1) * P], xcT[:, q, c, tk], ident[:, :])
                ins.then_inc(pt_full, 1)
                at_least(pe, pm_free, u8 + p)
                for s, w in enumerate((tri_le, tri_gt, ones)):
                    pe.matmul(CS[:, s * NH:(s + 1) * NH], w[:, :], a_s[:, q, k, :], start=True, stop=True)
                pe.transpose(BTR, bT[0:DS, q, tk], ident[0:DS, 0:DS])
                pe.matmul(CBT, bT[0:DS, q, tk], cT[0:DS, q, tk], start=True, stop=True).then_inc(pm_full, 1)
                pe.wait_ge(tri_ready, n + 1)
                for h in range(2):
                    at_least(pe, e_free, 2 * n - 1 + h)
                    pe.matmul(pe_[h][:, :], tri_gt[:, :],
                              tri_a[:, kq, 4 * h:4 * h + 4, :].rearrange("p h t -> p (h t)"),
                              start=True, stop=True).then_inc(seg_full, 1)

            def chunk_b(st, k):
                q, n, kq, u6 = st.q, 4 * st.u + k, k % 2, 6 * st.u
                if k > 0:
                    pe.wait_ge(z_free, u6 + 2 * k - 1)
                    pe.matmul(pz[:, :], cT[0:DS, q, k * P:(k + 1) * P],
                              state[0:DS, (k - 1) % 2].rearrange("p h d -> p (h d)"),
                              start=True, stop=True).then_inc(z_full, 1)
                pe.wait_ge(m_done, n + 1)
                pe.wait_ge(dtx_ready, n + 1)
                at_least(pe, y_free, n)
                for h in range(NH):
                    ins = pe.matmul(py[:, h * HD:(h + 1) * HD], mix[:, kq, h, :], dtx[:, kq, h, :], start=True, stop=True)
                ins.then_inc(y_full, 1)
                if k < NK - 1:
                    pe.wait_ge(xw_ready, 3 * st.u + k + 1)
                    at_least(pe, z_free, u6 + 2 * k)
                    pe.wait_ge(pm_read, n + 1)
                    pe.matmul(pz[0:DS, :], bs[:, kq, :], xw[:, kq].rearrange("p h d -> p (h d)"),
                              start=True, stop=True).then_inc(z_full, 1)

            def chunk_c(st, k):
                u8, p = 8 * st.u, PAIRS.index(f"o{k}")
                pe.wait_ge(g_ready, 4 * st.u + k + 1)
                pe.wait_ge(pt_free, u8 + p)
                gk = g[:, k % 2].rearrange("p h d -> p (h d)")
                for c in range(NCT):
                    ins = pe.transpose(pt[:, c * P:(c + 1) * P], gk[:, c * P:(c + 1) * P], ident[:, :])
                ins.then_inc(pt_full, 1)

            def chunk_d(st, k):
                u8, p = 8 * st.u, PAIRS.index(f"o{k}")
                pe.wait_ge(pt_free, u8 + p + 1)
                pe.wait_ge(pm_free, u8 + p)
                for c in range(NCT):
                    ins = pe.matmul(OUT, gT[:, k % 2, c, :], wout[:, st.layer, c, :], start=(c == 0), stop=(c == NCT - 1))
                ins.then_inc(pm_full, 1)

            def body(st):
                s1, s3 = not st.last, st.s3
                f = {(0, 1): ["ln0", "ln1"] * s1, (0, 2): ["dt"] * s1,
                     (1, 1): ["c4"] * s1, (1, 2): ["c0"] * s1 + ["t0", "t1"] * s3,
                     (2, 1): ["c1"] * s1, (2, 2): ["c2"] * s1 + ["lg"] * s3,
                     (3, 1): ["c3"] * s1, (3, 2): ["z0", "z1"] * s1 + ["rk"] * s3}
                for k in range(NK):
                    chunk_a(st, k)
                    if k > 0:
                        chunk_c(st, k - 1)
                    do_fills(st, f[k, 1])
                    chunk_b(st, k)
                    if k > 0:
                        chunk_d(st, k - 1)
                    do_fills(st, f[k, 2])
                chunk_c(st, NK - 1)
                do_fills(st, ["z2", "z3"] * s1)
                chunk_d(st, NK - 1)

            pe.wait_ge(consts, N_CONSTS)
            pe.wait_ge(prepared, 1)
            schedule(pe, body, lambda st: do_fills(st, PLAIN), lambda st: do_fills(st, ONLY3))

            def turn(i, r):
                b = r % WB
                pe.wait_ge(xq_in[b], 16 * (i + (r // WB + 1)))
                at_least(pe, f_t_free, WB * i + r)
                for d in range(KD):
                    ins = pe.transpose(pt[:, d * P:(d + 1) * P], xq[:, b, d * P:(d + 1) * P], ident[:, :])
                ins.then_inc(f_t_full, 1)

            def tile(i, r):
                j = WB * i + r
                w1 = wex[:, r, 0:KD * 2 * FF].rearrange("p (k n) -> p k n", k=KD)
                w2 = wex[:, r, KD * 2 * FF:KD * 2 * FF + NF * D].rearrange("p (k n) -> p k n", k=NF)
                pe.wait_ge(w_in_s[r], 32 * (i + 1))
                pe.wait_ge(f_t_free, j + 1)
                for half in range(2):
                    for bank, first, free in ((GATE[half], FF, 2 * half), (VALUE[half], 0, 2 * half + 1)):
                        if free % 2 == 0:
                            at_least(pe, silu_done[half], j)
                        else:
                            at_least(pe, act_done, 2 * j - 1 + half)
                        for f in range(4):
                            col = first + (4 * half + f) * P
                            for d in range(KD):
                                ins = pe.matmul(bank[:, f * P:(f + 1) * P], w1[:, d, col:col + P], xqT[:, r, d, :],
                                                start=(d == 0), stop=(d == KD - 1))
                        ins.then_inc(f_full[free], 1)
                turn(i, r + 1)
                at_least(pe, o_ready, j)
                for f in range(NF):
                    if f % 4 == 0:
                        pe.wait_ge(act_done, 2 * j + 1 + f // 4)
                    ins = pe.matmul(py[:, 0:D], act[:, r, f, :], w2[:, f, :], start=(f == 0), stop=(f == NF - 1))
                ins.then_inc(o_full, 1)

            turn(0, 0)
            for r in range(WB):
                tile(0, r)
            with pe.Fori(1, NJ // WB) as i:
                for r in range(WB):
                    tile(i, r)

        @block.scalar
        def _(act_e):
            e = act_e

            def wait_fill(st, name):
                bank, before = st.fill(name)
                e.wait_ge(a_full[bank], before + 1)
                return bank, before

            def ln_out(st, d):
                bank, _ = wait_fill(st, f"ln{d}")
                l = st.next_layer
                e.activation(uT[:, 1 - st.q, d, :], pa[bank][:, :], ACT.Identity, scale=lnw[:, l, d:d + 1],
                             bias=lnb[:, l, d:d + 1]).then_inc(a_free[bank], 1)

            def conv_first(st, c):
                idx = CONV_ORDER.index(c)
                l, m, mq = st.next_layer, 5 * (st.u + 1) + idx, (1 - st.q + idx) % 2
                bank, _ = wait_fill(st, c)
                at_least(e, xc_done, m - 1)
                ct = int(c[1])
                e.activation(acc[:, mq], pa[bank][:, :], ACT.Identity, scale=cw[:, l, ct, TAPS - 1:TAPS],
                             bias=cb[:, l, ct:ct + 1]).then_inc(acc_init, 1)

            def conv_tanh(st, c):
                idx = CONV_ORDER.index(c)
                mq = (1 - st.q + idx) % 2
                bank, before = st.fill(c)
                e.wait_ge(a_free[bank], before + 1)
                e.activation(th[:, mq], acc[:, mq], ACT.Tanh).then_inc(tanh_ready, 1)

            def z_tanh(st, k):
                bank, _ = wait_fill(st, f"z{k}")
                if k >= 2:
                    b2_, before = st.fill(f"z{k - 2}")
                    e.wait_ge(a_free[b2_], before + 1)
                e.activation(zt[:, k % 2], pa[bank][:, :], ACT.Tanh, scale=0.5).then_inc(zt_ready, 1)

            def softplus(st):
                v = st.u + 1
                e.wait_ge(sp_in, v + 1)
                e.activation(e1, nab, ACT.Exp).then_inc(c_act, 1)
                e.wait_ge(c_act, v + 1)
                e.activation(l1, e1, ACT.Ln, bias=1.0).then_inc(sp_ln, 1)

            def chunk_a(st, k):
                q, n, kq, u8 = st.q, 4 * st.u + k, k % 2, 8 * st.u
                p = PAIRS.index(f"a{k}")
                e.wait_ge(pt_full, u8 + p + 1)
                at_least(e, xd_ready, n - 1)
                e.activation(xs[:, kq].rearrange("p h d -> p (h d)"), pt[:, :], ACT.Copy).then_inc(pt_free, 1)
                e.wait_ge(pm_full, u8 + p + 1)
                e.activation(ex[:, kq].rearrange("p s h -> p (s h)"), CS, ACT.Exp)
                e.activation(bs[:, kq], BTR, ACT.Copy).then_inc(pm_read, 1)
                at_least(e, m_done, n - 1)
                for h in range(2):
                    e.wait_ge(seg_full, 2 * n + h + 1)
                    e.activation(decay[:, kq, 4 * h:4 * h + 4].rearrange("p h t -> p (h t)"), pe_[h][:, :],
                                 ACT.Exp).then_inc(e_free, 1)

            def chunk_c(st, k):
                q, n, kq = st.q, 4 * st.u + k, k % 2
                e.wait_ge(g_ready, n + 1)
                at_least(e, ss_ready, n)
                e.activation(junk, g[:, kq].rearrange("p h d -> p (h d)"), ACT.Square,
                             accum_out=ss[:, q, k:k + 1]).then_inc(ss_ready, 1)
                e.wait_ge(pt_full, 8 * st.u + PAIRS.index(f"o{k}") + 1)
                e.activation(gT[:, kq].rearrange("p c t -> p (c t)"), pt[:, :], ACT.Copy).then_inc(pt_free, 1)

            def chunk_d(st, k):
                q = st.q
                if k == 0:
                    e.wait_ge(stored[q], 16 * st.h + 16)
                    if st.layer == 1:
                        e.wait_ge(scattered[q], 128 * (st.h - 4) + 16)
                e.wait_ge(pm_full, 8 * st.u + PAIRS.index(f"o{k}") + 1)
                e.activation(ob[:, q, k, :], OUT, ACT.Copy).then_inc(pm_free, 1)

            def x1_out(st, d):
                bank, _ = wait_fill(st, f"t{d}")
                e.activation(x1T[:, d, :], pa[bank][:, :], ACT.Copy).then_inc(a_free[bank], 1)

            def gap_exp(st):
                e.wait_ge(gap_ready, st.u - NB)
                e.activation(p2, gap, ACT.Exp).then_inc(p2_ready, 1)

            def body(st):
                s1, s3 = not st.last, st.s3
                chunk_a(st, 0)
                if s1:
                    ln_out(st, 0)
                    ln_out(st, 1)
                    softplus(st)
                chunk_a(st, 1)
                if s1:
                    conv_first(st, "c4")
                chunk_c(st, 0)
                if s1:
                    conv_tanh(st, "c4")
                    conv_first(st, "c0")
                chunk_d(st, 0)
                if s3:
                    x1_out(st, 0)
                    x1_out(st, 1)
                if s1:
                    conv_tanh(st, "c0")
                chunk_a(st, 2)
                if s1:
                    conv_first(st, "c1")
                chunk_c(st, 1)
                if s1:
                    conv_tanh(st, "c1")
                    conv_first(st, "c2")
                chunk_d(st, 1)
                if s1:
                    conv_tanh(st, "c2")
                chunk_a(st, 3)
                if s1:
                    conv_first(st, "c3")
                chunk_c(st, 2)
                if s3:
                    gap_exp(st)
                if s1:
                    conv_tanh(st, "c3")
                    z_tanh(st, 0)
                chunk_d(st, 2)
                if s1:
                    z_tanh(st, 1)
                chunk_c(st, 3)
                if s1:
                    z_tanh(st, 2)
                    z_tanh(st, 3)
                chunk_d(st, 3)

            def prologue(st):
                ln_out(st, 0)
                ln_out(st, 1)
                softplus(st)
                for c in CONV_ORDER:
                    conv_first(st, c)
                    conv_tanh(st, c)
                for k in range(NK):
                    z_tanh(st, k)

            def epilogue(st):
                x1_out(st, 0)
                x1_out(st, 1)
                gap_exp(st)

            e.wait_ge(params, 16 * N_PARAMS)
            e.activation(aneg, aneg, ACT.Exp).then_inc(c_prep, 1)
            e.wait_ge(prepared, 1)
            schedule(e, body, prologue, epilogue)

            def rows_out(i, r):
                e.wait_ge(f_t_full, WB * i + (r + 1))
                e.activation(xqT[:, r % WB].rearrange("p d t -> p (d t)"), pt[:, 0:KD * P], ACT.Copy).then_inc(f_t_free, 1)

            def tile(i, r):
                j = WB * i + r
                b1 = wex[:, r, WEX - 2 * NF:WEX]
                for half in range(2):
                    e.wait_ge(f_full[2 * half], j + 1)
                    at_least(e, act_done, 2 * j - 1 + half)
                    for f in range(4):
                        ff = NF + 4 * half + f
                        ins = e.activation(sg[:, half, f, :], GATE[half][:, f * P:(f + 1) * P], ACT.Silu,
                                           bias=b1[:, ff:ff + 1])
                    ins.then_inc(silu_done[half], 1)
                rows_out(i, r + 1)

            rows_out(0, 0)
            for r in range(WB):
                tile(0, r)
            with e.Fori(1, NJ // WB) as i:
                for r in range(WB):
                    tile(i, r)

            with e.Fori(0, NB // 2) as i:
                for q in range(2):
                    e.wait_ge(f_var, 2 * i + (q + 1))
                    e.activation(fsd[:, q], fve[:, q], ACT.Sqrt).then_inc(f_rs, 1)

        @block.vector
        def _(dve):
            def ln_stats(w, hw, wq):
                ch = Chain(dve, c_dve1, 2, w)
                dve.wait_ge(hln_in[wq], 16 * (hw + 1))
                for k in range(NK):
                    ins = dve.bn_stats(st6[:, k, :], hln[:, wq, k, :])
                ch.link(ins)
                dve.sem_inc(hop, 1)
                for k in range(NK):
                    ins = dve.bn_aggr(mv[:, k, :], st6[:, k, :])
                ch.link(ins)
                ch.close()
                dve.tensor_scalar(ve, mv[:, :, 1], EPS, None, ALU.add).then_inc(ln_var, 1)

            def ln_apply(w, wq):
                dve.wait_ge(ln_rs, w + 1)
                for k in range(NK):
                    ins = dve.tensor_scalar(hln[:, wq, k, :], hln[:, wq, k, :], mv[:, k, 0:1], rs[:, k:k + 1],
                                            ALU.subtract, ALU.mult)
                ins.then_inc(ln_done, 1)

            def wait_fill(st, name):
                bank, before = st.fill(name)
                dve.wait_ge(a_full[bank], before + 1)
                return bank, before

            def dt_first(st):
                l, v = st.next_layer, st.u + 1
                bank, _ = wait_fill(st, "dt")
                src = pa[bank][:, 0:NK * NH].rearrange("p (k h) -> p k h", k=NK)
                ins = dve.tensor_tensor(dtr, src, dtb[:, l].unsqueeze(1).to_broadcast([P, NK, NH]), ALU.add)
                ins.then_inc(a_free[bank], 1)
                dve.wait_ge(a_free[bank], st.fill("dt")[1] + 1)
                dve.scalar_tensor_tensor(nab, dtr, -1.0, dtr, ALU.mult, ALU.min).then_inc(sp_in, 1)

            def dt_last(st, ch):
                l, v, vq = st.next_layer, st.u + 1, 1 - st.q
                dve.wait_ge(sp_ln, v + 1)
                ch.link(dve.scalar_tensor_tensor(dt_s[:, vq], dtr, 0.0, l1, ALU.max, ALU.add))
                dve.tensor_tensor(a_s[:, vq], dt_s[:, vq], aneg[:, l].unsqueeze(1).to_broadcast([P, NK, NH]),
                                  ALU.mult).then_inc(a_ready, 1)

            def taps(st, c, ch):
                idx, ct, l = CONV_ORDER.index(c), int(c[1]), st.next_layer
                m, mq = 5 * (st.u + 1) + idx, (1 - st.q + idx) % 2
                bank, _ = st.fill(c)
                dve.wait_ge(acc_init, m + 1)
                for s in range(1, TAPS):
                    ins = dve.scalar_tensor_tensor(acc[:, mq, s:T], pa[bank][:, 0:T - s],
                                                   cw[:, l, ct, TAPS - 1 - s:TAPS - s], acc[:, mq, s:T],
                                                   ALU.mult, ALU.add)
                    if s < TAPS - 1:
                        ch.link(ins)
                ins.then_inc(a_free[bank], 1)

            def silu_x(st, c):
                idx, ct, vq = CONV_ORDER.index(c), int(c[1]), 1 - st.q
                m, mq = 5 * (st.u + 1) + idx, (1 - st.q + idx) % 2
                dve.wait_ge(tanh_ready, m + 1)
                if ct < NCT:
                    ins = dve.scalar_tensor_tensor(xcT[:, vq, ct, :], th[:, mq], 1.0, acc[:, mq], ALU.add, ALU.mult)
                else:
                    dve.scalar_tensor_tensor(bT[0:DS, vq], th[0:DS, mq], 1.0, acc[0:DS, mq], ALU.add, ALU.mult)
                    ins = dve.scalar_tensor_tensor(cT[0:DS, vq], th[DS:P, mq], 1.0, acc[DS:P, mq], ALU.add, ALU.mult)
                ins.then_inc(xc_done, 1)

            def z_gate(st, k):
                vq = 1 - st.q
                bank, _ = st.fill(f"z{k}")
                dve.wait_ge(zt_ready, 4 * (st.u + 1) + k + 1)
                dve.scalar_tensor_tensor(zs[:, vq, k, :], zt[:, k % 2], 1.0, pa[bank][:, :], ALU.add,
                                         ALU.mult).then_inc(a_free[bank], 1)

            def end_a(st):
                dve.wait_ge(ss_ready, 4 * st.u)
                dve.tensor_scalar(sve, ss[:, 1 - st.q], 1.0 / (4 * DI), EPS, ALU.mult, ALU.add).then_inc(sve_ready, 1)

            def end_b(st):
                wq = 1 - st.q
                dve.wait_ge(srs_ready, st.u)
                dve.wait_ge(pm_free, 8 * st.u)
                dve.wait_ge(hres_in[wq], 16 * ((st.h + 1) if wq == 0 else st.h))
                for k in range(NK):
                    ins = dve.scalar_tensor_tensor(ob[:, wq, k, :], ob[:, wq, k, :], srs[:, k:k + 1],
                                                   hres[:, wq, k, :], ALU.mult, ALU.add)
                ins.then_inc(h_ready, 1)

            def chunk_a(st, k):
                q, n, kq, u8 = st.q, 4 * st.u + k, k % 2, 8 * st.u
                p = PAIRS.index(f"a{k}")
                dve.wait_ge(pm_read, n + 1)
                if k == 0:
                    dve.wait_ge(a_ready, st.u + 1)
                dve.tensor_tensor(wdt[:, kq], ex[:, kq, 1], dt_s[:, q, k], ALU.mult).then_inc(wdt_ready, 1)
                dve.tensor_tensor(cbm[:, kq], CBT, tri_le[:, :], ALU.mult).then_inc(pm_free, 1)
                dve.wait_ge(pm_free, u8 + p + 1)
                dve.wait_ge(e_free, 2 * n + 2)
                at_least(dve, y_full, n - 1)
                dve.tensor_tensor(mix[:, kq], decay[:, kq], cbm[:, kq].unsqueeze(1).to_broadcast([P, NH, P]),
                                  ALU.mult).then_inc(m_done, 1)

            def chunk_b1(st, k):
                q, n, kq, u6 = st.q, 4 * st.u + k, k % 2, 6 * st.u
                if k > 0:
                    dve.wait_ge(z_full, u6 + 2 * k)
                    dve.tensor_tensor(y1[:, kq], pz.rearrange("p (h d) -> p h d", h=NH), over_p(ex[:, kq, 0]),
                                      ALU.mult).then_inc(z_free, 1)

            def chunk_b2(st, k):
                q, n, kq, u6 = st.q, 4 * st.u + k, k % 2, 6 * st.u
                dve.wait_ge(y_full, n + 1)
                at_least(dve, g_ready, n - 1)
                if k > 0:
                    dve.wait_ge(ysum_ready, 3 * st.u + k)
                    other = y1
                else:
                    dve.wait_ge(xd_ready, n + 1)
                    other = xd
                dve.tensor_tensor(y2[:, kq], py.rearrange("p (h d) -> p h d", h=NH), other[:, kq],
                                  ALU.add).then_inc(y_free, 1)
                if k < NK - 1:
                    dve.wait_ge(z_full, u6 + 2 * k + 1)
                    new = pz[0:DS].rearrange("p (h d) -> p h d", h=NH)
                    if k == 0:
                        dve.tensor_copy(state[0:DS, 0], new).then_inc(z_free, 1)
                    else:
                        dve.wait_ge(sd_ready, 2 * st.u + k)
                        dve.tensor_tensor(state[0:DS, kq], new, state_d[0:DS], ALU.add).then_inc(z_free, 1)

            def s3_stats(st):
                ch = Chain(dve, c_dve3, 12, st.u - (NB + 1))
                wq = 1 - st.q
                dve.wait_ge(r_sum, st.u - NB)
                for k in range(NK):
                    ins = dve.bn_stats(rst6[:, k, :], ob[:, wq, k, :])
                ch.link(ins)
                dve.sem_inc(hop, 1)
                for k in range(NK):
                    ins = dve.bn_aggr(rmv[:, k, :], rst6[:, k, :])
                ch.link(ins)
                dve.tensor_scalar(rve, rmv[:, :, 1], EPS, None, ALU.add).then_inc(r_var, 1)
                return ch

            def s3_apply(st):
                wq = 1 - st.q
                dve.wait_ge(r_rs, st.u - NB)
                for k in range(NK):
                    ins = dve.tensor_scalar(ob[:, wq, k, :], ob[:, wq, k, :], rmv[:, k, 0:1], rrs[:, k:k + 1],
                                            ALU.subtract, ALU.mult)
                ins.then_inc(x1_ready, 1)

            def s3_top(st, ch):
                bank, before = wait_fill(st, "lg")
                src = pa[bank][:, 0:NK * NE].rearrange("p (k e) -> p k e", k=NK)
                dve.tensor_tensor(logit, src, gb.unsqueeze(1).to_broadcast([P, NK, NE]), ALU.add).then_inc(a_free[bank], 1)
                dve.wait_ge(a_free[bank], before + 1)
                dve.sem_inc(hop, 1)
                for k in range(NK):
                    ins = dve.max(top8[:, k, :], logit[:, k, :])
                ch.link(ins)
                dve.sem_inc(hop, 1)
                for k in range(NK):
                    ins = dve.max_index(top_i[:, k, :], top8[:, k, :], logit[:, k, :])
                ch.link(ins)
                dve.tensor_tensor(gap, top8[:, :, 1], top8[:, :, 0], ALU.subtract).then_inc(gap_ready, 1)
                ch.link(dve.tensor_copy(top_f, top_i))
                iota = iota_e[:, :].unsqueeze(1).to_broadcast([P, NK, NE])
                dve.tensor_tensor(oh1, iota, top_f[:, :, 0].unsqueeze(2).to_broadcast([P, NK, NE]), ALU.is_equal)
                ch.link(dve.tensor_tensor(oh2, iota, top_f[:, :, 1].unsqueeze(2).to_broadcast([P, NK, NE]), ALU.is_equal))
                dve.tensor_tensor(oh, oh1, oh2, ALU.add).then_inc(oh_ready, 1)

            def s3_place(st, ch):
                bank, before = wait_fill(st, "rk")
                wq = 1 - st.q
                rank = pa[bank][:, 0:NK * NE].rearrange("p (k e) -> p k e", k=NK)
                total = pa[bank][:, NK * NE:2 * NK * NE].rearrange("p (k e) -> p k e", k=NK)
                dve.wait_ge(p2_ready, st.u - NB)
                dve.tensor_scalar(gap, p2, 1.0, None, ALU.add)
                prev = count
                for k in range(NK):
                    ins = dve.tensor_tensor(base[:, k, :], prev[:, :] if k == 0 else base[:, k - 1, :], total[:, k, :], ALU.add)
                    ch.link(ins)
                dve.tensor_tensor(pos[:, 0, :], rank[:, 0, :], count[:, :], ALU.add)
                dve.tensor_tensor(pos[:, 1:NK, :], rank[:, 1:NK, :], base[:, 0:NK - 1, :], ALU.add).then_inc(a_free[bank], 1)
                dve.wait_ge(a_free[bank], before + 1)
                dve.tensor_copy(count[:, :], base[:, NK - 1, :])
                dve.tensor_tensor(pick[:, 0], pos, oh1, ALU.mult)
                dve.reciprocal(pw[:, :, 0], gap)
                ch.link(dve.tensor_tensor(pick[:, 1], pos, oh2, ALU.mult))
                dve.tensor_tensor(pw[:, :, 1], p2, pw[:, :, 0], ALU.mult)
                dve.tensor_reduce(pw[:, :, 2], pick[:, 0], AX.X, ALU.add)
                ch.link(dve.tensor_reduce(pw[:, :, 3], pick[:, 1], AX.X, ALU.add))
                dve.wait_ge(scattered[wq], 128 * (st.h - 5 if wq == 1 else st.h - 4) + 16)
                for s in range(2):
                    ins = dve.tensor_copy(slot[:, wq, s * NK:(s + 1) * NK], pw[:, :, 2 + s])
                ins.then_inc(slot_ready, 1)
                dve.tensor_copy(route[:, bass.ds(NK * (st.u - (NB + 1)), NK), :], pw)
                ch.close()

            def body(st):
                s1, s3 = not st.last, st.s3
                if not st.first:
                    end_a(st)
                chunk_a(st, 0)
                if not st.first:
                    end_b(st)
                chunk_b2(st, 0)
                if s1:
                    ch1 = Chain(dve, c_dve2, S1_LINKS, st.u + 1)
                    dt_first(st)
                if s3:
                    ch3 = s3_stats(st)
                chunk_a(st, 1)
                if s1:
                    dt_last(st, ch1)
                    taps(st, "c4", ch1)
                chunk_b1(st, 1)
                chunk_b2(st, 1)
                if s3:
                    s3_apply(st)
                if s1:
                    silu_x(st, "c4")
                    taps(st, "c0", ch1)
                    silu_x(st, "c0")
                chunk_a(st, 2)
                if s1:
                    taps(st, "c1", ch1)
                chunk_b1(st, 2)
                chunk_b2(st, 2)
                if s1:
                    silu_x(st, "c1")
                    taps(st, "c2", ch1)
                    ln_stats(st.u + 2, st.h + 1, st.q)
                    silu_x(st, "c2")
                chunk_a(st, 3)
                if s3:
                    s3_top(st, ch3)
                if s1:
                    taps(st, "c3", ch1)
                    ch1.close()
                chunk_b1(st, 3)
                chunk_b2(st, 3)
                if s1:
                    ln_apply(st.u + 2, st.q)
                    silu_x(st, "c3")
                    z_gate(st, 0)
                    z_gate(st, 1)
                if s3:
                    s3_place(st, ch3)
                if s1:
                    z_gate(st, 2)
                    z_gate(st, 3)

            def prologue(st):
                ch1 = Chain(dve, c_dve2, S1_LINKS, 0)
                dt_first(st)
                dt_last(st, ch1)
                for c in CONV_ORDER:
                    taps(st, c, ch1)
                    silu_x(st, c)
                ch1.close()
                for k in range(NK):
                    z_gate(st, k)
                ln_stats(1, 0, 1)
                ln_apply(1, 1)

            def epilogue(st):
                end_a(st)
                end_b(st)
                ch3 = s3_stats(st)
                s3_apply(st)
                s3_top(st, ch3)
                s3_place(st, ch3)

            S1_LINKS = 1 + NC * (TAPS - 2)
            dve.wait_ge(consts, N_CONSTS)
            ln_stats(0, 0, 0)
            ln_apply(0, 0)
            dve.wait_ge(params, 16 * N_PARAMS)
            dve.tensor_scalar(cw, cw, 0.5, None, ALU.mult)
            dve.tensor_scalar(cb, cb, 0.5, None, ALU.mult)
            dve.tensor_scalar(rmsw, rmsw, 0.5, None, ALU.mult).then_inc(c_prep, 1)
            dve.wait_ge(c_prep, 2)
            dve.tensor_scalar(aneg, aneg, -1.0, None, ALU.mult)
            for l in range(2):
                for c in range(NCT):
                    ins = dve.tensor_scalar(wout[:, l, c, :], wout[:, l, c, :], rmsw[:, l, c:c + 1], None, ALU.mult)
            ins.then_inc(prepared, 1)
            dve.wait_ge(prepared, 1)
            schedule(dve, body, prologue, epilogue)

            at = [0]

            def step(ins):
                at[0] += 1
                ins.then_inc(c_plan, 1)
                dve.wait_ge(c_plan, at[0])

            def cells(ap, n=NJT):
                return ap.unsqueeze(2).to_broadcast([1, n, NE])

            jr, jd = jrow[0:1, :], jdum[0:1, :]
            row_f, e_f = plan_f[0:1, 0:NJT], plan_f[0:1, NJT:2 * NJT]
            need_f, len_f = plan_f[0:1, 2 * NJT:3 * NJT], plan_f[0:1, 3 * NJT:3 * NJT + NE]
            step(dve.tensor_scalar(j128, jrow[:, 0:NTILE], float(P), None, ALU.mult))
            step(dve.tensor_tensor(cnt, count[:, :], qbase[:, :], ALU.subtract))
            dve.tensor_copy(len_f, cnt[0:1, :])
            step(dve.tensor_tensor(tcmp, cnt.unsqueeze(2).to_broadcast([P, NE, NTILE]),
                                   j128.unsqueeze(1).to_broadcast([P, NE, NTILE]), ALU.is_gt))
            step(dve.tensor_reduce(nt, tcmp, AX.X, ALU.add))
            step(dve.tensor_copy(end[0:1, 0:1], nt[0:1, 0:1]))
            for e in range(1, NE):
                step(dve.tensor_tensor(end[0:1, e:e + 1], end[0:1, e - 1:e], nt[0:1, e:e + 1], ALU.add))
            step(dve.tensor_tensor(cmp_[0:1], cells(jr), end[0:1].unsqueeze(1).to_broadcast([1, NJT, NE]), ALU.is_ge))
            dve.tensor_reduce(ej[0:1], cmp_[0:1], AX.X, ALU.add)
            step(dve.tensor_tensor(cmp_nt[0:1], cmp_[0:1], nt[0:1].unsqueeze(1).to_broadcast([1, NJT, NE]), ALU.mult))
            dve.tensor_reduce(stj[0:1], cmp_nt[0:1], AX.X, ALU.add)
            dve.tensor_scalar(usedj[0:1], ej[0:1], float(NE), None, ALU.is_lt)
            step(dve.tensor_scalar(e_f, ej[0:1], float(NE - 1), None, ALU.min))
            step(dve.tensor_tensor(tmpj[0:1], jr, stj[0:1], ALU.subtract))
            step(dve.tensor_scalar(tmpj[0:1], tmpj[0:1], float(P), None, ALU.mult))
            step(dve.scalar_tensor_tensor(tmpj[0:1], ej[0:1], float(QROWS), tmpj[0:1], ALU.mult, ALU.add))
            step(dve.tensor_tensor(tmpj[0:1], tmpj[0:1], jd, ALU.subtract))
            step(dve.tensor_tensor(tmpj[0:1], tmpj[0:1], usedj[0:1], ALU.mult))
            dve.tensor_tensor(row_f, tmpj[0:1], jd, ALU.add)
            dve.memset(need_f[:, 0:WB], 1.0)
            step(dve.tensor_tensor(need_f[:, WB:NJT], e_f[:, WB:NJT], e_f[:, 0:NJT - WB], ALU.not_equal))
            dve.tensor_copy(plan_i[0:1, :], plan_f[0:1, :]).then_inc(plan_done, 1)
            step(dve.tensor_scalar(moved, nt[:, 0:NE - 1], float(P), -float(QROWS), ALU.mult, ALU.add))
            for s in range(2):
                step(dve.tensor_tensor(behind, route[:, :, 2 + s].unsqueeze(2).to_broadcast([P, NTILE, NE - 1]),
                                       qbase[:, 1:NE].unsqueeze(1).to_broadcast([P, NTILE, NE - 1]), ALU.is_ge))
                step(dve.tensor_tensor(behind, behind, moved.unsqueeze(1).to_broadcast([P, NTILE, NE - 1]), ALU.mult))
                step(dve.tensor_reduce(shift, behind, AX.X, ALU.add))
                step(dve.tensor_tensor(rows_u[:, :, s], route[:, :, 2 + s], shift, ALU.add))

            def tile(i, r, first):
                j = WB * i + r
                b1 = wex[:, r, WEX - 2 * NF:WEX]
                for half in range(2):
                    dve.wait_ge(f_full[2 * half + 1], j + 1)
                    dve.wait_ge(silu_done[half], j + 1)
                    for f in range(4):
                        ff = 4 * half + f
                        ins = dve.scalar_tensor_tensor(act[:, r, ff, :], VALUE[half][:, f * P:(f + 1) * P],
                                                       b1[:, ff:ff + 1], sg[:, half, f, :], ALU.add, ALU.mult)
                    ins.then_inc(act_done, 1)
                dve.wait_ge(o_full, j + 1)
                if not first:
                    dve.wait_ge(ans_out[r], 16 * i)
                dve.tensor_tensor(yt[:, r], py[:, 0:D], b2b[:, r], ALU.add).then_inc(o_ready, 1)

            for r in range(WB):
                tile(0, r, True)
            with dve.Fori(1, NJ // WB) as i:
                for r in range(WB):
                    tile(i, r, False)

            def slots(i, q):
                for s in range(2):
                    ins = dve.tensor_copy(slot_c[:, q, s * LG:(s + 1) * LG],
                                          rows_u[:, bass.ds(LG * (2 * i + q), LG), s])
                ins.then_inc(idx_ready, 1)

            def finish(i, q, ahead):
                ch = Chain(dve, c_fin, 6, 2 * i + q)
                dve.wait_ge(got[q], 32 * LG * (i + 1))
                dve.wait_ge(x1_back[q], 16 * (i + 1))
                dve.sem_inc(hop, 1)
                if ahead:
                    slots(i + 1, q)
                ch.link(dve.tensor_copy(wv[:, q], route[:, bass.ds(LG * (2 * i + q), LG), :]))
                for k in range(LG):
                    ins = dve.scalar_tensor_tensor(fsum[:, q, k], got1[:, q, k], wv[:, q, k, 0:1], back[:, q, k],
                                                   ALU.mult, ALU.add)
                ch.link(ins)
                for k in range(LG):
                    ins = dve.scalar_tensor_tensor(fsum[:, q, k], got2[:, q, k], wv[:, q, k, 1:2], fsum[:, q, k],
                                                   ALU.mult, ALU.add)
                ins.then_inc(f_sum, 1)
                dve.wait_ge(f_sum, 2 * i + (q + 1))
                for k in range(LG):
                    ins = dve.bn_stats(fst[:, q, k], fsum[:, q, k])
                ch.link(ins)
                dve.sem_inc(hop, 1)
                for k in range(LG):
                    ins = dve.bn_aggr(fmv[:, q, k], fst[:, q, k])
                ch.link(ins)
                dve.tensor_scalar(fve[:, q], fmv[:, q, :, 1], EPS, None, ALU.add).then_inc(f_var, 1)
                dve.wait_ge(f_rs, 2 * i + (q + 1))
                ch.link(dve.reciprocal(frs[:, q], fsd[:, q]))
                if not (isinstance(i, int) and i == 0):
                    dve.wait_ge(out_done[q], 16 * i)
                for k in range(LG):
                    ins = dve.tensor_scalar(fin[:, q, k], fsum[:, q, k], fmv[:, q, k, 0:1], frs[:, q, k:k + 1],
                                            ALU.subtract, ALU.mult)
                ch.link(ins)
                ch.close()
                dve.sem_inc(f_out, 1)

            for q in range(2):
                slots(0, q)
            for q in range(2):
                finish(0, q, True)
            with dve.Fori(1, NB // 2 - 1) as i:
                for q in range(2):
                    finish(i, q, True)
            for q in range(2):
                finish(NB // 2 - 1, q, False)

        @block.gpsimd
        def _(pool):
            own = [0]

            def next_(ins):
                own[0] += 1
                ins.then_inc(c_pool, 1)
                pool.wait_ge(c_pool, own[0])

            next_(pool.memset(zeros[:, :], 0.0))
            for s in range(2):
                row = DUMMY + s * P
                pool.dma_start(queue[row:row + P, :], zeros[:, :]).then_inc(scattered[s], 16)
            next_(pool.memset(ones[:, :], 1.0))
            pool.memset(half_neg[:, :], -0.5)
            pool.iota(jrow_i[:, :], [[1, NJT]], base=0, channel_multiplier=0)
            next_(pool.iota(jdum_i[:, :], [[0, NJT // WB], [P, WB]], base=DUMMY, channel_multiplier=0))
            pool.tensor_copy(jrow[:, :], jrow_i[:, :])
            next_(pool.tensor_copy(jdum[:, :], jdum_i[:, :]))
            pool.tensor_copy(iota_e[:, :], jrow[:, 0:NE])
            pool.tensor_scalar(qbase[:, :], jrow[:, 0:NE], float(QROWS), 0.0, ALU.mult, ALU.add)
            pool.tensor_scalar(count[:, :], jrow[:, 0:NE], float(QROWS), 0.0, ALU.mult, ALU.add)
            pool.affine_select(out=tri_le[:, :], in_=ones[:, :], compare_op=ALU.is_ge, fill=0.0, base=0,
                               pattern=[[1, P]], channel_multiplier=-1)
            pool.affine_select(out=tri_lt[:, :], in_=ones[:, :], compare_op=ALU.is_gt, fill=0.0, base=0,
                               pattern=[[1, P]], channel_multiplier=-1)
            pool.affine_select(out=tri_gt[:, :], in_=ones[:, :], compare_op=ALU.is_gt, fill=0.0, base=0,
                               pattern=[[-1, P]], channel_multiplier=1)
            next_(pool.affine_select(out=ident[:, :], in_=ones[:, :], compare_op=ALU.is_equal, fill=0.0, base=0,
                                     pattern=[[-1, P]], channel_multiplier=1))
            pool.sem_inc(consts, 1)

            def by_head(ap):
                return ap.unsqueeze(2).to_broadcast([ap.shape[0], NH, HD])

            def rsqrt_ln(w):
                pool.wait_ge(ln_var, w + 1)
                pool.tensor_tensor(rs, ve, half_neg[:, :], ALU.pow).then_inc(ln_rs, 1)

            def spread_a(q, kq, k):
                pool.tensor_tensor(tri_a[:, kq], tri_le[:, :].unsqueeze(1).to_broadcast([P, NH, P]),
                                   a_s[:, q, k].unsqueeze(2).to_broadcast([P, NH, P]), ALU.mult).then_inc(tri_ready, 1)

            def end(st):
                pool.wait_ge(sve_ready, st.u)
                pool.tensor_tensor(srs, sve, half_neg[:, :], ALU.pow).then_inc(srs_ready, 1)

            def add_x(st):
                wq = 1 - st.q
                pool.wait_ge(h_ready, st.u)
                pool.wait_ge(xin_in[wq], 16 * ((st.h - 4) if wq == 1 else (st.h - 3)))
                pool.tensor_tensor(ob[:, wq], ob[:, wq], xin[:, wq], ALU.add).then_inc(r_sum, 1)

            def rsqrt_x1(st):
                pool.wait_ge(r_var, st.u - NB)
                pool.tensor_tensor(rrs, rve, half_neg[:, :], ALU.pow).then_inc(r_rs, 1)

            def scatter(st):
                wq = 1 - st.q
                pool.wait_ge(slot_ready, st.u - NB)
                pool.sem_inc(hop, 1)
                for s in range(2):
                    for k in range(NK):
                        m = s * NK + k
                        pool.indirect_dma_start(queue, bass.IndirectOffsetOnAxis(ap=slot[:, wq, m:m + 1], axis=0),
                                                ob[:, wq, k, :], None).then_inc(scattered[wq], 16)

            def operands(st, k):
                q, n, kq, u6 = st.q, 4 * st.u + k, k % 2, 6 * st.u
                pool.wait_ge(pt_free, 8 * st.u + PAIRS.index(f"a{k}") + 1)
                at_least(pool, y_full, n - 1)
                pool.tensor_tensor(dtx[:, kq], xs[:, kq], by_head(dt_s[:, q, k]), ALU.mult).then_inc(dtx_ready, 1)
                if k < NK - 1:
                    pool.wait_ge(wdt_ready, n + 1)
                    at_least(pool, z_full, (u6 + 1) if k == 2 else (u6 - 1 - 2 * k))
                    pool.tensor_tensor(xw[:, kq], xs[:, kq], by_head(wdt[:, kq]), ALU.mult).then_inc(xw_ready, 1)
                at_least(pool, y_free, n - 1)
                pool.tensor_tensor(xd[:, kq], xs[:, kq], by_head(dsk[:, st.layer]), ALU.mult).then_inc(xd_ready, 1)
                if k in (1, 2):
                    pool.wait_ge(z_free, u6 + 2 * k - 1)
                    pool.tensor_tensor(state_d[0:DS], state[0:DS, (k - 1) % 2], by_head(ex[0:DS, kq, 2]),
                                       ALU.mult).then_inc(sd_ready, 1)

            def look_ahead(st, k):
                n = 4 * st.u + k
                at_least(pool, seg_full, 2 * n)
                if k < NK - 1:
                    spread_a(st.q, (k + 1) % 2, k + 1)
                else:
                    pool.wait_ge(a_ready, st.u + 2)
                    spread_a(1 - st.q, 0, 0)

            def gated(st, k):
                q, n, kq, u8 = st.q, 4 * st.u + k, k % 2, 8 * st.u
                if k > 0:
                    pool.wait_ge(z_free, 6 * st.u + 2 * k)
                    pool.wait_ge(xd_ready, n + 1)
                    pool.tensor_tensor(y1[:, kq], y1[:, kq], xd[:, kq], ALU.add).then_inc(ysum_ready, 1)
                pool.wait_ge(y_free, n + 1)
                at_least(pool, pt_free, u8 + (PAIRS.index(f"o{k - 2}") + 1 if k >= 2 else k - 1))
                pool.tensor_tensor(g[:, kq], y2[:, kq], zs[:, q, k].rearrange("p (h d) -> p h d", h=NH),
                                   ALU.mult).then_inc(g_ready, 1)

            def body(st):
                if not st.first:
                    end(st)
                for k in range(NK):
                    operands(st, k)
                    if not (st.last and k == NK - 1):
                        look_ahead(st, k)
                    if k == 0 and st.s3:
                        add_x(st)
                    if k == 3 and not st.last:
                        rsqrt_ln(st.u + 2)
                    gated(st, k)
                    if k == 0 and st.s3:
                        rsqrt_x1(st)
                if st.s3:
                    scatter(st)

            def prologue(st):
                pool.wait_ge(a_ready, 1)
                spread_a(0, 0, 0)
                rsqrt_ln(1)

            def epilogue(st):
                end(st)
                add_x(st)
                rsqrt_x1(st)
                scatter(st)

            rsqrt_ln(0)
            schedule(pool, body, prologue, epilogue)

            def tile(i, r):
                pool.wait_ge(o_ready, WB * i + (r + 1))
                pool.sem_inc(hop, 1)
                pool.dma_start(answer[bass.ds((WB * i + r) * P, P), :], yt[:, r]).then_inc(ans_out[r], 16)

            with pool.Fori(0, NJ // WB) as i:
                for r in range(WB):
                    tile(i, r)

            for s in range(WB):
                pool.wait_ge(ans_out[s], 16 * (NJ // WB))

            def gather(i, q, first):
                pool.wait_ge(idx_ready, 2 * i + (q + 1))
                if not first:
                    pool.wait_ge(f_sum, 2 * i + (q - 1))
                pool.sem_inc(hop, 1)
                for s, dst in enumerate((got1, got2)):
                    for k in range(LG):
                        m = s * LG + k
                        pool.indirect_dma_start(dst[:, q, k, :], None, answer,
                                                bass.IndirectOffsetOnAxis(ap=slot_c[:, q, m:m + 1], axis=0)
                                                ).then_inc(got[q], 16)

            for q in range(2):
                gather(0, q, True)
            with pool.Fori(1, NB // 2) as i:
                for q in range(2):
                    gather(i, q, False)


def kernel(**inputs):
    import numpy as _np
    import concourse.bacc as _bacc
    from concourse import mybir as _mybir
    from concourse.bass_utils import run_bass_kernel_spmd as _run

    def get(name):
        return _np.asarray(inputs["L0_" + name])

    def columns(a, tiles):
        a = a.reshape((a.shape[0], tiles, P) + a.shape[2:])
        return _np.moveaxis(a, 2, 0)

    def by_partition(a, tiles):
        return a.reshape(NE, tiles, P, -1).transpose(0, 2, 1, 3).reshape(NE, P, -1)

    laid = {
        "x": get("attn_x"),
        "w_in": get("attn_in_proj_w").transpose(0, 2, 1),
        "conv_w": columns(get("attn_conv_w"), NC),
        "conv_b": columns(get("attn_conv_b"), NC),
        "ln_w": columns(get("attn_ln_w"), KD),
        "ln_b": columns(get("attn_ln_b"), KD),
        "dt_bias": get("attn_dt_bias"),
        "a_log": get("attn_A_log"),
        "d_skip": get("attn_D"),
        "rms_w": columns(get("attn_rms_w"), NCT),
        "w_out": get("attn_out_proj_w").transpose(0, 2, 1),
        "gate_w": get("ffn_gate_w"),
        "gate_b": get("ffn_gate_b"),
        "w_exp": _np.concatenate([by_partition(get("ffn_w1"), KD), by_partition(get("ffn_w2"), NF),
                                  get("ffn_b1").reshape(NE, 2 * NF, P).transpose(0, 2, 1)], axis=2),
        "b2": get("ffn_b2"),
    }
    nc = _bacc.Bacc("TRN2", target_bir_lowering=False, num_devices=1)
    arrays, args = {}, []
    for name, a in laid.items():
        a = _np.ascontiguousarray(a)
        arrays[f"in_{name}"] = a
        args.append(nc.dram_tensor(f"in_{name}", a.shape, _mybir.dt.from_np(a.dtype), kind="ExternalInput").ap())
    args.append(nc.dram_tensor("out_0", (NTOK, D), F32, kind="ExternalOutput").ap())
    build(nc, *args)
    r = _run(nc, [arrays], core_ids=[0])
    return r.results[0]["out_0"].reshape(NB, T, D)
```

```python
from contextlib import ExitStack

import concourse.bass as bass
from concourse import mybir

F32 = mybir.dt.float32
F16 = mybir.dt.float16
I32 = mybir.dt.int32
U32 = mybir.dt.uint32
ALU = mybir.AluOpType
ACT = mybir.ActivationFunctionType
AX = mybir.AxisListType

P = 128
NB, T, D = 8, 512, 256
NK = T // P
KD = D // P
NH, HD, DS = 8, 64, 64
DI = NH * HD
NCT = DI // P
NC = NCT + 1
TAPS = 4
DPROJ = 2 * DI + 2 * DS + NH
OX, OBC, ODT = DI, 2 * DI, 2 * DI + 2 * DS
EPS = 1e-5
NE, FF = 8, 1024
NF = FF // P
NTOK = NB * T
NTILE = NTOK // P
W1N, W2N = KD * 2 * FF, NF * D
WEX = W1N + W2N
S1, S2 = 16.0, 32.0
QROWS = NTOK + P
DUMMY = NE * QROWS
WB = 3
NJ = (2 * NTOK) // P + NE - 1
NJ += -NJ % WB
NJT = NJ + WB
LG = NK

PLAIN = ["dt", "c4", "c0", "c1", "c2", "c3", "z0", "z1", "z2", "ln0", "ln1", "z3"]
WITH3 = ["dt", "c4", "c0", "c1", "c2", "c3", "t0", "t1", "z0", "lg", "z1", "z2", "rk", "ln0", "ln1", "z3"]
FIRST = ["ln0", "ln1"] + PLAIN[:-3] + ["ln0n", "ln1n", "z3"]
ONLY3 = ["t0", "t1", "lg", "rk"]
LAST_HB = 109
USES = {"a0": -1, "a1": 1, "o0": 2, "a2": 3, "o1": 4, "a3": 5, "o2": 6, "o3": 8}
CONV_ORDER = ["c4", "c0", "c1", "c2", "c3"]
MAMBA_UNITS = 2 * NB
NCOUNT_Z = 2 * (NK - 1)


def at_least(eng, sem, count):
    if isinstance(count, int) and count <= 0:
        return
    eng.wait_ge(sem, count)


class Chain:

    def __init__(self, eng, sem, per, unit):
        self.eng, self.sem, self.base, self.per, self.n = eng, sem, per * unit, per, 0

    def link(self, ins):
        self.n += 1
        ins.then_inc(self.sem, 1)
        self.eng.wait_ge(self.sem, self.base + self.n)

    def close(self):
        assert self.n == self.per, (self.n, self.per)


def quarter(n):
    a, b = n * WEX // 4, (n + 1) * WEX // 4
    cuts = [a, W1N, b] if a < W1N < b else [a, b]
    return [(u, v, S1 if v <= W1N else S2) for u, v in zip(cuts, cuts[1:])]


class Step:

    def __init__(self, u, half, layer, parity, fills, half_base, first=False, last=False, s3=False):
        self.u, self.h, self.layer, self.q = u, half, layer, parity
        self.fills, self.hb = fills, half_base
        self.first, self.last, self.s3 = first, last, s3
        self.epilogue = isinstance(u, int) and u >= MAMBA_UNITS
        self.next_layer = 1 if (layer == 1 or (isinstance(u, int) and u == NB - 1)) else 0

    def fill(self, name):
        p = self.fills.index(name)
        return p % 2, self.hb + p // 2


class Chunk:

    def __init__(self, st, k):
        ahead = 1 if k == NK else 0
        self.k, self.u = k % NK, st.u + ahead
        self.q = (st.q + ahead) % 2
        self.kq, self.n = k % 2, NK * self.u + self.k
        self.layer = st.next_layer if ahead else st.layer
        self.u6, self.st = (NCOUNT_Z * self.u), st

    def use(self, kind):
        off = USES[f"{kind}{self.k}"]
        if isinstance(self.u, int):
            if self.u == 0 and off < 0:
                off = 0
            if self.u == MAMBA_UNITS - 1 and off == 8:
                off = 7
        return 8 * self.u + off


def schedule(eng, body, prologue, epilogue):
    prologue(Step(-1, -1, 0, 1, FIRST, 0))
    body(Step(0, 0, 0, 0, PLAIN, 7, first=True))
    with eng.Fori(0, 3) as i:
        for r in range(2):
            body(Step(2 * i + (1 + r), i + r, 0, (1 + r) % 2, PLAIN, 6 * (2 * i) + (13 + 6 * r)))
    body(Step(7, 3, 0, 1, PLAIN, 49))
    body(Step(8, 4, 1, 0, PLAIN, 55))
    with eng.Fori(0, 3) as i:
        for r in range(2):
            body(Step(2 * i + (9 + r), i + (4 + r), 1, (1 + r) % 2, WITH3, 16 * i + (61 + 8 * r), s3=True))
    body(Step(15, 7, 1, 1, ONLY3, LAST_HB, last=True, s3=True))
    epilogue(Step(16, 8, 1, 0, ONLY3, LAST_HB + 2, s3=True))


def build(nc, x, w_in, conv_w, conv_b, ln_w, ln_b, dt_bias, a_log, d_skip, rms_w, w_out,
          gate_w, gate_b, w_exp, b1, b2, out):
    h1 = nc.dram_tensor("h1", [NB, T, D], F32, kind="Internal").ap()
    hx = nc.dram_tensor("hx", [NB, T, D], F32, kind="Internal").ap()
    x1_rows = nc.dram_tensor("x1_rows", [NTOK, D], F32, kind="Internal").ap()
    queue = nc.dram_tensor("queue", [DUMMY + 4 * P, D], F32, kind="Internal").ap()
    answer = nc.dram_tensor("answer", [NJ * P, D], F32, kind="Internal").ap()

    ctx = ExitStack()
    with ctx:
        def sb(name, shape, dt=F32):
            return ctx.enter_context(nc.sbuf_tensor(name, shape, dt))

        def sem(name):
            return ctx.enter_context(nc.semaphore(name))

        ident = sb("ident", [P, P])
        tri_le = sb("tri_le", [P, P])
        tri_gt = sb("tri_gt", [P, P])
        tri_lt = sb("tri_lt", [P, P])
        ones = sb("ones", [P, P])
        zeros = sb("zeros", [P, D])
        half_neg = sb("half_neg", [P, NK])
        iota_e = sb("iota_e", [P, NE])
        qbase = sb("qbase", [P, NE])
        route = sb("route", [P, NTILE, 4])
        count = sb("count", [P, NE])
        jrow = sb("jrow", [P, NJT])
        jdum = sb("jdum", [P, NJT])
        jrow_i = sb("jrow_i", [P, NJT], I32)
        jdum_i = sb("jdum_i", [P, NJT], I32)
        sign_i = sb("sign_i", [P, NE], I32)
        sign = sb("sign", [P, NE])
        ARENA = 49600
        arena = sb("arena", [P, ARENA])

        def carver():
            at = [0]

            def carve(*shape, dt=F32):
                n = 1
                for s in shape:
                    n *= s
                if dt is F16:
                    n //= 2
                ap = arena[:, at[0]:at[0] + n]
                at[0] += n
                assert at[0] <= ARENA, at[0]
                if dt is not F32:
                    ap = ap.bitcast(dt)
                if len(shape) == 2:
                    ap = ap.rearrange("p (a b) -> p a b", a=shape[0])
                elif len(shape) == 3:
                    ap = ap.rearrange("p (a b c) -> p a b c", a=shape[0], b=shape[1])
                elif len(shape) == 4:
                    ap = ap.rearrange("p (a b c d) -> p a b c d", a=shape[0], b=shape[1], c=shape[2])
                return ap
            return carve

        carve = carver()
        win = carve(2, KD, DPROJ)
        hln = carve(2, NK, D)
        uT = carve(2, KD, T)
        acc, th = carve(2, T), carve(2, T)
        zt = carve(2, DI)
        xcT = carve(2, NCT, T)
        wout = carve(2, NCT, D)
        cw, cb = carve(2, NC, TAPS), carve(2, NC)
        lnw, lnb = carve(MAMBA_UNITS + 1, KD), carve(MAMBA_UNITS + 1, KD)
        rmsw = carve(2, NCT)
        dtb, aneg, dsk = carve(2, NH), carve(2, NH), carve(2, NH)
        gw, gb = carve(KD, NE), carve(NE)
        hres = carve(2, NK, D)
        bT, cT = carve(2, T), carve(2, T)
        zs = carve(2, NK, DI)
        tri_a = carve(2, NH, P)
        xs, dtx, xw, xd = carve(2, NH, HD), carve(2, NH, HD), carve(2, NH, HD), carve(2, NH, HD)
        decay, mix = carve(2, NH, P), carve(2, NH, P)
        cbm = carve(2, P)
        bs = carve(2, DS)
        ex = carve(2, 3, NH)
        wdt = carve(2, NH)
        y1, y2, g = carve(2, NH, HD), carve(2, NH, HD), carve(2, NH, HD)
        state, state_d = carve(2, NH, HD), carve(NH, HD)
        gT = carve(2, NCT, P)
        junk = carve(DI)
        ob = carve(2, NK, D)
        x1T = carve(KD, T)
        st6, mv, ve, rs = carve(NK, 6), carve(NK, 2), carve(NK), carve(NK)
        rst6, rmv, rve, rrs = carve(NK, 6), carve(NK, 2), carve(NK), carve(NK)
        ss, sve, srs = carve(2, NK), carve(NK), carve(NK)
        dtr, nab, e1, l1 = carve(NK, NH), carve(NK, NH), carve(NK, NH), carve(NK, NH)
        dt_s, a_s = carve(2, NK, NH), carve(2, NK, NH)
        logit, top8 = carve(NK, NE), carve(NK, 8)
        top_i, top_f = carve(NK, 8, dt=U32), carve(NK, 8)
        gap, p2 = carve(NK), carve(NK)
        oh1, oh2, oh = carve(NK, NE), carve(NK, NE), carve(NK, NE)
        pos, pick, base = carve(NK, NE), carve(2, NK, NE), carve(NK, NE)
        pw = carve(NK, 4)
        slot = carve(2, 2 * NK, dt=U32)
        x1b = carve(2, NK, D)

        carve = carver()
        w_raw = carve(WEX)
        w_split = carve(2, 2, WEX, dt=F16)
        b1a, b1v = carve(NE, 2 * NF), carve(NE, NF)
        b2a = carve(NE, D)
        xq = carve(WB, D)
        xh, xl = carve(WB, KD, P, dt=F16), carve(WB, KD, P, dt=F16)
        sg = carve(2, 4, P)
        glu = carve(2, 4 * P)
        acth, actl = carve(WB, NF, P, dt=F16), carve(WB, NF, P, dt=F16)
        yt = carve(WB, D)
        cnt, moved = carve(NE), carve(NE - 1)
        behind, shift = carve(NTILE, NE - 1), carve(NTILE)
        rows_u = carve(NTILE, 2)
        nt, end = carve(NE), carve(NE)
        tcmp = carve(NE, NTILE)
        j128 = carve(NTILE)
        cmp_, cmp_nt = carve(NJT, NE), carve(NJT, NE)
        ej, stj, usedj, tmpj = carve(NJT), carve(NJT), carve(NJT), carve(NJT)
        plan_f = carve(3 * NJT + 2 * NE)
        plan_i = carve(3 * NJT + 2 * NE, dt=I32)
        slot_c = carve(2, 2 * LG, dt=U32)
        wv = carve(2, LG, 4)
        back, got1, got2 = carve(2, LG, D), carve(2, LG, D), carve(2, LG, D)
        fsum, fin = carve(2, LG, D), carve(2, LG, D)
        fst, fmv = carve(2, LG, 6), carve(2, LG, 2)
        fve, fsd, frs = carve(2, LG), carve(2, LG), carve(2, LG)

        pa = [ctx.enter_context(nc.psum_tensor(f"pa{i}", [P, T], F32)) for i in range(2)]
        pe_ = [ctx.enter_context(nc.psum_tensor(f"pe{i}", [P, T], F32)) for i in range(2)]
        pt = ctx.enter_context(nc.psum_tensor("pt", [P, T], F32))
        pm = ctx.enter_context(nc.psum_tensor("pm", [P, T], F32))
        py = ctx.enter_context(nc.psum_tensor("py", [P, T], F32))
        pz = ctx.enter_context(nc.psum_tensor("pz", [P, T], F32))
        CBT, BTR, CS = pm[:, 0:P], pm[:, P:P + DS], pm[:, P + DS:P + DS + 3 * NH]
        OUT = pm[:, T - D:T]

        consts = sem("consts")
        params = sem("params")
        prepared = sem("prepared")
        hln_in = [sem("hln_in0"), sem("hln_in1")]
        hres_in = [sem("hres_in0"), sem("hres_in1")]
        ln_var = sem("ln_var")
        ln_rs = sem("ln_rs")
        ln_done = sem("ln_done")
        a_full = [sem("a_full0"), sem("a_full1")]
        a_free = [sem("a_free0"), sem("a_free1")]
        sp_in = sem("sp_in")
        sp_ln = sem("sp_ln")
        a_ready = sem("a_ready")
        acc_init = sem("acc_init")
        tanh_ready = sem("tanh_ready")
        xc_done = sem("xc_done")
        zt_ready = sem("zt_ready")
        tri_ready = sem("tri_ready")
        pt_full, pt_free = sem("pt_full"), sem("pt_free")
        pm_full, pm_free = sem("pm_full"), sem("pm_free")
        seg_full, e_free = sem("seg_full"), sem("e_free")
        pm_read = sem("pm_read")
        wdt_ready = sem("wdt_ready")
        m_done = sem("m_done")
        dtx_ready = sem("dtx_ready")
        xw_ready = sem("xw_ready")
        xd_ready = sem("xd_ready")
        y_full, y_free = sem("y_full"), sem("y_free")
        z_full, z_free = sem("z_full"), sem("z_free")
        s_ready = sem("s_ready")
        sd_ready = sem("sd_ready")
        ysum_ready = sem("ysum_ready")
        g_ready = sem("g_ready")
        ss_ready = sem("ss_ready")
        sve_ready, srs_ready = sem("sve_ready"), sem("srs_ready")
        h_ready = sem("h_ready")
        stored = [sem("stored0"), sem("stored1")]
        hx_ready = sem("hx_ready")
        hx_out = [sem("hx_out0"), sem("hx_out1")]
        r_var, r_rs, x1_ready = sem("r_var"), sem("r_rs"), sem("x1_ready")
        gap_ready, p2_ready = sem("gap_ready"), sem("p2_ready")
        oh_ready = sem("oh_ready")
        slot_ready = sem("slot_ready")
        scattered = [sem("scattered0"), sem("scattered1")]
        c_dve1, c_dve2, c_dve3 = sem("c_dve1"), sem("c_dve2"), sem("c_dve3")
        c_act, c_prep, c_pool = sem("c_act"), sem("c_prep"), sem("c_pool")
        hop = sem("hop")
        plan_done = sem("plan_done")
        padded = sem("padded")
        w_raw_in = sem("w_raw_in")
        w_have = sem("w_have")
        bias_in = sem("bias_in")
        xh_ready, x_done = sem("xh_ready"), sem("x_done")
        high0 = sem("high0")
        c_glu = sem("c_glu")
        xq_in = [sem(f"xq_in{i}") for i in range(WB)]
        f_t_full, f_t_free = sem("f_t_full"), sem("f_t_free")
        f_full = [sem(f"f_full{i}") for i in range(4)]
        silu_done = [sem("silu_done0"), sem("silu_done1")]
        act_done = sem("act_done")
        o_full, o_ready = sem("o_full"), sem("o_ready")
        ans_out = [sem(f"ans_out{i}") for i in range(WB)]
        c_plan = sem("c_plan")
        idx_ready = sem("idx_ready")
        x1_back = [sem("x1_back0"), sem("x1_back1")]
        got = [sem("got0"), sem("got1")]
        f_sum, f_var, f_rs, f_out = sem("f_sum"), sem("f_var"), sem("f_rs"), sem("f_out")
        out_done = [sem("out_done0"), sem("out_done1")]
        c_fin = sem("c_fin")

        N_PARAMS = 16
        N_CONSTS = 1


        GATE, VALUE = [pe_[0], pe_[1]], [pa[0], pa[1]]

        def rows(dram, b):
            return dram[b].rearrange("(k p) d -> p k d", p=P)

        def over_p(ap, k=None):
            return ap.unsqueeze(2).to_broadcast([ap.shape[0], NH, HD])

        block = ctx.enter_context(nc.Block())

        @block.sync
        def _(sp):
            def turned(v):
                if v == 0:
                    return 1, 1
                return 0, 1 + 6 * v if v <= 10 else 69 + 8 * (v - 11)

            def load_hln(w):
                q = w % 2
                if w >= 2:
                    bank, fills = turned(w - 2)
                    sp.wait_ge(a_full[bank], fills)
                if w < NB:
                    sp.dma_start(hln[:, q], rows(x, w)).then_inc(hln_in[q], 16)
                else:
                    b = min(w - NB, NB - 1)
                    sp.wait_ge(stored[b % 2], 16 * (b // 2 + 1) + 16)
                    sp.dma_start(hln[:, q], rows(h1, b)).then_inc(hln_in[q], 16)

            load_hln(0)
            n_params = [0]

            def param(dst, src):
                sp.dma_start(dst, src).then_inc(params, 16)
                n_params[0] += 1

            for dst, src in ((lnw, ln_w), (lnb, ln_b)):
                param(dst[:, 0:NB], src[:, 0:1].to_broadcast([P, NB, KD]))
                param(dst[:, NB:2 * NB + 1], src[:, 1:2].to_broadcast([P, NB + 1, KD]))
            param(dtb, dt_bias.unsqueeze(0).to_broadcast([P, 2, NH]))
            param(aneg, a_log.unsqueeze(0).to_broadcast([P, 2, NH]))
            param(dsk, d_skip.unsqueeze(0).to_broadcast([P, 2, NH]))
            param(cw, conv_w)
            param(cb, conv_b)
            param(rmsw, rms_w)
            param(gw, gate_w.rearrange("(k p) e -> p k e", p=P))
            param(gb, gate_b.unsqueeze(0).to_broadcast([P, NE]))
            param(win[:, 0], w_in[0].rearrange("(k p) n -> p k n", p=P))
            load_hln(1)
            param(wout[:, 0], w_out[0].rearrange("(k p) n -> p k n", p=P))
            param(wout[:, 1], w_out[1].rearrange("(k p) n -> p k n", p=P))
            param(win[:, 1], w_in[1].rearrange("(k p) n -> p k n", p=P))
            assert n_params[0] == N_PARAMS
            load_hln(2)
            sp.wait_ge(consts, N_CONSTS)
            for s in range(2):
                row = DUMMY + (2 + s) * P
                sp.dma_start(queue[row:row + P, :], zeros[:, :]).then_inc(stored[s], 16)
            for u in range(MAMBA_UNITS + 1):
                q = u % 2
                if u < MAMBA_UNITS:
                    at_least(sp, h_ready, u - 1)
                    if u >= 2:
                        sp.wait_ge(hx_out[q], 16 * (min(u - 2, NB - 2 + q) // 2 + 1))
                    sp.dma_start(hres[:, q], rows(x, u) if u < NB else rows(hx, u - NB)).then_inc(hres_in[q], 16)
                if 1 <= u <= NB:
                    sp.wait_ge(h_ready, u)
                    sp.dma_start(rows(h1, u - 1), ob[:, 1 - q]).then_inc(stored[1 - q], 16)
                    sp.wait_ge(hx_ready, u)
                    sp.dma_start(rows(hx, u - 1), hres[:, 1 - q]).then_inc(hx_out[1 - q], 16)
                if u > NB:
                    b = u - 1 - NB
                    sp.wait_ge(x1_ready, b + 1)
                    sp.dma_start(x1_rows[b * T:(b + 1) * T, :].rearrange("(k p) d -> p k d", p=P),
                                 x1b[:, 1 - q]).then_inc(stored[1 - q], 16)
                if u + 3 <= MAMBA_UNITS:
                    load_hln(u + 3)

            sp.wait_ge(plan_done, 1)
            for e in range(NE):
                end_e = sp.value_load(plan_i[0:1, 3 * NJT + e:3 * NJT + e + 1], min_val=0, max_val=NTOK)
                sp.dma_start(queue[bass.ds(end_e + e * QROWS, P), :], zeros[:, :]).then_inc(padded, 16)
            sp.wait_ge(padded, 16 * NE)
            for s in range(2):
                sp.wait_ge(scattered[s], 16 * 2 * NK * (NB // 2) + 16)
                sp.wait_ge(stored[s], 16 * NB + 16)

            def load_rows(i, r):
                row = sp.value_load(plan_i[0:1, bass.ds(WB * i + r, 1)], min_val=0, max_val=DUMMY + (WB - 1) * P)
                sp.dma_start(xq[:, r % WB], queue[bass.ds(row, P), :]).then_inc(xq_in[r % WB], 16)

            for r in range(WB):
                load_rows(0, r)
            sp.dma_start(b1a, b1).then_inc(bias_in, 16)
            sp.dma_start(b2a, b2.unsqueeze(0).to_broadcast([P, NE, D])).then_inc(bias_in, 16)
            with sp.Fori(0, NJ // WB) as i:
                for r in range(WB):
                    sp.wait_ge(o_ready, WB * i + (r + 2))
                    sp.sem_inc(hop, 1)
                    sp.dma_start(answer[bass.ds((WB * i + r) * P, P), :], yt[:, r]).then_inc(ans_out[r], 16)
                    load_rows(i + 1, r)

            for s in range(WB):
                sp.wait_ge(ans_out[s], 16 * (NJ // WB))

            def load_back(i, q):
                sp.dma_start(back[:, q], x1_rows[bass.ds((2 * i + q) * T, T), :].rearrange(
                    "(k p) d -> p k d", p=P)).then_inc(x1_back[q], 16)

            def store_out(i, q):
                sp.wait_ge(f_out, 2 * i + (q + 1))
                sp.sem_inc(hop, 1)
                sp.dma_start(out[bass.ds((2 * i + q) * T, T), :].rearrange("(k p) d -> p k d", p=P),
                             fin[:, q]).then_inc(out_done[q], 16)

            for q in range(2):
                load_back(0, q)
            with sp.Fori(1, NB // 2) as i:
                for q in range(2):
                    sp.wait_ge(f_sum, 2 * i + (q - 1))
                    sp.sem_inc(hop, 1)
                    load_back(i, q)
                    store_out(i - 1, q)
            for q in range(2):
                store_out(NB // 2 - 1, q)
            for q in range(2):
                sp.wait_ge(out_done[q], 16 * (NB // 2))

        @block.tensor
        def _(pe):
            def fill(st, name, product):
                bank, before = st.fill(name)
                at_least(pe, a_free[bank], before)
                product(pa[bank]).then_inc(a_full[bank], 1)

            def s1_fill(st, name):
                l, vq = st.next_layer, 1 - st.q
                v = st.u + 1
                if name[:2] == "ln":
                    d, ahead = int(name[2]), not (st.u == -1 and len(name) == 3) if isinstance(st.u, int) else True
                    w, wq = (st.u + 2, st.q) if ahead else (0, 0)
                    if d == 0:
                        pe.wait_ge(ln_done, w + 1)

                    def go(bank):
                        for k in range(NK):
                            ins = pe.transpose(bank[:, k * P:(k + 1) * P], hln[:, wq, k, d * P:(d + 1) * P], ident[:, :])
                        return ins
                elif name == "dt":
                    if isinstance(v, int) and v == 0:
                        pe.wait_ge(a_free[0], 1)
                        pe.wait_ge(a_free[1], 1)
                    else:
                        pe.wait_ge(a_free[0], st.hb)
                        pe.wait_ge(a_free[1], st.hb - 1)
                    if isinstance(v, int) and v == 0:
                        pe.wait_ge(params, 16 * N_PARAMS)

                    def go(bank):
                        for k in range(NK):
                            for d in range(KD):
                                ins = pe.matmul(bank[:, k * NH:(k + 1) * NH], uT[:, vq, d, k * P:(k + 1) * P],
                                                win[:, l, d, ODT:ODT + NH], start=(d == 0), stop=(d == KD - 1))
                        return ins
                elif name[0] == "c":
                    c = int(name[1])

                    def go(bank):
                        for d in range(KD):
                            ins = pe.matmul(bank[:, :], win[:, l, d, OX + c * P:OX + (c + 1) * P], uT[:, vq, d, :],
                                            start=(d == 0), stop=(d == KD - 1))
                        return ins
                else:
                    k = int(name[1])

                    def go(bank):
                        for d in range(KD):
                            ins = pe.matmul(bank[:, :], uT[:, vq, d, k * P:(k + 1) * P], win[:, l, d, 0:DI],
                                            start=(d == 0), stop=(d == KD - 1))
                        return ins
                fill(st, name, go)

            def s3_fill(st, name):
                w_q = 1 - st.q
                if name in ("t0", "t1"):
                    d = int(name[1])
                    if d == 0:
                        pe.wait_ge(x1_ready, st.u - NB)

                    def go(bank):
                        for k in range(NK):
                            ins = pe.transpose(bank[:, k * P:(k + 1) * P], x1b[:, w_q, k, d * P:(d + 1) * P], ident[:, :])
                        return ins
                elif name == "lg":
                    for n in ("t0", "t1"):
                        bank, before = st.fill(n)
                        pe.wait_ge(a_free[bank], before + 1)

                    def go(bank):
                        for k in range(NK):
                            for d in range(KD):
                                ins = pe.matmul(bank[:, k * NE:(k + 1) * NE], x1T[:, d, k * P:(k + 1) * P],
                                                gw[:, d, :], start=(d == 0), stop=(d == KD - 1))
                        return ins
                else:
                    pe.wait_ge(oh_ready, st.u - NB)

                    def go(bank):
                        pe.matmul(bank[:, 0:NK * NE], tri_lt[:, :], oh.rearrange("p k e -> p (k e)"), start=True, stop=True)
                        return pe.matmul(bank[:, NK * NE:2 * NK * NE], ones[:, :], oh.rearrange("p k e -> p (k e)"),
                                         start=True, stop=True)
                fill(st, name, go)

            def do_fills(st, names):
                for n in names:
                    if n in ONLY3:
                        s3_fill(st, n)
                    else:
                        s1_fill(st, n)

            def chunk_a(c):
                q, n, k = c.q, c.n, c.k
                tk = slice(k * P, (k + 1) * P)
                if k == 0:
                    pe.wait_ge(xc_done, 5 * c.u + 5)
                    pe.wait_ge(a_ready, c.u + 1)
                at_least(pe, pt_free, c.use("a"))
                for t in range(NCT):
                    ins = pe.transpose(pt[:, t * P:(t + 1) * P], xcT[:, q, t, tk], ident[:, :])
                ins.then_inc(pt_full, 1)
                at_least(pe, pm_free, c.use("a"))
                for s, w in enumerate((tri_le, tri_gt, ones)):
                    pe.matmul(CS[:, s * NH:(s + 1) * NH], w[:, :], a_s[:, q, k, :], start=True, stop=True)
                pe.transpose(BTR, bT[0:DS, q, tk], ident[0:DS, 0:DS])
                pe.matmul(CBT, bT[0:DS, q, tk], cT[0:DS, q, tk], start=True, stop=True).then_inc(pm_full, 1)
                pe.wait_ge(tri_ready, n + 1)
                for h in range(2):
                    at_least(pe, e_free, 2 * n - 1 + h)
                    pe.matmul(pe_[h][:, :], tri_gt[:, :],
                              tri_a[:, c.kq, 4 * h:4 * h + 4, :].rearrange("p h t -> p (h t)"),
                              start=True, stop=True).then_inc(seg_full, 1)

            def chunk_b(c):
                q, n, k, kq, u6 = c.q, c.n, c.k, c.kq, c.u6
                if k > 0:
                    pe.wait_ge(z_free, u6 + 2 * k - 1)
                    pe.matmul(pz[:, :], cT[0:DS, q, k * P:(k + 1) * P],
                              state[0:DS, (k - 1) % 2].rearrange("p h d -> p (h d)"),
                              start=True, stop=True).then_inc(z_full, 1)
                pe.wait_ge(m_done, n + 1)
                pe.wait_ge(dtx_ready, n + 1)
                at_least(pe, y_free, n)
                for h in range(NH):
                    ins = pe.matmul(py[:, h * HD:(h + 1) * HD], mix[:, kq, h, :], dtx[:, kq, h, :], start=True, stop=True)
                ins.then_inc(y_full, 1)
                if k < NK - 1:
                    pe.wait_ge(xw_ready, 3 * c.u + k + 1)
                    at_least(pe, z_free, u6 + 2 * k)
                    pe.wait_ge(pm_read, n + 1)
                    pe.matmul(pz[0:DS, :], bs[:, kq, :], xw[:, kq].rearrange("p h d -> p (h d)"),
                              start=True, stop=True).then_inc(z_full, 1)

            def chunk_c(c):
                pe.wait_ge(g_ready, c.n + 1)
                pe.wait_ge(pt_free, c.use("o"))
                gk = g[:, c.kq].rearrange("p h d -> p (h d)")
                for t in range(NCT):
                    ins = pe.transpose(pt[:, t * P:(t + 1) * P], gk[:, t * P:(t + 1) * P], ident[:, :])
                ins.then_inc(pt_full, 1)

            def chunk_d(c):
                pe.wait_ge(pt_free, c.use("o") + 1)
                pe.wait_ge(pm_free, c.use("o"))
                for t in range(NCT):
                    ins = pe.matmul(OUT, gT[:, c.kq, t, :], wout[:, c.layer, t, :], start=(t == 0), stop=(t == NCT - 1))
                ins.then_inc(pm_full, 1)

            def body(st):
                s1, s3 = not st.last, st.s3
                c = [Chunk(st, k) for k in range(NK + 1)]
                do_fills(st, ["dt", "c4", "c0"] * s1)
                chunk_b(c[0])
                chunk_a(c[1])
                chunk_c(c[0])
                do_fills(st, ["c1"] * s1)
                chunk_d(c[0])
                do_fills(st, ["c2"] * s1)
                chunk_b(c[1])
                chunk_a(c[2])
                chunk_c(c[1])
                do_fills(st, ["c3"] * s1)
                chunk_d(c[1])
                do_fills(st, ["t0", "t1"] * s3 + ["z0"] * s1)
                chunk_b(c[2])
                chunk_a(c[3])
                chunk_c(c[2])
                do_fills(st, ["lg"] * s3 + ["z1"] * s1)
                chunk_d(c[2])
                do_fills(st, ["z2"] * s1 + ["rk"] * s3)
                chunk_b(c[3])
                if s1:
                    chunk_a(c[4])
                chunk_c(c[3])
                do_fills(st, ["ln0", "ln1"] * s1)
                chunk_d(c[3])
                do_fills(st, ["z3"] * s1)

            def prologue(st):
                do_fills(st, FIRST)
                chunk_a(Chunk(st, NK))

            pe.wait_ge(consts, N_CONSTS)
            pe.wait_ge(prepared, 1)
            schedule(pe, body, prologue, lambda st: do_fills(st, ONLY3))

            def part(p, hl, first, n):
                return w_split[:, bass.ds(p, 1), hl, first:first + n].rearrange("p a b -> p (a b)")

            def parities(i):
                v = pe.value_load(plan_i[0:1, bass.ds(i + 2 * NJT, 1)], min_val=0, max_val=15)
                return [v % 2, (v // 2) % 2, (v // 4) % 2, v // 8]

            def turn(i, r):
                b = r % WB
                pe.wait_ge(xq_in[b], 16 * (i + (r // WB + 1)))
                at_least(pe, x_done, WB * i + r)
                for d in range(KD):
                    ins = pe.transpose(pt[:, d * P:(d + 1) * P], xq[:, b, d * P:(d + 1) * P], ident[:, :])
                ins.then_inc(f_t_full, 1)

            def hidden(i, r, p):
                j = WB * i + r
                pe.wait_ge(x_done, j + 1)
                pe.sem_inc(hop, 1)
                with pe.If(p < 1):
                    products(j, r, 0)
                with pe.Else():
                    products(j, r, 1)

            def products(j, r, p):
                for half in range(2):
                    for bank, first, full in ((GATE[half], FF, 2 * half), (VALUE[half], 0, 2 * half + 1)):
                        if full % 2 == 0:
                            at_least(pe, silu_done[half], j)
                        else:
                            at_least(pe, act_done, 2 * j - 1 + half)
                        for f in range(4):
                            col = first + (4 * half + f) * P
                            passes = [(hl, x, d) for d in range(KD) for hl, x in ((0, xh), (0, xl), (1, xh))]
                            for n, (hl, x, d) in enumerate(passes):
                                ins = pe.matmul(bank[:, f * P:(f + 1) * P], w_split[:, p, hl, d * 2 * FF + col:d * 2 * FF + col + P],
                                                x[:, r, d, :], start=(n == 0), stop=(n == len(passes) - 1))
                        ins.then_inc(f_full[full], 1)

            def result(i, r, p):
                b = r % WB
                pe.wait_ge(o_ready, WB * i + (r + 1))
                for half in range(2):
                    pe.wait_ge(act_done, 2 * (WB * i + r) + half + 1)
                    passes = [(hl, a, f) for f in range(4 * half, 4 * half + 4) for hl, a in ((0, acth), (0, actl), (1, acth))]
                    for n, (hl, a, f) in enumerate(passes):
                        ins = pe.matmul(py[:, 0:D], a[:, b, f, :], part(p, hl, W1N + f * D, D),
                                        start=(half == 0 and n == 0), stop=(half == 1 and n == len(passes) - 1))
                ins.then_inc(o_full, 1)

            turn(0, 0)
            pe.wait_ge(plan_done, 1)
            pe.sem_inc(hop, 1)
            p = parities(0)
            for r in range(WB):
                hidden(0, r, p[r])
                turn(0, r + 1)
                if r > 0:
                    result(0, r - 1, p[r - 1])
            with pe.Fori(1, NJ // WB) as i:
                p = parities(i)
                for r in range(WB):
                    hidden(i, r, p[r])
                    turn(i, r + 1)
                    result(i - 1 if r == 0 else i, (r - 1) % WB, p[(r - 1) % 4])
            p = parities(NJ // WB)
            result(NJ // WB - 1, WB - 1, p[3])

        @block.scalar
        def _(act_e):
            e = act_e

            def wait_fill(st, name):
                bank, before = st.fill(name)
                e.wait_ge(a_full[bank], before + 1)
                return bank, before

            def ln_out(st, name):
                bank, _ = wait_fill(st, name)
                d, ahead = int(name[2]), not (st.u == -1 and len(name) == 3) if isinstance(st.u, int) else True
                w, wq = (st.u + 2, st.q) if ahead else (0, 0)
                e.sem_inc(hop, 1)
                e.activation(uT[:, wq, d, :], pa[bank][:, :], ACT.Identity,
                             scale=lnw[:, bass.ds(w, 1), d], bias=lnb[:, bass.ds(w, 1), d]).then_inc(a_free[bank], 1)

            def spread(st, k):
                q, m = (st.q + k // NK) % 2, 4 * st.u + k
                at_least(e, seg_full, 2 * (m - 1))
                if k == NK:
                    e.wait_ge(a_ready, st.u + 2)
                for h in range(NH):
                    ins = e.activation(tri_a[:, k % 2, h], tri_le[:, :], ACT.Copy, scale=a_s[:, q, k % NK, h:h + 1])
                ins.then_inc(tri_ready, 1)

            def conv_first(st, c):
                idx = CONV_ORDER.index(c)
                l, m, mq = st.next_layer, 5 * (st.u + 1) + idx, (1 - st.q + idx) % 2
                bank, _ = wait_fill(st, c)
                at_least(e, xc_done, m - 1)
                ct = int(c[1])
                e.activation(acc[:, mq], pa[bank][:, :], ACT.Identity, scale=cw[:, l, ct, TAPS - 1:TAPS],
                             bias=cb[:, l, ct:ct + 1]).then_inc(acc_init, 1)

            def conv_tanh(st, c):
                idx = CONV_ORDER.index(c)
                mq = (1 - st.q + idx) % 2
                bank, before = st.fill(c)
                e.wait_ge(a_free[bank], before + 1)
                e.activation(th[:, mq], acc[:, mq], ACT.Tanh).then_inc(tanh_ready, 1)

            def z_tanh(st, k):
                bank, _ = wait_fill(st, f"z{k}")
                if k >= 2:
                    b2_, before = st.fill(f"z{k - 2}")
                    e.wait_ge(a_free[b2_], before + 1)
                e.activation(zt[:, k % 2], pa[bank][:, :], ACT.Tanh, scale=0.5).then_inc(zt_ready, 1)

            def softplus(st):
                v = st.u + 1
                e.wait_ge(sp_in, v + 1)
                e.activation(e1, nab, ACT.Exp).then_inc(c_act, 1)
                e.wait_ge(c_act, v + 1)
                e.activation(l1, e1, ACT.Ln, bias=1.0).then_inc(sp_ln, 1)

            def chunk_a(c):
                n, kq = c.n, c.kq
                e.wait_ge(pt_full, c.use("a") + 1)
                at_least(e, xd_ready, n - 1)
                e.activation(xs[:, kq].rearrange("p h d -> p (h d)"), pt[:, :], ACT.Copy).then_inc(pt_free, 1)
                e.wait_ge(pm_full, c.use("a") + 1)
                e.activation(ex[:, kq].rearrange("p s h -> p (s h)"), CS, ACT.Exp)
                e.activation(bs[:, kq], BTR, ACT.Copy).then_inc(pm_read, 1)
                at_least(e, m_done, n - 1)
                for h in range(2):
                    e.wait_ge(seg_full, 2 * n + h + 1)
                    e.activation(decay[:, kq, 4 * h:4 * h + 4].rearrange("p h t -> p (h t)"), pe_[h][:, :],
                                 ACT.Exp).then_inc(e_free, 1)

            def chunk_c(c):
                q, n, kq = c.q, c.n, c.kq
                e.wait_ge(g_ready, n + 1)
                at_least(e, ss_ready, n)
                e.activation(junk, g[:, kq].rearrange("p h d -> p (h d)"), ACT.Square,
                             accum_out=ss[:, q, c.k:c.k + 1]).then_inc(ss_ready, 1)
                e.wait_ge(pt_full, c.use("o") + 1)
                e.activation(gT[:, kq].rearrange("p c t -> p (c t)"), pt[:, :], ACT.Copy).then_inc(pt_free, 1)

            def chunk_d(c):
                if c.k == 0:
                    e.wait_ge(stored[c.q], 16 * c.st.h + 16)
                e.wait_ge(pm_full, c.use("o") + 1)
                e.activation(ob[:, c.q, c.k, :], OUT, ACT.Copy).then_inc(pm_free, 1)

            def x1_out(st, d):
                bank, _ = wait_fill(st, f"t{d}")
                e.activation(x1T[:, d, :], pa[bank][:, :], ACT.Copy).then_inc(a_free[bank], 1)

            def gap_exp(st):
                e.wait_ge(gap_ready, st.u - NB)
                e.activation(p2, gap, ACT.Exp).then_inc(p2_ready, 1)

            def high_parts(n):
                if n == 0:
                    e.wait_ge(w_raw_in, 16)
                for a, b, scale in quarter(n):
                    ins = e.activation(w_split[:, 0, 0, a:b], w_raw[:, a:b], ACT.Copy, scale=scale)
                ins.then_inc(high0, 1)

            def body(st):
                s1, s3 = not st.last, st.s3
                c = [Chunk(st, k) for k in range(NK + 1)]
                if s1:
                    softplus(st)
                    conv_first(st, "c4")
                    conv_first(st, "c0")
                    conv_tanh(st, "c4")
                chunk_a(c[1])
                chunk_c(c[0])
                if s1:
                    conv_tanh(st, "c0")
                    conv_first(st, "c1")
                spread(st, 2)
                chunk_d(c[0])
                if s1:
                    conv_first(st, "c2")
                    conv_tanh(st, "c1")
                chunk_a(c[2])
                chunk_c(c[1])
                if s1:
                    conv_tanh(st, "c2")
                    conv_first(st, "c3")
                spread(st, 3)
                chunk_d(c[1])
                if s3:
                    x1_out(st, 0)
                    x1_out(st, 1)
                if s1:
                    z_tanh(st, 0)
                    conv_tanh(st, "c3")
                chunk_a(c[3])
                chunk_c(c[2])
                if s1:
                    z_tanh(st, 1)
                    spread(st, 4)
                chunk_d(c[2])
                if s1:
                    z_tanh(st, 2)
                if s3:
                    gap_exp(st)
                if s1:
                    chunk_a(c[4])
                else:
                    high_parts(0)
                chunk_c(c[3])
                if s1:
                    ln_out(st, "ln0")
                    ln_out(st, "ln1")
                chunk_d(c[3])
                if s1:
                    spread(st, 5)
                    z_tanh(st, 3)
                else:
                    for n in range(1, 4):
                        high_parts(n)

            def prologue(st):
                ln_out(st, "ln0")
                ln_out(st, "ln1")
                softplus(st)
                spread(st, NK)
                spread(st, NK + 1)
                for c in CONV_ORDER:
                    conv_first(st, c)
                    conv_tanh(st, c)
                for k in range(NK - 1):
                    z_tanh(st, k)
                ln_out(st, "ln0n")
                ln_out(st, "ln1n")
                z_tanh(st, NK - 1)
                chunk_a(Chunk(st, NK))

            def epilogue(st):
                x1_out(st, 0)
                x1_out(st, 1)
                gap_exp(st)

            e.wait_ge(params, 16 * N_PARAMS)
            e.activation(aneg, aneg, ACT.Exp).then_inc(c_prep, 1)
            e.wait_ge(prepared, 1)
            schedule(e, body, prologue, epilogue)

            def rows_out(i, r):
                ex_ = e.value_load(plan_i[0:1, bass.ds(WB * i + (r + NJT), 1)], min_val=0, max_val=NE - 1)
                e.wait_ge(w_have, ex_ + 1)
                e.wait_ge(f_t_full, WB * i + (r + 1))
                e.activation(xh[:, r % WB].rearrange("p d t -> p (d t)"), pt[:, 0:KD * P], ACT.Copy).then_inc(xh_ready, 1)

            def tile(i, r):
                j = WB * i + r
                ex_ = e.value_load(plan_i[0:1, bass.ds(WB * i + (r + NJT), 1)], min_val=0, max_val=NE - 1)
                for half in range(2):
                    e.wait_ge(f_full[2 * half], j + 1)
                    at_least(e, act_done, 2 * j - 1 + half)
                    e.sem_inc(hop, 1)
                    for f in range(4):
                        ff = NF + 4 * half + f
                        ins = e.activation(sg[:, half, f, :], GATE[half][:, f * P:(f + 1) * P], ACT.Silu,
                                           bias=b1a[:, bass.ds(ex_, 1), ff], scale=1.0 / S1)
                    ins.then_inc(silu_done[half], 1)
                rows_out(i, r + 1)

            e.wait_ge(plan_done, 1)
            e.wait_ge(bias_in, 32)
            rows_out(0, 0)
            for r in range(WB):
                tile(0, r)
            with e.Fori(1, NJ // WB) as i:
                for r in range(WB):
                    tile(i, r)

            with e.Fori(0, NB // 2) as i:
                for q in range(2):
                    e.wait_ge(f_var, 2 * i + (q + 1))
                    e.activation(fsd[:, q], fve[:, q], ACT.Sqrt).then_inc(f_rs, 1)

        @block.vector
        def _(dve):
            def ln_stats(w, hw, wq):
                ch = Chain(dve, c_dve1, 2, w)
                dve.wait_ge(hln_in[wq], 16 * (hw + 1))
                for k in range(NK):
                    ins = dve.bn_stats(st6[:, k, :], hln[:, wq, k, :])
                ch.link(ins)
                dve.sem_inc(hop, 1)
                for k in range(NK):
                    ins = dve.bn_aggr(mv[:, k, :], st6[:, k, :])
                ch.link(ins)
                ch.close()
                dve.tensor_scalar(ve, mv[:, :, 1], EPS, None, ALU.add).then_inc(ln_var, 1)

            def ln_apply(w, wq):
                dve.wait_ge(ln_rs, w + 1)
                for k in range(NK):
                    ins = dve.tensor_scalar(hln[:, wq, k, :], hln[:, wq, k, :], mv[:, k, 0:1], rs[:, k:k + 1],
                                            ALU.subtract, ALU.mult)
                ins.then_inc(ln_done, 1)

            def wait_fill(st, name):
                bank, before = st.fill(name)
                dve.wait_ge(a_full[bank], before + 1)
                return bank, before

            def dt_first(st):
                l, v = st.next_layer, st.u + 1
                bank, _ = wait_fill(st, "dt")
                src = pa[bank][:, 0:NK * NH].rearrange("p (k h) -> p k h", k=NK)
                ins = dve.tensor_tensor(dtr, src, dtb[:, l].unsqueeze(1).to_broadcast([P, NK, NH]), ALU.add)
                ins.then_inc(a_free[bank], 1)
                dve.wait_ge(a_free[bank], st.fill("dt")[1] + 1)
                dve.scalar_tensor_tensor(nab, dtr, -1.0, dtr, ALU.mult, ALU.min).then_inc(sp_in, 1)

            def dt_last(st, ch):
                l, v, vq = st.next_layer, st.u + 1, 1 - st.q
                dve.wait_ge(sp_ln, v + 1)
                ch.link(dve.scalar_tensor_tensor(dt_s[:, vq], dtr, 0.0, l1, ALU.max, ALU.add))
                dve.tensor_tensor(a_s[:, vq], dt_s[:, vq], aneg[:, l].unsqueeze(1).to_broadcast([P, NK, NH]),
                                  ALU.mult).then_inc(a_ready, 1)

            def taps(st, c, ch):
                idx, ct, l = CONV_ORDER.index(c), int(c[1]), st.next_layer
                m, mq = 5 * (st.u + 1) + idx, (1 - st.q + idx) % 2
                bank, _ = st.fill(c)
                dve.wait_ge(acc_init, m + 1)
                for s in range(1, TAPS):
                    ins = dve.scalar_tensor_tensor(acc[:, mq, s:T], pa[bank][:, 0:T - s],
                                                   cw[:, l, ct, TAPS - 1 - s:TAPS - s], acc[:, mq, s:T],
                                                   ALU.mult, ALU.add)
                    if s < TAPS - 1:
                        ch.link(ins)
                ins.then_inc(a_free[bank], 1)

            def silu_x(st, c):
                idx, ct, vq = CONV_ORDER.index(c), int(c[1]), 1 - st.q
                m, mq = 5 * (st.u + 1) + idx, (1 - st.q + idx) % 2
                dve.wait_ge(tanh_ready, m + 1)
                if ct < NCT:
                    ins = dve.scalar_tensor_tensor(xcT[:, vq, ct, :], th[:, mq], 1.0, acc[:, mq], ALU.add, ALU.mult)
                else:
                    dve.scalar_tensor_tensor(bT[0:DS, vq], th[0:DS, mq], 1.0, acc[0:DS, mq], ALU.add, ALU.mult)
                    ins = dve.scalar_tensor_tensor(cT[0:DS, vq], th[DS:P, mq], 1.0, acc[DS:P, mq], ALU.add, ALU.mult)
                ins.then_inc(xc_done, 1)

            def z_gate(st, k):
                vq = 1 - st.q
                bank, _ = st.fill(f"z{k}")
                dve.wait_ge(zt_ready, 4 * (st.u + 1) + k + 1)
                dve.scalar_tensor_tensor(zs[:, vq, k, :], zt[:, k % 2], 1.0, pa[bank][:, :], ALU.add,
                                         ALU.mult).then_inc(a_free[bank], 1)

            def end_a(st):
                dve.wait_ge(ss_ready, 4 * st.u)
                dve.tensor_scalar(sve, ss[:, 1 - st.q], 1.0 / (4 * DI), EPS, ALU.mult, ALU.add).then_inc(sve_ready, 1)

            def end_b(st):
                wq = 1 - st.q
                dve.wait_ge(srs_ready, st.u)
                dve.wait_ge(pm_free, 8 * st.u + (0 if st.epilogue else 1))
                dve.wait_ge(hres_in[wq], 16 * ((st.h + 1) if wq == 0 else st.h))
                for k in range(NK):
                    ins = dve.scalar_tensor_tensor(ob[:, wq, k, :], ob[:, wq, k, :], srs[:, k:k + 1],
                                                   hres[:, wq, k, :], ALU.mult, ALU.add)
                ins.then_inc(h_ready, 1)

            def chunk_a(c):
                n, kq = c.n, c.kq
                dve.wait_ge(pm_read, n + 1)
                if c.k == 0:
                    dve.wait_ge(a_ready, c.u + 1)
                dve.tensor_tensor(wdt[:, kq], ex[:, kq, 1], dt_s[:, c.q, c.k], ALU.mult).then_inc(wdt_ready, 1)
                dve.tensor_tensor(cbm[:, kq], CBT, tri_le[:, :], ALU.mult).then_inc(pm_free, 1)

            def chunk_mix(c):
                n, kq = c.n, c.kq
                dve.wait_ge(pm_free, c.use("a") + 1)
                dve.wait_ge(e_free, 2 * n + 2)
                at_least(dve, y_full, n - 1)
                dve.tensor_tensor(mix[:, kq], decay[:, kq], cbm[:, kq].unsqueeze(1).to_broadcast([P, NH, P]),
                                  ALU.mult).then_inc(m_done, 1)

            def chunk_b1(c):
                if c.k > 0:
                    dve.wait_ge(z_full, c.u6 + 2 * c.k)
                    dve.tensor_tensor(y1[:, c.kq], pz.rearrange("p (h d) -> p h d", h=NH), over_p(ex[:, c.kq, 0]),
                                      ALU.mult).then_inc(z_free, 1)

            def chunk_b2(c):
                n, k, kq = c.n, c.k, c.kq
                dve.wait_ge(y_full, n + 1)
                at_least(dve, g_ready, n - 1)
                if k > 0:
                    dve.wait_ge(ysum_ready, 3 * c.u + k)
                    other = y1
                else:
                    dve.wait_ge(xd_ready, n + 1)
                    other = xd
                dve.tensor_tensor(y2[:, kq], py.rearrange("p (h d) -> p h d", h=NH), other[:, kq],
                                  ALU.add).then_inc(y_free, 1)
                if k < NK - 1:
                    dve.wait_ge(z_full, c.u6 + 2 * k + 1)
                    new = pz[0:DS].rearrange("p (h d) -> p h d", h=NH)
                    if k == 0:
                        dve.tensor_copy(state[0:DS, 0], new).then_inc(z_free, 1)
                    else:
                        dve.wait_ge(sd_ready, 2 * c.u + k)
                        dve.tensor_tensor(state[0:DS, kq], new, state_d[0:DS], ALU.add).then_inc(z_free, 1)

            def s3_stats(st):
                ch = Chain(dve, c_dve3, 12, st.u - (NB + 1))
                wq = 1 - st.q
                dve.wait_ge(h_ready, st.u)
                for k in range(NK):
                    ins = dve.bn_stats(rst6[:, k, :], ob[:, wq, k, :])
                ch.link(ins)
                dve.sem_inc(hop, 1)
                for k in range(NK):
                    ins = dve.bn_aggr(rmv[:, k, :], rst6[:, k, :])
                ch.link(ins)
                dve.tensor_scalar(rve, rmv[:, :, 1], EPS, None, ALU.add).then_inc(r_var, 1)
                return ch

            def s3_apply(st):
                wq = 1 - st.q
                dve.wait_ge(r_rs, st.u - NB)
                before = st.h - 1 if wq == 1 else st.h
                dve.wait_ge(stored[wq], 16 * before + 16)
                dve.wait_ge(scattered[wq], 128 * (before - 4) + 16)
                for k in range(NK):
                    ins = dve.tensor_scalar(x1b[:, wq, k, :], ob[:, wq, k, :], rmv[:, k, 0:1], rrs[:, k:k + 1],
                                            ALU.subtract, ALU.mult)
                ins.then_inc(x1_ready, 1)

            def s3_top(st, ch):
                bank, before = wait_fill(st, "lg")
                src = pa[bank][:, 0:NK * NE].rearrange("p (k e) -> p k e", k=NK)
                dve.tensor_tensor(logit, src, gb.unsqueeze(1).to_broadcast([P, NK, NE]), ALU.add).then_inc(a_free[bank], 1)
                dve.wait_ge(a_free[bank], before + 1)
                dve.sem_inc(hop, 1)
                for k in range(NK):
                    ins = dve.max(top8[:, k, :], logit[:, k, :])
                ch.link(ins)
                dve.sem_inc(hop, 1)
                for k in range(NK):
                    ins = dve.max_index(top_i[:, k, :], top8[:, k, :], logit[:, k, :])
                ch.link(ins)
                dve.tensor_tensor(gap, top8[:, :, 1], top8[:, :, 0], ALU.subtract).then_inc(gap_ready, 1)
                ch.link(dve.tensor_copy(top_f, top_i))
                iota = iota_e[:, :].unsqueeze(1).to_broadcast([P, NK, NE])
                dve.tensor_tensor(oh1, iota, top_f[:, :, 0].unsqueeze(2).to_broadcast([P, NK, NE]), ALU.is_equal)
                ch.link(dve.tensor_tensor(oh2, iota, top_f[:, :, 1].unsqueeze(2).to_broadcast([P, NK, NE]), ALU.is_equal))
                dve.tensor_tensor(oh, oh1, oh2, ALU.add).then_inc(oh_ready, 1)

            def s3_place(st, ch):
                bank, before = wait_fill(st, "rk")
                wq = 1 - st.q
                rank = pa[bank][:, 0:NK * NE].rearrange("p (k e) -> p k e", k=NK)
                total = pa[bank][:, NK * NE:2 * NK * NE].rearrange("p (k e) -> p k e", k=NK)
                dve.wait_ge(p2_ready, st.u - NB)
                dve.tensor_scalar(gap, p2, 1.0, None, ALU.add)
                prev = count
                for k in range(NK):
                    ins = dve.tensor_tensor(base[:, k, :], prev[:, :] if k == 0 else base[:, k - 1, :], total[:, k, :], ALU.add)
                    ch.link(ins)
                dve.tensor_tensor(pos[:, 0, :], rank[:, 0, :], count[:, :], ALU.add)
                dve.tensor_tensor(pos[:, 1:NK, :], rank[:, 1:NK, :], base[:, 0:NK - 1, :], ALU.add).then_inc(a_free[bank], 1)
                dve.wait_ge(a_free[bank], before + 1)
                dve.tensor_copy(count[:, :], base[:, NK - 1, :])
                dve.tensor_tensor(pick[:, 0], pos, oh1, ALU.mult)
                dve.reciprocal(pw[:, :, 0], gap)
                ch.link(dve.tensor_tensor(pick[:, 1], pos, oh2, ALU.mult))
                dve.tensor_tensor(pw[:, :, 1], p2, pw[:, :, 0], ALU.mult)
                dve.tensor_reduce(pw[:, :, 2], pick[:, 0], AX.X, ALU.add)
                ch.link(dve.tensor_reduce(pw[:, :, 3], pick[:, 1], AX.X, ALU.add))
                for s in range(2):
                    ins = dve.tensor_copy(slot[:, wq, s * NK:(s + 1) * NK], pw[:, :, 2 + s])
                ins.then_inc(slot_ready, 1)
                dve.tensor_copy(route[:, bass.ds(NK * (st.u - (NB + 1)), NK), :], pw)
                ch.close()

            def body(st):
                s1, s3 = not st.last, st.s3
                c = [Chunk(st, k) for k in range(NK + 1)]
                if not st.first:
                    end_a(st)
                if s1:
                    ch1 = Chain(dve, c_dve2, S1_LINKS, st.u + 1)
                    dt_first(st)
                if not st.first:
                    end_b(st)
                if s1:
                    dt_last(st, ch1)
                    taps(st, "c4", ch1)
                chunk_b2(c[0])
                if s1:
                    taps(st, "c0", ch1)
                chunk_a(c[1])
                if s1:
                    silu_x(st, "c4")
                chunk_mix(c[1])
                if s3:
                    ch3 = s3_stats(st)
                if s1:
                    silu_x(st, "c0")
                    taps(st, "c1", ch1)
                chunk_b1(c[1])
                if s1:
                    taps(st, "c2", ch1)
                chunk_b2(c[1])
                if s1:
                    silu_x(st, "c1")
                chunk_a(c[2])
                if s3:
                    s3_apply(st)
                if s1:
                    silu_x(st, "c2")
                chunk_mix(c[2])
                if s1:
                    taps(st, "c3", ch1)
                    ch1.close()
                chunk_b1(c[2])
                if s1:
                    ln_stats(st.u + 2, st.h + 1, st.q)
                chunk_b2(c[2])
                if s1:
                    z_gate(st, 0)
                chunk_a(c[3])
                if s1:
                    silu_x(st, "c3")
                if s3:
                    s3_top(st, ch3)
                chunk_mix(c[3])
                if s1:
                    z_gate(st, 1)
                chunk_b1(c[3])
                if s1:
                    ln_apply(st.u + 2, st.q)
                chunk_b2(c[3])
                if s1:
                    z_gate(st, 2)
                    chunk_a(c[4])
                if s3:
                    s3_place(st, ch3)
                if s1:
                    chunk_mix(c[4])
                    z_gate(st, 3)

            def low_parts(n):
                dve.wait_ge(high0, n + 1)
                for a, b, scale in quarter(n):
                    ins = dve.scalar_tensor_tensor(w_split[:, 0, 1, a:b], w_raw[:, a:b], scale, w_split[:, 0, 0, a:b],
                                                   ALU.mult, ALU.subtract)
                if n == 3:
                    ins.then_inc(w_have, 1)

            def prologue(st):
                ch1 = Chain(dve, c_dve2, S1_LINKS, 0)
                dt_first(st)
                dt_last(st, ch1)
                for c in CONV_ORDER:
                    taps(st, c, ch1)
                    silu_x(st, c)
                ch1.close()
                ln_stats(1, 0, 1)
                ln_apply(1, 1)
                for k in range(NK - 1):
                    z_gate(st, k)
                z_gate(st, NK - 1)
                chunk_a(Chunk(st, NK))
                chunk_mix(Chunk(st, NK))

            def epilogue(st):
                end_a(st)
                end_b(st)
                ch3 = s3_stats(st)
                low_parts(0)
                s3_apply(st)
                low_parts(1)
                low_parts(2)
                s3_top(st, ch3)
                low_parts(3)
                s3_place(st, ch3)

            S1_LINKS = 1 + NC * (TAPS - 2)
            dve.wait_ge(consts, N_CONSTS)
            ln_stats(0, 0, 0)
            ln_apply(0, 0)
            dve.wait_ge(params, 16 * N_PARAMS)
            dve.tensor_scalar(cw, cw, 0.5, None, ALU.mult)
            dve.tensor_scalar(cb, cb, 0.5, None, ALU.mult)
            dve.tensor_scalar(rmsw, rmsw, 0.5, None, ALU.mult).then_inc(c_prep, 1)
            dve.wait_ge(c_prep, 2)
            dve.tensor_scalar(aneg, aneg, -1.0, None, ALU.mult)
            for l in range(2):
                for c in range(NCT):
                    ins = dve.tensor_scalar(wout[:, l, c, :], wout[:, l, c, :], rmsw[:, l, c:c + 1], None, ALU.mult)
            ins.then_inc(prepared, 1)
            dve.wait_ge(prepared, 1)
            schedule(dve, body, prologue, epilogue)

            at = [0]

            def step(ins):
                at[0] += 1
                ins.then_inc(c_plan, 1)
                dve.wait_ge(c_plan, at[0])

            def cells(ap, n=NJT):
                return ap.unsqueeze(2).to_broadcast([1, n, NE])

            jr, jd = jrow[0:1, :], jdum[0:1, :]
            row_f, e_f = plan_f[0:1, 0:NJT], plan_f[0:1, NJT:2 * NJT]
            par_f, len_f = plan_f[0:1, 2 * NJT:3 * NJT], plan_f[0:1, 3 * NJT:3 * NJT + NE]
            step(dve.tensor_scalar(j128, jrow[:, 0:NTILE], float(P), None, ALU.mult))
            step(dve.tensor_tensor(cnt, count[:, :], qbase[:, :], ALU.subtract))
            dve.tensor_copy(len_f, cnt[0:1, :])
            step(dve.tensor_tensor(tcmp, cnt.unsqueeze(2).to_broadcast([P, NE, NTILE]),
                                   j128.unsqueeze(1).to_broadcast([P, NE, NTILE]), ALU.is_gt))
            step(dve.tensor_reduce(nt, tcmp, AX.X, ALU.add))
            step(dve.tensor_copy(end[0:1, 0:1], nt[0:1, 0:1]))
            for e in range(1, NE):
                step(dve.tensor_tensor(end[0:1, e:e + 1], end[0:1, e - 1:e], nt[0:1, e:e + 1], ALU.add))
            step(dve.tensor_tensor(cmp_[0:1], cells(jr), end[0:1].unsqueeze(1).to_broadcast([1, NJT, NE]), ALU.is_ge))
            dve.tensor_reduce(e_f, cmp_[0:1, :, 0:NE - 1], AX.X, ALU.add)
            dve.tensor_scalar(usedj[0:1], cmp_[0:1, :, NE - 1], -1.0, 1.0, ALU.mult, ALU.add)
            step(dve.tensor_tensor(cmp_nt[0:1], cmp_[0:1], nt[0:1].unsqueeze(1).to_broadcast([1, NJT, NE]), ALU.mult))
            dve.tensor_reduce(stj[0:1], cmp_nt[0:1], AX.X, ALU.add)
            step(dve.tensor_tensor(cmp_[0:1], cmp_[0:1], sign[0:1, :].unsqueeze(1).to_broadcast([1, NJT, NE]), ALU.mult))
            step(dve.tensor_reduce(ej[0:1], cmp_[0:1, :, 0:NE - 1], AX.X, ALU.add))
            NG = NJT // WB
            par, packed = ej[0:1].rearrange("p (g r) -> p g r", r=WB), par_f[:, 0:NG]
            step(dve.tensor_copy(packed, par[:, :, 0]))
            for m in range(1, WB):
                step(dve.scalar_tensor_tensor(packed, par[:, :, m], float(1 << m), packed, ALU.mult, ALU.add))
            step(dve.scalar_tensor_tensor(packed[:, 1:NG], par[:, 0:NG - 1, WB - 1], float(1 << WB), packed[:, 1:NG],
                                          ALU.mult, ALU.add))
            step(dve.tensor_tensor(tmpj[0:1], jr, stj[0:1], ALU.subtract))
            step(dve.tensor_scalar(tmpj[0:1], tmpj[0:1], float(P), None, ALU.mult))
            step(dve.scalar_tensor_tensor(tmpj[0:1], e_f, float(QROWS), tmpj[0:1], ALU.mult, ALU.add))
            step(dve.tensor_tensor(tmpj[0:1], tmpj[0:1], jd, ALU.subtract))
            step(dve.tensor_tensor(tmpj[0:1], tmpj[0:1], usedj[0:1], ALU.mult))
            dve.tensor_copy(plan_f[0:1, 3 * NJT + NE:3 * NJT + 2 * NE], end[0:1, :])
            step(dve.tensor_tensor(row_f, tmpj[0:1], jd, ALU.add))
            dve.tensor_copy(plan_i[0:1, :], plan_f[0:1, :]).then_inc(plan_done, 1)
            step(dve.tensor_scalar(moved, nt[:, 0:NE - 1], float(P), -float(QROWS), ALU.mult, ALU.add))
            for s in range(2):
                step(dve.tensor_tensor(behind, route[:, :, 2 + s].unsqueeze(2).to_broadcast([P, NTILE, NE - 1]),
                                       qbase[:, 1:NE].unsqueeze(1).to_broadcast([P, NTILE, NE - 1]), ALU.is_ge))
                step(dve.tensor_tensor(behind, behind, moved.unsqueeze(1).to_broadcast([P, NTILE, NE - 1]), ALU.mult))
                step(dve.tensor_reduce(shift, behind, AX.X, ALU.add))
                step(dve.tensor_tensor(rows_u[:, :, s], route[:, :, 2 + s], shift, ALU.add))

            dve.wait_ge(bias_in, 32)
            dve.tensor_scalar(b1v, b1a[:, :, 0:NF], S1, None, ALU.mult).then_inc(c_glu, 1)
            dve.sem_inc(o_ready, 1)

            def rows_low(i, r):
                dve.wait_ge(xh_ready, WB * i + (r + 1))
                dve.tensor_tensor(xl[:, r % WB].rearrange("p d t -> p (d t)"), pt[:, 0:KD * P],
                                  xh[:, r % WB].rearrange("p d t -> p (d t)"), ALU.subtract).then_inc(x_done, 1)

            def gated(i, r):
                j = WB * i + r
                ex_ = dve.value_load(plan_i[0:1, bass.ds(WB * i + (r + NJT), 1)], min_val=0, max_val=NE - 1)
                for half in range(2):
                    dve.wait_ge(f_full[2 * half + 1], j + 1)
                    dve.wait_ge(silu_done[half], j + 1)
                    dve.sem_inc(hop, 1)
                    for f in range(4):
                        ff = 4 * half + f
                        ins = dve.scalar_tensor_tensor(glu[:, half, f * P:(f + 1) * P], VALUE[half][:, f * P:(f + 1) * P],
                                                       b1v[:, bass.ds(ex_, 1), ff], sg[:, half, f, :],
                                                       ALU.add, ALU.mult)
                    ins.then_inc(c_glu, 1)
                    dve.wait_ge(c_glu, 4 * j + 2 * half + 2)
                    high = acth[:, r, 4 * half:4 * half + 4].rearrange("p f t -> p (f t)")
                    dve.tensor_copy(high, glu[:, half]).then_inc(c_glu, 1)
                    dve.wait_ge(c_glu, 4 * j + 2 * half + 3)
                    dve.tensor_tensor(actl[:, r, 4 * half:4 * half + 4].rearrange("p f t -> p (f t)"), glu[:, half],
                                      high, ALU.subtract).then_inc(act_done, 1)

            def result(i, r, first):
                b = r % WB
                ex_ = dve.value_load(plan_i[0:1, bass.ds(WB * i + (r + NJT), 1)], min_val=0, max_val=NE - 1)
                dve.wait_ge(o_full, WB * i + (r + 1))
                if not first:
                    dve.wait_ge(ans_out[b], 16 * i)
                dve.sem_inc(hop, 1)
                dve.scalar_tensor_tensor(yt[:, b], py[:, 0:D], 1.0 / (S1 * S2),
                                         b2a[:, bass.ds(ex_, 1), :].rearrange("p o d -> p (o d)"),
                                         ALU.mult, ALU.add).then_inc(o_ready, 1)

            rows_low(0, 0)
            for r in range(WB):
                gated(0, r)
                rows_low(0, r + 1)
                if r > 0:
                    result(0, r - 1, True)
            gated(1, 0)
            rows_low(1, 1)
            result(0, WB - 1, True)
            for r in range(1, WB):
                gated(1, r)
                rows_low(1, r + 1)
                result(1, r - 1, False)
            with dve.Fori(2, NJ // WB) as i:
                for r in range(WB):
                    gated(i, r)
                    rows_low(i, r + 1)
                    result(i - 1 if r == 0 else i, (r - 1) % WB, False)
            result(NJ // WB - 1, WB - 1, False)

            def slots(i, q):
                for s in range(2):
                    ins = dve.tensor_copy(slot_c[:, q, s * LG:(s + 1) * LG],
                                          rows_u[:, bass.ds(LG * (2 * i + q), LG), s])
                ins.then_inc(idx_ready, 1)

            def finish(i, q, ahead):
                ch = Chain(dve, c_fin, 6, 2 * i + q)
                dve.wait_ge(got[q], 32 * LG * (i + 1))
                dve.wait_ge(x1_back[q], 16 * (i + 1))
                dve.sem_inc(hop, 1)
                if ahead:
                    slots(i + 1, q)
                ch.link(dve.tensor_copy(wv[:, q], route[:, bass.ds(LG * (2 * i + q), LG), :]))
                for k in range(LG):
                    ins = dve.scalar_tensor_tensor(fsum[:, q, k], got1[:, q, k], wv[:, q, k, 0:1], back[:, q, k],
                                                   ALU.mult, ALU.add)
                ch.link(ins)
                for k in range(LG):
                    ins = dve.scalar_tensor_tensor(fsum[:, q, k], got2[:, q, k], wv[:, q, k, 1:2], fsum[:, q, k],
                                                   ALU.mult, ALU.add)
                ins.then_inc(f_sum, 1)
                dve.wait_ge(f_sum, 2 * i + (q + 1))
                for k in range(LG):
                    ins = dve.bn_stats(fst[:, q, k], fsum[:, q, k])
                ch.link(ins)
                dve.sem_inc(hop, 1)
                for k in range(LG):
                    ins = dve.bn_aggr(fmv[:, q, k], fst[:, q, k])
                ch.link(ins)
                dve.tensor_scalar(fve[:, q], fmv[:, q, :, 1], EPS, None, ALU.add).then_inc(f_var, 1)
                dve.wait_ge(f_rs, 2 * i + (q + 1))
                ch.link(dve.reciprocal(frs[:, q], fsd[:, q]))
                if not (isinstance(i, int) and i == 0):
                    dve.wait_ge(out_done[q], 16 * i)
                for k in range(LG):
                    ins = dve.tensor_scalar(fin[:, q, k], fsum[:, q, k], fmv[:, q, k, 0:1], frs[:, q, k:k + 1],
                                            ALU.subtract, ALU.mult)
                ch.link(ins)
                ch.close()
                dve.sem_inc(f_out, 1)

            for q in range(2):
                slots(0, q)
            for q in range(2):
                finish(0, q, True)
            with dve.Fori(1, NB // 2 - 1) as i:
                for q in range(2):
                    finish(i, q, True)
            for q in range(2):
                finish(NB // 2 - 1, q, False)

        @block.gpsimd
        def _(pool):
            own = [0]

            def next_(ins):
                own[0] += 1
                ins.then_inc(c_pool, 1)
                pool.wait_ge(c_pool, own[0])

            next_(pool.memset(zeros[:, :], 0.0))
            for s in range(2):
                row = DUMMY + s * P
                pool.dma_start(queue[row:row + P, :], zeros[:, :]).then_inc(scattered[s], 16)
            next_(pool.memset(ones[:, :], 1.0))
            pool.memset(half_neg[:, :], -0.5)
            pool.iota(sign_i[:, :], [[0, NE // 2], [-2, 2]], base=1, channel_multiplier=0)
            pool.iota(jrow_i[:, :], [[1, NJT]], base=0, channel_multiplier=0)
            next_(pool.iota(jdum_i[:, :], [[0, NJT // WB], [P, WB]], base=DUMMY, channel_multiplier=0))
            pool.tensor_copy(sign[:, :], sign_i[:, :])
            pool.tensor_copy(jrow[:, :], jrow_i[:, :])
            next_(pool.tensor_copy(jdum[:, :], jdum_i[:, :]))
            pool.tensor_copy(iota_e[:, :], jrow[:, 0:NE])
            pool.tensor_scalar(qbase[:, :], jrow[:, 0:NE], float(QROWS), 0.0, ALU.mult, ALU.add)
            pool.tensor_scalar(count[:, :], jrow[:, 0:NE], float(QROWS), 0.0, ALU.mult, ALU.add)
            pool.affine_select(out=tri_le[:, :], in_=ones[:, :], compare_op=ALU.is_ge, fill=0.0, base=0,
                               pattern=[[1, P]], channel_multiplier=-1)
            pool.affine_select(out=tri_lt[:, :], in_=ones[:, :], compare_op=ALU.is_gt, fill=0.0, base=0,
                               pattern=[[1, P]], channel_multiplier=-1)
            pool.affine_select(out=tri_gt[:, :], in_=ones[:, :], compare_op=ALU.is_gt, fill=0.0, base=0,
                               pattern=[[-1, P]], channel_multiplier=1)
            next_(pool.affine_select(out=ident[:, :], in_=ones[:, :], compare_op=ALU.is_equal, fill=0.0, base=0,
                                     pattern=[[-1, P]], channel_multiplier=1))
            pool.sem_inc(consts, 1)

            def by_head(ap):
                return ap.unsqueeze(2).to_broadcast([ap.shape[0], NH, HD])

            def load_weights(e):
                pool.dma_start(w_raw, w_exp[e]).then_inc(w_raw_in, 16)

            def split(e):
                p = e % 2
                for n in range(4):
                    for a, b, scale in quarter(n):
                        raw, high, low = w_raw[:, a:b], w_split[:, p, 0, a:b], w_split[:, p, 1, a:b]
                        pool.tensor_scalar(high, raw, scale, 0.0, ALU.mult, ALU.add)
                        next_(pool.tensor_scalar(raw, raw, scale, 0.0, ALU.mult, ALU.add))
                        ins = pool.tensor_tensor(low, raw, high, ALU.subtract)
                next_(ins)
                pool.sem_inc(w_have, 1)

            def rsqrt_ln(w):
                pool.wait_ge(ln_var, w + 1)
                pool.tensor_tensor(rs, ve, half_neg[:, :], ALU.pow).then_inc(ln_rs, 1)

            def end(st):
                pool.wait_ge(sve_ready, st.u)
                pool.tensor_tensor(srs, sve, half_neg[:, :], ALU.pow).then_inc(srs_ready, 1)

            def add_x(st):
                wq = 1 - st.q
                pool.wait_ge(h_ready, st.u)
                pool.tensor_tensor(hres[:, wq], ob[:, wq], hres[:, wq], ALU.add).then_inc(hx_ready, 1)

            def rsqrt_x1(st):
                pool.wait_ge(r_var, st.u - NB)
                pool.tensor_tensor(rrs, rve, half_neg[:, :], ALU.pow).then_inc(r_rs, 1)

            def scatter(st, first, end_):
                wq = 1 - st.q
                if first == 0:
                    pool.wait_ge(slot_ready, st.u - NB)
                    pool.sem_inc(hop, 1)
                for m in range(first, end_):
                    pool.indirect_dma_start(queue, bass.IndirectOffsetOnAxis(ap=slot[:, wq, m:m + 1], axis=0),
                                            x1b[:, wq, m % NK, :], None).then_inc(scattered[wq], 16)

            def operands(c):
                q, n, k, kq, u6 = c.q, c.n, c.k, c.kq, c.u6
                pool.wait_ge(pt_free, c.use("a") + 1)
                at_least(pool, y_full, n - 1)
                pool.tensor_tensor(dtx[:, kq], xs[:, kq], by_head(dt_s[:, q, k]), ALU.mult).then_inc(dtx_ready, 1)
                if k < NK - 1:
                    pool.wait_ge(wdt_ready, n + 1)
                    at_least(pool, z_full, (u6 + 1) if k == 2 else (u6 - 1 - 2 * k))
                    pool.tensor_tensor(xw[:, kq], xs[:, kq], by_head(wdt[:, kq]), ALU.mult).then_inc(xw_ready, 1)
                at_least(pool, y_free, n - 1)
                pool.tensor_tensor(xd[:, kq], xs[:, kq], by_head(dsk[:, c.layer]), ALU.mult).then_inc(xd_ready, 1)
                if k in (1, 2):
                    pool.wait_ge(z_free, u6 + 2 * k - 1)
                    pool.tensor_tensor(state_d[0:DS], state[0:DS, (k - 1) % 2], by_head(ex[0:DS, kq, 2]),
                                       ALU.mult).then_inc(sd_ready, 1)

            def gated(c):
                n, k, kq = c.n, c.k, c.kq
                if k > 0:
                    pool.wait_ge(z_free, c.u6 + 2 * k)
                    pool.wait_ge(xd_ready, n + 1)
                    pool.tensor_tensor(y1[:, kq], y1[:, kq], xd[:, kq], ALU.add).then_inc(ysum_ready, 1)
                pool.wait_ge(y_free, n + 1)
                before = {0: -1, 1: 1, 2: 3, 3: 5}[k]
                if isinstance(c.u, int) and c.u == 0 and k < 2:
                    before = 0
                at_least(pool, pt_free, 8 * c.u + before if before or k >= 2 else 0)
                pool.tensor_tensor(g[:, kq], y2[:, kq], zs[:, c.q, k].rearrange("p (h d) -> p h d", h=NH),
                                   ALU.mult).then_inc(g_ready, 1)

            def body(st):
                c = [Chunk(st, k) for k in range(NK + 1)]
                if not st.first:
                    end(st)
                if st.last:
                    for s in range(2):
                        pool.wait_ge(a_free[s], LAST_HB)
                    load_weights(0)
                gated(c[0])
                operands(c[1])
                if st.s3:
                    rsqrt_x1(st)
                if not st.first and not st.s3:
                    add_x(st)
                gated(c[1])
                operands(c[2])
                if not st.last:
                    rsqrt_ln(st.u + 2)
                gated(c[2])
                operands(c[3])
                gated(c[3])
                if not st.last:
                    operands(c[4])
                if st.s3:
                    scatter(st, 0, 2 * NK)

            def prologue(st):
                rsqrt_ln(1)
                operands(Chunk(st, NK))

            def epilogue(st):
                end(st)
                rsqrt_x1(st)
                scatter(st, 0, 2 * NK)

            rsqrt_ln(0)
            schedule(pool, body, prologue, epilogue)

            for e in range(1, NE):
                if e == 1:
                    pool.wait_ge(plan_done, 1)
                    for s in range(2):
                        pool.wait_ge(scattered[s], 16 * 2 * NK * (NB // 2) + 16)
                        pool.wait_ge(stored[s], 16 * NB + 16)
                load_weights(e)
                if e >= 2:
                    end_e = pool.value_load(plan_i[0:1, 3 * NJT + NE + e - 2:3 * NJT + NE + e - 1], min_val=0, max_val=NJ)
                    pool.wait_ge(o_ready, end_e + 1)
                    pool.sem_inc(hop, 1)
                pool.wait_ge(w_raw_in, 16 * (e + 1))
                split(e)

            for s in range(WB):
                pool.wait_ge(ans_out[s], 16 * (NJ // WB))

            def gather(i, q, first):
                pool.wait_ge(idx_ready, 2 * i + (q + 1))
                if not first:
                    pool.wait_ge(f_sum, 2 * i + (q - 1))
                pool.sem_inc(hop, 1)
                for s, dst in enumerate((got1, got2)):
                    for k in range(LG):
                        m = s * LG + k
                        pool.indirect_dma_start(dst[:, q, k, :], None, answer,
                                                bass.IndirectOffsetOnAxis(ap=slot_c[:, q, m:m + 1], axis=0)
                                                ).then_inc(got[q], 16)

            for q in range(2):
                gather(0, q, True)
            with pool.Fori(1, NB // 2) as i:
                for q in range(2):
                    gather(i, q, False)


def kernel(**inputs):
    import numpy as _np
    import concourse.bacc as _bacc
    from concourse import mybir as _mybir
    from concourse.bass_utils import run_bass_kernel_spmd as _run

    def get(name):
        return _np.asarray(inputs["L0_" + name])

    def columns(a, tiles):
        a = a.reshape((a.shape[0], tiles, P) + a.shape[2:])
        return _np.moveaxis(a, 2, 0)

    def by_partition(a, tiles):
        return a.reshape(NE, tiles, P, -1).transpose(0, 2, 1, 3).reshape(NE, P, -1)

    laid = {
        "x": get("attn_x"),
        "w_in": get("attn_in_proj_w").transpose(0, 2, 1),
        "conv_w": columns(get("attn_conv_w"), NC),
        "conv_b": columns(get("attn_conv_b"), NC),
        "ln_w": columns(get("attn_ln_w"), KD),
        "ln_b": columns(get("attn_ln_b"), KD),
        "dt_bias": get("attn_dt_bias"),
        "a_log": get("attn_A_log"),
        "d_skip": get("attn_D"),
        "rms_w": columns(get("attn_rms_w"), NCT),
        "w_out": get("attn_out_proj_w").transpose(0, 2, 1),
        "gate_w": get("ffn_gate_w"),
        "gate_b": get("ffn_gate_b"),
        "w_exp": _np.concatenate([by_partition(get("ffn_w1"), KD), by_partition(get("ffn_w2"), NF)], axis=2),
        "b1": get("ffn_b1").reshape(NE, 2 * NF, P).transpose(2, 0, 1),
        "b2": get("ffn_b2"),
    }
    nc = _bacc.Bacc("TRN2", target_bir_lowering=False, num_devices=1)
    arrays, args = {}, []
    for name, a in laid.items():
        a = _np.ascontiguousarray(a)
        arrays[f"in_{name}"] = a
        args.append(nc.dram_tensor(f"in_{name}", a.shape, _mybir.dt.from_np(a.dtype), kind="ExternalInput").ap())
    args.append(nc.dram_tensor("out_0", (NTOK, D), F32, kind="ExternalOutput").ap())
    build(nc, *args)
    r = _run(nc, [arrays], core_ids=[0])
    return r.results[0]["out_0"].reshape(NB, T, D)
```

```python
from contextlib import ExitStack

import concourse.bass as bass
from concourse import mybir

F32 = mybir.dt.float32
F16 = mybir.dt.float16
I32 = mybir.dt.int32
U32 = mybir.dt.uint32
ALU = mybir.AluOpType
ACT = mybir.ActivationFunctionType
AX = mybir.AxisListType

P = 128
NB, T, D = 8, 512, 256
NK = T // P
KD = D // P
NH, HD, DS = 8, 64, 64
DI = NH * HD
NCT = DI // P
NC = NCT + 1
TAPS = 4
DPROJ = 2 * DI + 2 * DS + NH
OX, OBC, ODT = DI, 2 * DI, 2 * DI + 2 * DS
EPS = 1e-5
NE, FF = 8, 1024
NF = FF // P
NTOK = NB * T
NTILE = NTOK // P
W1N, W2N = KD * 2 * FF, NF * D
WEX = W1N + W2N
S1, S2 = 16.0, 32.0
SG = 1.0 / S1
PASSES = ((0, 0), (0, 1), (1, 0))
QROWS = NTOK + P
DUMMY = NE * QROWS
WB = 3
NJ = (2 * NTOK) // P + NE - 1
NJ += -NJ % WB
NJT = NJ + WB
LG = NK
CLEAR_STEPS = 10
CLEAR = (NJ - NTILE) // CLEAR_STEPS
assert CLEAR * CLEAR_STEPS == NJ - NTILE

PLAIN = ["dt", "c4", "c0", "c1", "c2", "c3", "z0", "z1", "z2", "ln0", "ln1", "z3"]
WITH3 = ["dt", "c4", "c0", "c1", "c2", "c3", "t0", "t1", "z0", "lg", "z1", "z2", "rk", "ln0", "ln1", "z3"]
FIRST = ["ln0", "ln1"] + PLAIN[:-3] + ["ln0n", "ln1n", "z3"]
ONLY3 = ["t0", "t1", "lg", "rk"]
LAST_HB = 109
USES = {"a0": -1, "a1": 1, "o0": 2, "a2": 3, "o1": 4, "a3": 5, "o2": 6, "o3": 8}
CONV_ORDER = ["c4", "c0", "c1", "c2", "c3"]
MAMBA_UNITS = 2 * NB
NCOUNT_Z = 2 * (NK - 1)


def at_least(eng, sem, count):
    if isinstance(count, int) and count <= 0:
        return
    eng.wait_ge(sem, count)


class Chain:

    def __init__(self, eng, sem, per, unit):
        self.eng, self.sem, self.base, self.per, self.n = eng, sem, per * unit, per, 0

    def link(self, ins):
        self.n += 1
        ins.then_inc(self.sem, 1)
        self.eng.wait_ge(self.sem, self.base + self.n)

    def close(self):
        assert self.n == self.per, (self.n, self.per)


def quarter(n):
    a, b = n * WEX // 4, (n + 1) * WEX // 4
    cuts = [a, W1N, b] if a < W1N < b else [a, b]
    return [(u, v, S1 if v <= W1N else S2) for u, v in zip(cuts, cuts[1:])]


class Step:

    def __init__(self, u, half, layer, parity, fills, half_base, first=False, last=False, s3=False):
        self.u, self.h, self.layer, self.q = u, half, layer, parity
        self.fills, self.hb = fills, half_base
        self.first, self.last, self.s3 = first, last, s3
        self.epilogue = isinstance(u, int) and u >= MAMBA_UNITS
        self.next_layer = 1 if (layer == 1 or (isinstance(u, int) and u == NB - 1)) else 0

    def fill(self, name):
        p = self.fills.index(name)
        return p % 2, self.hb + p // 2


class Chunk:

    def __init__(self, st, k):
        ahead = 1 if k == NK else 0
        self.k, self.u = k % NK, st.u + ahead
        self.q = (st.q + ahead) % 2
        self.kq, self.n = k % 2, NK * self.u + self.k
        self.layer = st.next_layer if ahead else st.layer
        self.u6, self.st = (NCOUNT_Z * self.u), st

    def use(self, kind):
        off = USES[f"{kind}{self.k}"]
        if isinstance(self.u, int):
            if self.u == 0 and off < 0:
                off = 0
            if self.u == MAMBA_UNITS - 1 and off == 8:
                off = 7
        return 8 * self.u + off


def schedule(eng, body, prologue, epilogue):
    prologue(Step(-1, -1, 0, 1, FIRST, 0))
    body(Step(0, 0, 0, 0, PLAIN, 7, first=True))
    with eng.Fori(0, 3) as i:
        for r in range(2):
            body(Step(2 * i + (1 + r), i + r, 0, (1 + r) % 2, PLAIN, 6 * (2 * i) + (13 + 6 * r)))
    body(Step(7, 3, 0, 1, PLAIN, 49))
    body(Step(8, 4, 1, 0, PLAIN, 55))
    body(Step(9, 4, 1, 1, WITH3, 61, s3=True))
    with eng.Fori(0, 2) as i:
        for r in range(2):
            body(Step(2 * i + (10 + r), i + 5, 1, r, WITH3, 16 * i + (69 + 8 * r), s3=True))
    body(Step(14, 7, 1, 0, WITH3, 101, s3=True))
    body(Step(15, 7, 1, 1, ONLY3, LAST_HB, last=True, s3=True))
    epilogue(Step(16, 8, 1, 0, ONLY3, LAST_HB + 2, s3=True))


def build(nc, x, w_in, conv_w, conv_b, ln_w, ln_b, dt_bias, a_log, d_skip, rms_w, w_out,
          gate_w, gate_b, w_exp, b1, b2, out):
    h1 = nc.dram_tensor("h1", [NB, T, D], F32, kind="Internal").ap()
    hx = nc.dram_tensor("hx", [NB, T, D], F32, kind="Internal").ap()
    x1_rows = nc.dram_tensor("x1_rows", [NTOK, D], F32, kind="Internal").ap()
    queue = nc.dram_tensor("queue", [DUMMY + 4 * P, D], F32, kind="Internal").ap()
    answer = nc.dram_tensor("answer", [NJ * P, D], F32, kind="Internal").ap()

    ctx = ExitStack()
    with ctx:
        def sb(name, shape, dt=F32):
            return ctx.enter_context(nc.sbuf_tensor(name, shape, dt))

        def sem(name):
            return ctx.enter_context(nc.semaphore(name))

        ident = sb("ident", [P, P])
        tri_le = sb("tri_le", [P, P])
        tri_gt = sb("tri_gt", [P, P])
        tri_lt = sb("tri_lt", [P, P])
        ones = sb("ones", [P, P])
        zeros = sb("zeros", [P, D])
        half_neg = sb("half_neg", [P, NK])
        iota_e = sb("iota_e", [P, NE])
        qbase = sb("qbase", [P, NE])
        route = sb("route", [P, NTILE, 4])
        count = sb("count", [P, NE])
        jrow = sb("jrow", [P, NJT])
        jdum = sb("jdum", [P, NJT])
        jrow_i = sb("jrow_i", [P, NJT], I32)
        jdum_i = sb("jdum_i", [P, NJT], I32)
        sign_i = sb("sign_i", [P, NE], I32)
        sign = sb("sign", [P, NE])
        ARENA = 50400
        arena = sb("arena", [P, ARENA])

        def carver():
            at = [0]

            def carve(*shape, dt=F32, peek=False):
                n = 1
                for s in shape:
                    n *= s
                if dt is F16:
                    n //= 2
                ap = arena[:, at[0]:at[0] + n]
                assert at[0] + n <= ARENA, at[0] + n
                if not peek:
                    at[0] += n
                if dt is not F32:
                    ap = ap.bitcast(dt)
                if len(shape) == 2:
                    ap = ap.rearrange("p (a b) -> p a b", a=shape[0])
                elif len(shape) == 3:
                    ap = ap.rearrange("p (a b c) -> p a b c", a=shape[0], b=shape[1])
                elif len(shape) == 4:
                    ap = ap.rearrange("p (a b c d) -> p a b c d", a=shape[0], b=shape[1], c=shape[2])
                return ap
            return carve

        carve = carver()
        win = carve(2, 2, KD, DPROJ, dt=F16)
        hln = carve(2, NK, D)
        uT = carve(2, 2, KD, T, dt=F16)
        uf = carve(KD, T)
        acc, th = carve(2, T), carve(2, T)
        zt = carve(2, DI)
        xcT = carve(2, NCT, T)
        wout = carve(2, 2, NCT, D, dt=F16)
        cw, cb = carve(2, NC, TAPS), carve(2, NC)
        lnw, lnb = carve(MAMBA_UNITS + 1, KD), carve(MAMBA_UNITS + 1, KD)
        rmsw = carve(2, NCT)
        dtb, aneg, dsk = carve(2, NH), carve(2, NH), carve(2, NH)
        gw, gb = carve(KD, NE), carve(NE)
        hres = carve(2, NK, D)
        bT, cT = carve(2, T), carve(2, T)
        zs = carve(2, NK, DI)
        tri_a = carve(2, NH, P)
        xs, dtx, xw, xd = carve(2, NH, HD), carve(2, NH, HD), carve(2, NH, HD), carve(2, NH, HD)
        decay, mix = carve(2, NH, P), carve(2, NH, P)
        cbm = carve(2, P)
        bs = carve(2, DS)
        ex = carve(2, 3, NH)
        wdt = carve(2, NH)
        wout_raw = [carve(NCT, D, peek=True)]
        y1, y2 = carve(2, NH, HD), carve(2, NH, HD)
        state, state_d = carve(2, NH, HD), carve(NH, HD)
        gT = carve(2, 2, NCT, P, dt=F16)
        junk = carve(DI)
        wout_raw.append(carve(NCT, D, peek=True))
        x1T = carve(KD, T)
        st6, mv, ve, rs = carve(NK, 6), carve(NK, 2), carve(NK), carve(NK)
        rst6, rmv, rve, rrs = carve(NK, 6), carve(NK, 2), carve(NK), carve(NK)
        ss, sve, srs = carve(2, NK), carve(NK), carve(NK)
        dtr, nab, e1, l1 = carve(NK, NH), carve(NK, NH), carve(NK, NH), carve(NK, NH)
        dt_s, a_s = carve(2, NK, NH), carve(2, NK, NH)
        logit, top8 = carve(NK, NE), carve(NK, 8)
        top_i, top_f = carve(NK, 8, dt=U32), carve(NK, 8)
        gap, p2 = carve(NK), carve(NK)
        oh1, oh2, oh = carve(NK, NE), carve(NK, NE), carve(NK, NE)
        pos, pick, base = carve(NK, NE), carve(2, NK, NE), carve(NK, NE)
        pw = carve(NK, 4)
        slot = carve(2, 2 * NK, dt=U32)
        win_raw = carve(2, KD, DPROJ, peek=True)
        g = carve(2, NH, HD)
        ob = carve(2, NK, D)
        x1b = carve(2, NK, D)

        carve = carver()
        w_raw = carve(WEX)
        w_split = carve(2, 2, WEX, dt=F16)
        b1a, b1v = carve(NE, 2 * NF), carve(NE, NF)
        b2a = carve(NE, D)
        xq = carve(WB, D)
        xh, xl = carve(WB, KD, P, dt=F16), carve(WB, KD, P, dt=F16)
        sg = carve(2, 4, P)
        glu = carve(2, 4 * P)
        acth, actl = carve(WB, NF, P, dt=F16), carve(WB, NF, P, dt=F16)
        yt = carve(WB, D)
        cnt, moved = carve(NE), carve(NE - 1)
        behind, shift = carve(NTILE, NE - 1), carve(NTILE)
        rows_u = carve(NTILE, 2)
        nt, end = carve(NE), carve(NE)
        tcmp = carve(NE, NTILE)
        j128 = carve(NTILE)
        cmp_, cmp_nt = carve(NJT, NE), carve(NJT, NE)
        ej, stj, usedj, tmpj = carve(NJT), carve(NJT), carve(NJT), carve(NJT)
        plan_f = carve(3 * NJT + 2 * NE + WB)
        plan_i = carve(3 * NJT + 2 * NE + WB, dt=I32)
        slot_c = carve(2, LG, dt=U32)
        wv = carve(2, LG, 2)
        got_high = carve(2, LG, D)
        fsum, fin = carve(2, LG, D), carve(2, LG, D)
        fst, fmv = carve(2, LG, 6), carve(2, LG, 2)
        fve, fsd, frs, fnb = carve(2, LG), carve(2, LG), carve(2, LG), carve(2, LG)
        got_low = carve(NTILE, D)
        rows_lh, w_lh = carve(2, NTILE), carve(NTILE, 2)
        swap, keep, w_part = carve(NTILE), carve(NTILE), carve(NTILE)
        slot_low = carve(NTILE, dt=U32)
        x1_all = carver()(NTILE, D)
        assert NTILE * D <= WEX + WEX and (NE - 2) % 2 == 0

        pa = [ctx.enter_context(nc.psum_tensor(f"pa{i}", [P, T], F32)) for i in range(2)]
        pe_ = [ctx.enter_context(nc.psum_tensor(f"pe{i}", [P, T], F32)) for i in range(2)]
        pt = ctx.enter_context(nc.psum_tensor("pt", [P, T], F32))
        pm = ctx.enter_context(nc.psum_tensor("pm", [P, T], F32))
        py = ctx.enter_context(nc.psum_tensor("py", [P, T], F32))
        pz = ctx.enter_context(nc.psum_tensor("pz", [P, T], F32))
        CBT, BTR, CS = pm[:, 0:P], pm[:, P:P + DS], pm[:, P + DS:P + DS + 3 * NH]
        OUT = pm[:, T - D:T]

        consts = sem("consts")
        params = sem("params")
        prepared = sem("prepared")
        hln_in = [sem("hln_in0"), sem("hln_in1")]
        hres_in = [sem("hres_in0"), sem("hres_in1")]
        ln_var = sem("ln_var")
        ln_rs = sem("ln_rs")
        ln_done = sem("ln_done")
        a_full = [sem("a_full0"), sem("a_full1")]
        a_free = [sem("a_free0"), sem("a_free1")]
        sp_in = sem("sp_in")
        sp_ln = sem("sp_ln")
        a_ready = sem("a_ready")
        acc_init = sem("acc_init")
        tanh_ready = sem("tanh_ready")
        xc_done = sem("xc_done")
        zt_ready = sem("zt_ready")
        tri_ready = sem("tri_ready")
        pt_full, pt_free = sem("pt_full"), sem("pt_free")
        pm_full, pm_free = sem("pm_full"), sem("pm_free")
        seg_full, e_free = sem("seg_full"), sem("e_free")
        pm_read = sem("pm_read")
        wdt_ready = sem("wdt_ready")
        m_done = sem("m_done")
        dtx_ready = sem("dtx_ready")
        xw_ready = sem("xw_ready")
        xd_ready = sem("xd_ready")
        y_full, y_free = sem("y_full"), sem("y_free")
        z_full, z_free = sem("z_full"), sem("z_free")
        s_ready = sem("s_ready")
        sd_ready = sem("sd_ready")
        ysum_ready = sem("ysum_ready")
        g_ready = sem("g_ready")
        ss_ready = sem("ss_ready")
        sve_ready, srs_ready = sem("sve_ready"), sem("srs_ready")
        h_ready = sem("h_ready")
        stored = [sem("stored0"), sem("stored1")]
        hx_ready = sem("hx_ready")
        hx_out = [sem("hx_out0"), sem("hx_out1")]
        r_var, r_rs, x1_ready = sem("r_var"), sem("r_rs"), sem("x1_ready")
        gap_ready, p2_ready = sem("gap_ready"), sem("p2_ready")
        oh_ready = sem("oh_ready")
        slot_ready = sem("slot_ready")
        scattered = [sem("scattered0"), sem("scattered1")]
        c_dve1, c_dve2, c_dve3 = sem("c_dve1"), sem("c_dve2"), sem("c_dve3")
        c_act, c_prep, c_pool = sem("c_act"), sem("c_prep"), sem("c_pool")
        hop = sem("hop")
        plan_done = sem("plan_done")
        padded = sem("padded")
        w_raw_in = sem("w_raw_in")
        w_have = sem("w_have")
        bias_in = sem("bias_in")
        xh_ready, x_done = sem("xh_ready"), sem("x_done")
        high0 = sem("high0")
        c_glu = sem("c_glu")
        high_w = sem("high_w")
        uf_ready, ul_ready = sem("uf_ready"), sem("ul_ready")
        gh_ready = sem("gh_ready")
        late_w = sem("late_w")
        xq_in = [sem(f"xq_in{i}") for i in range(WB)]
        f_t_full, f_t_free = sem("f_t_full"), sem("f_t_free")
        f_full = [sem(f"f_full{i}") for i in range(4)]
        silu_done = [sem("silu_done0"), sem("silu_done1")]
        act_done = sem("act_done")
        o_full, o_ready = sem("o_full"), sem("o_ready")
        ans_out = [sem(f"ans_out{i}") for i in range(WB)]
        c_plan = sem("c_plan")
        idx_ready = sem("idx_ready")
        x1_back = sem("x1_back")
        low_sum = sem("low_sum")
        got = [sem("got0"), sem("got1")]
        f_sum, f_var, f_rs, f_out = sem("f_sum"), sem("f_var"), sem("f_rs"), sem("f_out")
        f_scale = sem("f_scale")
        cleared = sem("cleared")
        low_rows = sem("low_rows")
        low_got = sem("low_got")
        out_done = [sem("out_done0"), sem("out_done1")]
        c_fin = sem("c_fin")

        N_PARAMS = 16
        N_CONSTS = 1


        GATE, VALUE = [pe_[0], pe_[1]], [pa[0], pa[1]]

        def rows(dram, b):
            return dram[b].rearrange("(k p) d -> p k d", p=P)

        def over_p(ap, k=None):
            return ap.unsqueeze(2).to_broadcast([ap.shape[0], NH, HD])

        block = ctx.enter_context(nc.Block())

        @block.sync
        def _(sp):
            def turned(v):
                if v == 0:
                    return 1, 1
                return 0, 1 + 6 * v if v <= 10 else 69 + 8 * (v - 11)

            def load_hln(w):
                q = w % 2
                if w >= 2:
                    bank, fills = turned(w - 2)
                    sp.wait_ge(a_full[bank], fills)
                if w < NB:
                    sp.dma_start(hln[:, q], rows(x, w)).then_inc(hln_in[q], 16)
                else:
                    b = min(w - NB, NB - 1)
                    sp.wait_ge(stored[b % 2], 16 * (b // 2 + 1) + 16)
                    sp.dma_start(hln[:, q], rows(h1, b)).then_inc(hln_in[q], 16)

            load_hln(0)
            n_params = [0]

            def param(dst, src):
                sp.dma_start(dst, src).then_inc(params, 16)
                n_params[0] += 1

            for dst, src in ((lnw, ln_w), (lnb, ln_b)):
                param(dst[:, 0:NB], src[:, 0:1].to_broadcast([P, NB, KD]))
                param(dst[:, NB:2 * NB + 1], src[:, 1:2].to_broadcast([P, NB + 1, KD]))
            param(dtb, dt_bias.unsqueeze(0).to_broadcast([P, 2, NH]))
            param(aneg, a_log.unsqueeze(0).to_broadcast([P, 2, NH]))
            param(dsk, d_skip.unsqueeze(0).to_broadcast([P, 2, NH]))
            param(cw, conv_w)
            param(cb, conv_b)
            param(rmsw, rms_w)
            param(gw, gate_w.rearrange("(k p) e -> p k e", p=P))
            param(gb, gate_b.unsqueeze(0).to_broadcast([P, NE]))
            param(win_raw[:, 0], w_in[0].rearrange("(k p) n -> p k n", p=P))
            load_hln(1)
            param(wout_raw[0], w_out[0].rearrange("(k p) n -> p k n", p=P))
            param(wout_raw[1], w_out[1].rearrange("(k p) n -> p k n", p=P))
            param(win_raw[:, 1], w_in[1].rearrange("(k p) n -> p k n", p=P))
            assert n_params[0] == N_PARAMS
            load_hln(2)
            sp.wait_ge(consts, N_CONSTS)
            for s in range(2):
                row = DUMMY + (2 + s) * P
                sp.dma_start(queue[row:row + P, :], zeros[:, :]).then_inc(stored[s], 16)
            for u in range(MAMBA_UNITS + 1):
                q = u % 2
                if u < MAMBA_UNITS:
                    at_least(sp, h_ready, u - 1)
                    if u >= 2:
                        sp.wait_ge(hx_out[q], 16 * (min(u - 2, NB - 2 + q) // 2 + 1))
                    sp.dma_start(hres[:, q], rows(x, u) if u < NB else rows(hx, u - NB)).then_inc(hres_in[q], 16)
                if 1 <= u <= NB:
                    sp.wait_ge(h_ready, u)
                    sp.dma_start(rows(h1, u - 1), ob[:, 1 - q]).then_inc(stored[1 - q], 16)
                    sp.wait_ge(hx_ready, u)
                    sp.dma_start(rows(hx, u - 1), hres[:, 1 - q]).then_inc(hx_out[1 - q], 16)
                if 2 <= u < 2 + CLEAR_STEPS:
                    a, b = NTILE + (u - 2) * CLEAR, NTILE + (u - 1) * CLEAR
                    sp.dma_start(answer[a * P:b * P, :].rearrange("(j p) d -> p j d", p=P),
                                 zeros[:, :].unsqueeze(1).to_broadcast([P, CLEAR, D])).then_inc(cleared, 16)
                if u > NB:
                    b = u - 1 - NB
                    sp.wait_ge(x1_ready, b + 1)
                    sp.dma_start(x1_rows[b * T:(b + 1) * T, :].rearrange("(k p) d -> p k d", p=P),
                                 x1b[:, 1 - q]).then_inc(stored[1 - q], 16)
                if u + 3 <= MAMBA_UNITS:
                    load_hln(u + 3)

            sp.wait_ge(plan_done, 1)
            for e in range(NE):
                end_e = sp.value_load(plan_i[0:1, 3 * NJT + e:3 * NJT + e + 1], min_val=0, max_val=NTOK)
                sp.dma_start(queue[bass.ds(end_e + e * QROWS, P), :], zeros[:, :]).then_inc(padded, 16)
            sp.wait_ge(padded, 16 * NE)
            for s in range(2):
                sp.wait_ge(scattered[s], 16 * 2 * NK * (NB // 2) + 16)
                sp.wait_ge(stored[s], 16 * NB + 16)

            def load_rows(i, r):
                row = sp.value_load(plan_i[0:1, bass.ds(WB * i + r, 1)], min_val=0, max_val=DUMMY + (WB - 1) * P)
                sp.dma_start(xq[:, r % WB], queue[bass.ds(row, P), :]).then_inc(xq_in[r % WB], 16)

            sp.wait_ge(cleared, 16 * CLEAR_STEPS)
            for r in range(WB):
                load_rows(0, r)
            sp.dma_start(b1a, b1).then_inc(bias_in, 16)
            sp.dma_start(b2a, b2.unsqueeze(0).to_broadcast([P, NE, D])).then_inc(bias_in, 16)
            with sp.Fori(0, NJ // WB) as i:
                for r in range(WB):
                    sp.wait_ge(o_ready, WB * i + (r + 2))
                    sp.sem_inc(hop, 1)
                    sp.dma_start(answer[bass.ds((WB * i + r) * P, P), :], yt[:, r]).then_inc(ans_out[r], 16)
                    load_rows(i + 1, r)

            def store_out(i, q):
                sp.wait_ge(f_out, 2 * i + (q + 1))
                sp.sem_inc(hop, 1)
                sp.dma_start(out[bass.ds((2 * i + q) * T, T), :].rearrange("(k p) d -> p k d", p=P),
                             fin[:, q]).then_inc(out_done[q], 16)

            with sp.Fori(0, NB // 2) as i:
                for q in range(2):
                    store_out(i, q)
            for q in range(2):
                sp.wait_ge(out_done[q], 16 * (NB // 2))

        @block.tensor
        def _(pe):
            def fill(st, name, product):
                bank, before = st.fill(name)
                at_least(pe, a_free[bank], before)
                product(pa[bank]).then_inc(a_full[bank], 1)

            def s1_fill(st, name):
                l, vq = st.next_layer, 1 - st.q
                v = st.u + 1
                passes = [(d, ab) for d in range(KD) for ab in PASSES]
                if name[:2] == "ln":
                    d, ahead = int(name[2]), not (st.u == -1 and len(name) == 3) if isinstance(st.u, int) else True
                    w, wq = (st.u + 2, st.q) if ahead else (0, 0)
                    if d == 0:
                        pe.wait_ge(ln_done, w + 1)

                    def go(bank):
                        for k in range(NK):
                            ins = pe.transpose(bank[:, k * P:(k + 1) * P], hln[:, wq, k, d * P:(d + 1) * P], ident[:, :])
                        return ins
                elif name == "dt":
                    pe.wait_ge(ul_ready, KD * (v + 1))
                    if isinstance(v, int) and v == 0:
                        pe.wait_ge(prepared, 1)
                    if isinstance(v, int) and v == NB:
                        pe.wait_ge(late_w, 1)

                    def go(bank):
                        for k in range(NK):
                            for n, (d, (a, b)) in enumerate(passes):
                                ins = pe.matmul(bank[:, k * NH:(k + 1) * NH], uT[:, vq, a, d, k * P:(k + 1) * P],
                                                win[:, l, b, d, ODT:ODT + NH], start=(n == 0), stop=(n == len(passes) - 1))
                        return ins
                elif name[0] == "c":
                    c = int(name[1])

                    def go(bank):
                        for n, (d, (a, b)) in enumerate(passes):
                            ins = pe.matmul(bank[:, :], win[:, l, b, d, OX + c * P:OX + (c + 1) * P], uT[:, vq, a, d, :],
                                            start=(n == 0), stop=(n == len(passes) - 1))
                        return ins
                else:
                    k = int(name[1])

                    def go(bank):
                        for n, (d, (a, b)) in enumerate(passes):
                            ins = pe.matmul(bank[:, :], uT[:, vq, a, d, k * P:(k + 1) * P], win[:, l, b, d, 0:DI],
                                            start=(n == 0), stop=(n == len(passes) - 1))
                        return ins
                fill(st, name, go)

            def s3_fill(st, name):
                w_q = 1 - st.q
                if name in ("t0", "t1"):
                    d = int(name[1])
                    if d == 0:
                        pe.wait_ge(x1_ready, st.u - NB)

                    def go(bank):
                        for k in range(NK):
                            ins = pe.transpose(bank[:, k * P:(k + 1) * P], x1b[:, w_q, k, d * P:(d + 1) * P], ident[:, :])
                        return ins
                elif name == "lg":
                    for n in ("t0", "t1"):
                        bank, before = st.fill(n)
                        pe.wait_ge(a_free[bank], before + 1)

                    def go(bank):
                        for k in range(NK):
                            for d in range(KD):
                                ins = pe.matmul(bank[:, k * NE:(k + 1) * NE], x1T[:, d, k * P:(k + 1) * P],
                                                gw[:, d, :], start=(d == 0), stop=(d == KD - 1))
                        return ins
                else:
                    pe.wait_ge(oh_ready, st.u - NB)

                    def go(bank):
                        pe.matmul(bank[:, 0:NK * NE], tri_lt[:, :], oh.rearrange("p k e -> p (k e)"), start=True, stop=True)
                        return pe.matmul(bank[:, NK * NE:2 * NK * NE], ones[:, :], oh.rearrange("p k e -> p (k e)"),
                                         start=True, stop=True)
                fill(st, name, go)

            def do_fills(st, names):
                for n in names:
                    if n in ONLY3:
                        s3_fill(st, n)
                    else:
                        s1_fill(st, n)

            def chunk_a(c):
                q, n, k = c.q, c.n, c.k
                tk = slice(k * P, (k + 1) * P)
                if k == 0:
                    pe.wait_ge(xc_done, 5 * c.u + 5)
                    pe.wait_ge(a_ready, c.u + 1)
                at_least(pe, pt_free, c.use("a"))
                for t in range(NCT):
                    ins = pe.transpose(pt[:, t * P:(t + 1) * P], xcT[:, q, t, tk], ident[:, :])
                ins.then_inc(pt_full, 1)
                at_least(pe, pm_free, c.use("a"))
                for s, w in enumerate((tri_le, tri_gt, ones)):
                    pe.matmul(CS[:, s * NH:(s + 1) * NH], w[:, :], a_s[:, q, k, :], start=True, stop=True)
                pe.transpose(BTR, bT[0:DS, q, tk], ident[0:DS, 0:DS])
                pe.matmul(CBT, bT[0:DS, q, tk], cT[0:DS, q, tk], start=True, stop=True).then_inc(pm_full, 1)
                pe.wait_ge(tri_ready, n + 1)
                for h in range(2):
                    at_least(pe, e_free, 2 * n - 1 + h)
                    pe.matmul(pe_[h][:, :], tri_gt[:, :],
                              tri_a[:, c.kq, 4 * h:4 * h + 4, :].rearrange("p h t -> p (h t)"),
                              start=True, stop=True).then_inc(seg_full, 1)

            def chunk_z(c):
                pe.wait_ge(z_free, c.u6 + 2 * c.k - 1)
                pe.matmul(pz[:, :], cT[0:DS, c.q, c.k * P:(c.k + 1) * P],
                          state[0:DS, (c.k - 1) % 2].rearrange("p h d -> p (h d)"),
                          start=True, stop=True).then_inc(z_full, 1)

            def chunk_b(c):
                q, n, k, kq, u6 = c.q, c.n, c.k, c.kq, c.u6
                pe.wait_ge(m_done, n + 1)
                pe.wait_ge(dtx_ready, n + 1)
                at_least(pe, y_free, n)
                for h in range(NH):
                    ins = pe.matmul(py[:, h * HD:(h + 1) * HD], mix[:, kq, h, :], dtx[:, kq, h, :], start=True, stop=True)
                ins.then_inc(y_full, 1)
                if k < NK - 1:
                    pe.wait_ge(xw_ready, 3 * c.u + k + 1)
                    at_least(pe, z_free, u6 + 2 * k)
                    pe.wait_ge(pm_read, n + 1)
                    pe.matmul(pz[0:DS, :], bs[:, kq, :], xw[:, kq].rearrange("p h d -> p (h d)"),
                              start=True, stop=True).then_inc(z_full, 1)

            def chunk_c(c):
                pe.wait_ge(g_ready, c.n + 1)
                pe.wait_ge(pt_free, c.use("o"))
                gk = g[:, c.kq].rearrange("p h d -> p (h d)")
                for t in range(NCT):
                    ins = pe.transpose(pt[:, t * P:(t + 1) * P], gk[:, t * P:(t + 1) * P], ident[:, :])
                ins.then_inc(pt_full, 1)

            def chunk_d(c):
                pe.wait_ge(pt_free, c.use("o") + 1)
                pe.wait_ge(pm_free, c.use("o"))
                passes = [(t, ab) for t in range(NCT) for ab in PASSES]
                for n, (t, (a, b)) in enumerate(passes):
                    ins = pe.matmul(OUT, gT[:, c.kq, a, t, :], wout[:, c.layer, b, t, :],
                                    start=(n == 0), stop=(n == len(passes) - 1))
                ins.then_inc(pm_full, 1)

            def body(st):
                s1, s3 = not st.last, st.s3
                c = [Chunk(st, k) for k in range(NK + 1)]
                do_fills(st, ["dt", "c4", "c0"] * s1)
                chunk_b(c[0])
                chunk_a(c[1])
                chunk_c(c[0])
                chunk_z(c[1])
                do_fills(st, ["c1"] * s1)
                chunk_d(c[0])
                do_fills(st, ["c2"] * s1)
                chunk_b(c[1])
                chunk_a(c[2])
                chunk_c(c[1])
                chunk_z(c[2])
                do_fills(st, ["c3"] * s1)
                chunk_d(c[1])
                do_fills(st, ["t0", "t1"] * s3 + ["z0"] * s1)
                chunk_b(c[2])
                chunk_a(c[3])
                chunk_c(c[2])
                chunk_z(c[3])
                do_fills(st, ["lg"] * s3 + ["z1"] * s1)
                chunk_d(c[2])
                do_fills(st, ["z2"] * s1 + ["rk"] * s3)
                chunk_b(c[3])
                if s1:
                    chunk_a(c[4])
                chunk_c(c[3])
                do_fills(st, ["ln0", "ln1"] * s1)
                chunk_d(c[3])
                do_fills(st, ["z3"] * s1)

            def prologue(st):
                do_fills(st, FIRST[:-1])
                chunk_a(Chunk(st, NK))
                do_fills(st, FIRST[-1:])

            pe.wait_ge(consts, N_CONSTS)
            schedule(pe, body, prologue, lambda st: do_fills(st, ONLY3))

            def part(p, hl, first, n):
                return w_split[:, bass.ds(p, 1), hl, first:first + n].rearrange("p a b -> p (a b)")

            def parities(i):
                v = pe.value_load(plan_i[0:1, bass.ds(i + 2 * NJT, 1)], min_val=0, max_val=15)
                return [v % 2, (v // 2) % 2, (v // 4) % 2, v // 8], v % 8

            def turn(i, r):
                b = r % WB
                pe.wait_ge(xq_in[b], 16 * (i + (r // WB + 1)))
                at_least(pe, x_done, WB * i + r)
                for d in range(KD):
                    ins = pe.transpose(pt[:, d * P:(d + 1) * P], xq[:, b, d * P:(d + 1) * P], ident[:, :])
                ins.then_inc(f_t_full, 1)

            def hidden(i, r, p):
                j = WB * i + r
                pe.wait_ge(x_done, j + 1)
                pe.sem_inc(hop, 1)
                with pe.If(p < 1):
                    products(j, r, 0)
                with pe.Else():
                    products(j, r, 1)

            def products(j, r, p):
                for half in range(2):
                    for bank, first, full in ((GATE[half], FF, 2 * half), (VALUE[half], 0, 2 * half + 1)):
                        if full % 2 == 0:
                            at_least(pe, silu_done[half], j)
                        else:
                            at_least(pe, act_done, 2 * j - 1 + half)
                        for f in range(4):
                            col = first + (4 * half + f) * P
                            passes = [(hl, x, d) for d in range(KD) for hl, x in ((0, xh), (0, xl), (1, xh))]
                            for n, (hl, x, d) in enumerate(passes):
                                ins = pe.matmul(bank[:, f * P:(f + 1) * P], w_split[:, p, hl, d * 2 * FF + col:d * 2 * FF + col + P],
                                                x[:, r, d, :], start=(n == 0), stop=(n == len(passes) - 1))
                        ins.then_inc(f_full[full], 1)

            def result(i, r, p):
                b = r % WB
                pe.wait_ge(o_ready, WB * i + (r + 1))
                for half in range(2):
                    pe.wait_ge(act_done, 2 * (WB * i + r) + half + 1)
                    passes = [(hl, a, f) for f in range(4 * half, 4 * half + 4) for hl, a in ((0, acth), (0, actl), (1, acth))]
                    for n, (hl, a, f) in enumerate(passes):
                        ins = pe.matmul(py[:, 0:D], a[:, b, f, :], part(p, hl, W1N + f * D, D),
                                        start=(half == 0 and n == 0), stop=(half == 1 and n == len(passes) - 1))
                ins.then_inc(o_full, 1)

            turn(0, 0)
            pe.wait_ge(plan_done, 1)
            pe.sem_inc(hop, 1)
            p, _ = parities(0)
            for r in range(WB):
                hidden(0, r, p[r])
                turn(0, r + 1)
                if r > 0:
                    result(0, r - 1, p[r - 1])
            def tiles(i, p, buffer):
                for r in range(WB):
                    if buffer is None:
                        hidden(i, r, p[r])
                    else:
                        pe.wait_ge(x_done, WB * i + (r + 1))
                        products(WB * i + r, r, buffer)
                    turn(i, r + 1)
                    result(i - 1 if r == 0 else i, (r - 1) % WB, p[(r - 1) % 4])

            with pe.Fori(1, NJ // WB) as i:
                p, three = parities(i)
                with pe.If(three < 1):
                    tiles(i, p, 0)
                with pe.Else():
                    with pe.If(three >= 7):
                        tiles(i, p, 1)
                    with pe.Else():
                        tiles(i, p, None)
                    pe.sem_inc(hop, 1)
            p, _ = parities(NJ // WB)
            result(NJ // WB - 1, WB - 1, p[3])

        @block.scalar
        def _(act_e):
            e = act_e

            def wait_fill(st, name):
                bank, before = st.fill(name)
                e.wait_ge(a_full[bank], before + 1)
                return bank, before

            def ln_out(st, name):
                bank, _ = wait_fill(st, name)
                d, ahead = int(name[2]), not (st.u == -1 and len(name) == 3) if isinstance(st.u, int) else True
                w, wq = (st.u + 2, st.q) if ahead else (0, 0)
                e.sem_inc(hop, 1)
                for dst in (uT[:, wq, 0, d, :], uf[:, d, :]):
                    ins = e.activation(dst, pa[bank][:, :], ACT.Identity,
                                       scale=lnw[:, bass.ds(w, 1), d], bias=lnb[:, bass.ds(w, 1), d])
                ins.then_inc(a_free[bank], 1)

            def spread(st, k):
                q, m = (st.q + k // NK) % 2, 4 * st.u + k
                at_least(e, seg_full, 2 * (m - 1))
                if k == NK:
                    e.wait_ge(a_ready, st.u + 2)
                for h in range(NH):
                    ins = e.activation(tri_a[:, k % 2, h], tri_le[:, :], ACT.Copy, scale=a_s[:, q, k % NK, h:h + 1])
                ins.then_inc(tri_ready, 1)

            def conv_first(st, c):
                idx = CONV_ORDER.index(c)
                l, m, mq = st.next_layer, 5 * (st.u + 1) + idx, (1 - st.q + idx) % 2
                bank, _ = wait_fill(st, c)
                at_least(e, xc_done, m - 1)
                ct = int(c[1])
                e.activation(acc[:, mq], pa[bank][:, :], ACT.Identity, scale=cw[:, l, ct, TAPS - 1:TAPS],
                             bias=cb[:, l, ct:ct + 1]).then_inc(acc_init, 1)

            def conv_tanh(st, c):
                idx = CONV_ORDER.index(c)
                mq = (1 - st.q + idx) % 2
                bank, before = st.fill(c)
                e.wait_ge(a_free[bank], before + 1)
                e.activation(th[:, mq], acc[:, mq], ACT.Tanh).then_inc(tanh_ready, 1)

            def z_tanh(st, k):
                bank, _ = wait_fill(st, f"z{k}")
                if k >= 2:
                    b2_, before = st.fill(f"z{k - 2}")
                    e.wait_ge(a_free[b2_], before + 1)
                e.activation(zt[:, k % 2], pa[bank][:, :], ACT.Tanh, scale=0.5 / S1).then_inc(zt_ready, 1)

            def softplus(st):
                v = st.u + 1
                e.wait_ge(sp_in, v + 1)
                e.activation(e1, nab, ACT.Exp).then_inc(c_act, 1)
                e.wait_ge(c_act, v + 1)
                e.activation(l1, e1, ACT.Ln, bias=1.0).then_inc(sp_ln, 1)

            def chunk_a(c):
                n, kq = c.n, c.kq
                e.wait_ge(pt_full, c.use("a") + 1)
                at_least(e, xd_ready, n - 1)
                e.activation(xs[:, kq].rearrange("p h d -> p (h d)"), pt[:, :], ACT.Copy).then_inc(pt_free, 1)
                e.wait_ge(pm_full, c.use("a") + 1)
                e.activation(ex[:, kq].rearrange("p s h -> p (s h)"), CS, ACT.Exp)
                e.activation(bs[:, kq], BTR, ACT.Copy).then_inc(pm_read, 1)
                at_least(e, m_done, n - 1)
                for h in range(2):
                    e.wait_ge(seg_full, 2 * n + h + 1)
                    e.activation(decay[:, kq, 4 * h:4 * h + 4].rearrange("p h t -> p (h t)"), pe_[h][:, :],
                                 ACT.Exp).then_inc(e_free, 1)

            def chunk_c(c):
                q, n, kq = c.q, c.n, c.kq
                e.wait_ge(pt_full, c.use("o") + 1)
                e.activation(gT[:, kq, 0].rearrange("p c t -> p (c t)"), pt[:, :], ACT.Copy, scale=SG).then_inc(gh_ready, 1)
                e.wait_ge(g_ready, n + 1)
                at_least(e, ss_ready, n)
                e.activation(junk, g[:, kq].rearrange("p h d -> p (h d)"), ACT.Square,
                             accum_out=ss[:, q, c.k:c.k + 1]).then_inc(ss_ready, 1)

            def chunk_d(c):
                if c.k == 0:
                    e.wait_ge(stored[c.q], 16 * c.st.h + 16)
                e.wait_ge(pm_full, c.use("o") + 1)
                e.activation(ob[:, c.q, c.k, :], OUT, ACT.Copy, scale=1.0 / S2).then_inc(pm_free, 1)

            def x1_out(st, d):
                bank, _ = wait_fill(st, f"t{d}")
                e.activation(x1T[:, d, :], pa[bank][:, :], ACT.Copy).then_inc(a_free[bank], 1)

            def gap_exp(st):
                e.wait_ge(gap_ready, st.u - NB)
                e.activation(p2, gap, ACT.Exp).then_inc(p2_ready, 1)

            def high_parts(n):
                if n == 0:
                    e.wait_ge(w_raw_in, 64)
                for a, b, scale in quarter(n):
                    ins = e.activation(w_split[:, 0, 0, a:b], w_raw[:, a:b], ACT.Copy, scale=scale)
                ins.then_inc(high0, 1)

            def body(st):
                s1, s3 = not st.last, st.s3
                c = [Chunk(st, k) for k in range(NK + 1)]
                if s1:
                    softplus(st)
                    conv_first(st, "c4")
                    conv_first(st, "c0")
                if st.first:
                    high_weights(1)
                if s1:
                    conv_tanh(st, "c4")
                chunk_a(c[1])
                chunk_c(c[0])
                if s1:
                    conv_tanh(st, "c0")
                    conv_first(st, "c1")
                spread(st, 2)
                chunk_d(c[0])
                if s1:
                    conv_first(st, "c2")
                    conv_tanh(st, "c1")
                chunk_a(c[2])
                chunk_c(c[1])
                if s1:
                    conv_tanh(st, "c2")
                    conv_first(st, "c3")
                spread(st, 3)
                chunk_d(c[1])
                if s3:
                    x1_out(st, 0)
                    x1_out(st, 1)
                if s1:
                    z_tanh(st, 0)
                    conv_tanh(st, "c3")
                chunk_a(c[3])
                chunk_c(c[2])
                if s1:
                    z_tanh(st, 1)
                    spread(st, 4)
                chunk_d(c[2])
                if s1:
                    z_tanh(st, 2)
                if s3:
                    gap_exp(st)
                if s1:
                    chunk_a(c[4])
                else:
                    high_parts(0)
                chunk_c(c[3])
                if s1:
                    ln_out(st, "ln0")
                    ln_out(st, "ln1")
                chunk_d(c[3])
                if s1:
                    z_tanh(st, 3)
                    spread(st, 5)
                else:
                    for n in range(1, 4):
                        high_parts(n)

            def prologue(st):
                ln_out(st, "ln0")
                ln_out(st, "ln1")
                softplus(st)
                conv_first(st, "c4")
                for c, then in zip(CONV_ORDER, CONV_ORDER[1:]):
                    conv_first(st, then)
                    conv_tanh(st, c)
                z_tanh(st, 0)
                conv_tanh(st, CONV_ORDER[-1])
                z_tanh(st, 1)
                z_tanh(st, 2)
                spread(st, NK)
                ln_out(st, "ln0n")
                ln_out(st, "ln1n")
                chunk_a(Chunk(st, NK))
                z_tanh(st, NK - 1)
                spread(st, NK + 1)

            def epilogue(st):
                x1_out(st, 0)
                x1_out(st, 1)
                gap_exp(st)

            e.wait_ge(params, 16 * N_PARAMS)
            e.activation(aneg, aneg, ACT.Exp).then_inc(c_prep, 1)

            def high_weights(l):
                e.activation(win[:, l, 0], win_raw[:, l], ACT.Copy, scale=S1).then_inc(high_w, 1)
                e.wait_ge(c_prep, 3 + l)
                e.activation(wout[:, l, 0], wout_raw[l], ACT.Copy).then_inc(high_w, 1)

            high_weights(0)
            e.wait_ge(prepared, 1)
            schedule(e, body, prologue, epilogue)

            def rows_out(i, r):
                ex_ = e.value_load(plan_i[0:1, bass.ds(WB * i + (r + NJT), 1)], min_val=0, max_val=NE - 1)
                e.wait_ge(w_have, ex_ + 1)
                e.wait_ge(f_t_full, WB * i + (r + 1))
                e.activation(xh[:, r % WB].rearrange("p d t -> p (d t)"), pt[:, 0:KD * P], ACT.Copy).then_inc(xh_ready, 1)

            def tile(i, r):
                j = WB * i + r
                ex_ = e.value_load(plan_i[0:1, bass.ds(WB * i + (r + NJT), 1)], min_val=0, max_val=NE - 1)
                for half in range(2):
                    e.wait_ge(f_full[2 * half], j + 1)
                    at_least(e, act_done, 2 * j - 1 + half)
                    e.sem_inc(hop, 1)
                    for f in range(4):
                        ff = NF + 4 * half + f
                        ins = e.activation(sg[:, half, f, :], GATE[half][:, f * P:(f + 1) * P], ACT.Silu,
                                           bias=b1a[:, bass.ds(ex_, 1), ff], scale=1.0 / S1)
                    ins.then_inc(silu_done[half], 1)
                rows_out(i, r + 1)

            e.wait_ge(plan_done, 1)
            rows_out(0, 0)
            e.wait_ge(bias_in, 32)
            for r in range(WB):
                tile(0, r)
            with e.Fori(1, NJ // WB) as i:
                for r in range(WB):
                    tile(i, r)

            def normalise(i, first):
                for q in range(2):
                    e.wait_ge(f_var, 2 * i + (q + 1))
                    e.activation(fsd[:, q], fve[:, q], ACT.Sqrt).then_inc(f_rs, 1)
                    e.wait_ge(f_scale, 2 * i + (q + 1))
                    if not first:
                        e.wait_ge(out_done[q], 16 * i)
                    e.sem_inc(hop, 1)
                    for k in range(LG):
                        ins = e.activation(fin[:, q, k], fsum[:, q, k], ACT.Identity, scale=frs[:, q, k:k + 1],
                                           bias=fnb[:, q, k:k + 1])
                    ins.then_inc(f_out, 1)

            normalise(0, True)
            with e.Fori(1, NB // 2) as i:
                normalise(i, False)

        @block.vector
        def _(dve):
            def ln_stats(w, hw, wq):
                ch = Chain(dve, c_dve1, 2, w)
                dve.wait_ge(hln_in[wq], 16 * (hw + 1))
                for k in range(NK):
                    ins = dve.bn_stats(st6[:, k, :], hln[:, wq, k, :])
                ch.link(ins)
                dve.sem_inc(hop, 1)
                for k in range(NK):
                    ins = dve.bn_aggr(mv[:, k, :], st6[:, k, :])
                ch.link(ins)
                ch.close()
                dve.tensor_scalar(ve, mv[:, :, 1], EPS, None, ALU.add).then_inc(ln_var, 1)

            def ln_apply(w, wq):
                dve.wait_ge(ln_rs, w + 1)
                for k in range(NK):
                    ins = dve.tensor_scalar(hln[:, wq, k, :], hln[:, wq, k, :], mv[:, k, 0:1], rs[:, k:k + 1],
                                            ALU.subtract, ALU.mult)
                ins.then_inc(ln_done, 1)

            def wait_fill(st, name):
                bank, before = st.fill(name)
                dve.wait_ge(a_full[bank], before + 1)
                return bank, before

            def u_low(w, wq, d, bank, fills):
                dve.wait_ge(a_free[bank], fills)
                dve.tensor_tensor(uT[:, wq, 1, d, :], uf[:, d, :], uT[:, wq, 0, d, :], ALU.subtract).then_inc(ul_ready, 1)

            def u_lows(st):
                for d in range(KD):
                    bank, before = st.fill(f"ln{d}")
                    u_low(st.u + 2, st.q, d, bank, before + 1)

            def g_low(c):
                dve.wait_ge(gh_ready, c.n + 1)
                dve.scalar_tensor_tensor(gT[:, c.kq, 1].rearrange("p c t -> p (c t)"), pt[:, :], SG,
                                         gT[:, c.kq, 0].rearrange("p c t -> p (c t)"), ALU.mult,
                                         ALU.subtract).then_inc(pt_free, 1)

            def dt_first(st):
                l, v = st.next_layer, st.u + 1
                bank, _ = wait_fill(st, "dt")
                src = pa[bank][:, 0:NK * NH].rearrange("p (k h) -> p k h", k=NK)
                ins = dve.scalar_tensor_tensor(dtr, src, 1.0 / S1, dtb[:, l].unsqueeze(1).to_broadcast([P, NK, NH]),
                                               ALU.mult, ALU.add)
                ins.then_inc(a_free[bank], 1)
                dve.wait_ge(a_free[bank], st.fill("dt")[1] + 1)
                dve.scalar_tensor_tensor(nab, dtr, -1.0, dtr, ALU.mult, ALU.min).then_inc(sp_in, 1)

            def dt_last(st, ch):
                l, v, vq = st.next_layer, st.u + 1, 1 - st.q
                dve.wait_ge(sp_ln, v + 1)
                ch.link(dve.scalar_tensor_tensor(dt_s[:, vq], dtr, 0.0, l1, ALU.max, ALU.add))
                dve.tensor_tensor(a_s[:, vq], dt_s[:, vq], aneg[:, l].unsqueeze(1).to_broadcast([P, NK, NH]),
                                  ALU.mult).then_inc(a_ready, 1)

            def taps(st, c, ch):
                idx, ct, l = CONV_ORDER.index(c), int(c[1]), st.next_layer
                m, mq = 5 * (st.u + 1) + idx, (1 - st.q + idx) % 2
                bank, _ = st.fill(c)
                dve.wait_ge(acc_init, m + 1)
                for s in range(1, TAPS):
                    ins = dve.scalar_tensor_tensor(acc[:, mq, s:T], pa[bank][:, 0:T - s],
                                                   cw[:, l, ct, TAPS - 1 - s:TAPS - s], acc[:, mq, s:T],
                                                   ALU.mult, ALU.add)
                    if s < TAPS - 1:
                        ch.link(ins)
                ins.then_inc(a_free[bank], 1)

            def silu_x(st, c):
                idx, ct, vq = CONV_ORDER.index(c), int(c[1]), 1 - st.q
                m, mq = 5 * (st.u + 1) + idx, (1 - st.q + idx) % 2
                dve.wait_ge(tanh_ready, m + 1)
                if ct < NCT:
                    ins = dve.scalar_tensor_tensor(xcT[:, vq, ct, :], th[:, mq], 1.0, acc[:, mq], ALU.add, ALU.mult)
                else:
                    dve.scalar_tensor_tensor(bT[0:DS, vq], th[0:DS, mq], 1.0, acc[0:DS, mq], ALU.add, ALU.mult)
                    ins = dve.scalar_tensor_tensor(cT[0:DS, vq], th[DS:P, mq], 1.0, acc[DS:P, mq], ALU.add, ALU.mult)
                ins.then_inc(xc_done, 1)

            def z_gate(st, k):
                vq = 1 - st.q
                bank, _ = st.fill(f"z{k}")
                dve.wait_ge(zt_ready, 4 * (st.u + 1) + k + 1)
                dve.scalar_tensor_tensor(zs[:, vq, k, :], zt[:, k % 2], 1.0, pa[bank][:, :], ALU.add,
                                         ALU.mult).then_inc(a_free[bank], 1)

            def end_a(st):
                dve.wait_ge(ss_ready, 4 * st.u)
                dve.tensor_scalar(sve, ss[:, 1 - st.q], 1.0 / (4 * S1 * S1 * DI), EPS, ALU.mult, ALU.add).then_inc(sve_ready, 1)

            def end_b(st):
                wq = 1 - st.q
                dve.wait_ge(srs_ready, st.u)
                dve.wait_ge(pm_free, 8 * st.u + (0 if st.epilogue else 1))
                dve.wait_ge(hres_in[wq], 16 * ((st.h + 1) if wq == 0 else st.h))
                for k in range(NK):
                    ins = dve.scalar_tensor_tensor(ob[:, wq, k, :], ob[:, wq, k, :], srs[:, k:k + 1],
                                                   hres[:, wq, k, :], ALU.mult, ALU.add)
                ins.then_inc(h_ready, 1)

            def chunk_a(c):
                n, kq = c.n, c.kq
                dve.wait_ge(pm_read, n + 1)
                if c.k == 0:
                    dve.wait_ge(a_ready, c.u + 1)
                dve.tensor_tensor(wdt[:, kq], ex[:, kq, 1], dt_s[:, c.q, c.k], ALU.mult).then_inc(wdt_ready, 1)
                dve.tensor_tensor(cbm[:, kq], CBT, tri_le[:, :], ALU.mult).then_inc(pm_free, 1)

            def chunk_mix(c):
                n, kq = c.n, c.kq
                dve.wait_ge(pm_free, c.use("a") + 1)
                dve.wait_ge(e_free, 2 * n + 2)
                at_least(dve, y_full, n - 1)
                dve.tensor_tensor(mix[:, kq], decay[:, kq], cbm[:, kq].unsqueeze(1).to_broadcast([P, NH, P]),
                                  ALU.mult).then_inc(m_done, 1)

            def chunk_b1(c):
                if c.k > 0:
                    dve.wait_ge(z_full, c.u6 + 2 * c.k)
                    dve.tensor_tensor(y1[:, c.kq], pz.rearrange("p (h d) -> p h d", h=NH), over_p(ex[:, c.kq, 0]),
                                      ALU.mult).then_inc(z_free, 1)

            def chunk_b2(c):
                n, k, kq = c.n, c.k, c.kq
                dve.wait_ge(y_full, n + 1)
                at_least(dve, g_ready, n - 1)
                if k > 0:
                    dve.wait_ge(ysum_ready, 3 * c.u + k)
                    other = y1
                else:
                    dve.wait_ge(xd_ready, n + 1)
                    other = xd
                dve.tensor_tensor(y2[:, kq], py.rearrange("p (h d) -> p h d", h=NH), other[:, kq],
                                  ALU.add).then_inc(y_free, 1)
                if k < NK - 1:
                    dve.wait_ge(z_full, c.u6 + 2 * k + 1)
                    new = pz[0:DS].rearrange("p (h d) -> p h d", h=NH)
                    if k == 0:
                        dve.tensor_copy(state[0:DS, 0], new).then_inc(z_free, 1)
                    else:
                        dve.wait_ge(sd_ready, 2 * c.u + k)
                        dve.tensor_tensor(state[0:DS, kq], new, state_d[0:DS], ALU.add).then_inc(z_free, 1)

            def s3_stats(st):
                ch = Chain(dve, c_dve3, 12, st.u - (NB + 1))
                wq = 1 - st.q
                dve.wait_ge(h_ready, st.u)
                for k in range(NK):
                    ins = dve.bn_stats(rst6[:, k, :], ob[:, wq, k, :])
                ch.link(ins)
                dve.sem_inc(hop, 1)
                for k in range(NK):
                    ins = dve.bn_aggr(rmv[:, k, :], rst6[:, k, :])
                ch.link(ins)
                dve.tensor_scalar(rve, rmv[:, :, 1], EPS, None, ALU.add).then_inc(r_var, 1)
                return ch

            def s3_apply(st):
                wq = 1 - st.q
                dve.wait_ge(r_rs, st.u - NB)
                before = st.h - 1 if wq == 1 else st.h
                dve.wait_ge(stored[wq], 16 * before + 16)
                dve.wait_ge(scattered[wq], 128 * (before - 4) + 16)
                for k in range(NK):
                    ins = dve.tensor_scalar(x1b[:, wq, k, :], ob[:, wq, k, :], rmv[:, k, 0:1], rrs[:, k:k + 1],
                                            ALU.subtract, ALU.mult)
                ins.then_inc(x1_ready, 1)

            def s3_top(st, ch):
                bank, before = wait_fill(st, "lg")
                src = pa[bank][:, 0:NK * NE].rearrange("p (k e) -> p k e", k=NK)
                dve.tensor_tensor(logit, src, gb.unsqueeze(1).to_broadcast([P, NK, NE]), ALU.add).then_inc(a_free[bank], 1)
                dve.wait_ge(a_free[bank], before + 1)
                dve.sem_inc(hop, 1)
                for k in range(NK):
                    ins = dve.max(top8[:, k, :], logit[:, k, :])
                ch.link(ins)
                dve.sem_inc(hop, 1)
                for k in range(NK):
                    ins = dve.max_index(top_i[:, k, :], top8[:, k, :], logit[:, k, :])
                ch.link(ins)
                dve.tensor_tensor(gap, top8[:, :, 1], top8[:, :, 0], ALU.subtract).then_inc(gap_ready, 1)
                ch.link(dve.tensor_copy(top_f, top_i))
                iota = iota_e[:, :].unsqueeze(1).to_broadcast([P, NK, NE])
                dve.tensor_tensor(oh1, iota, top_f[:, :, 0].unsqueeze(2).to_broadcast([P, NK, NE]), ALU.is_equal)
                ch.link(dve.tensor_tensor(oh2, iota, top_f[:, :, 1].unsqueeze(2).to_broadcast([P, NK, NE]), ALU.is_equal))
                dve.tensor_tensor(oh, oh1, oh2, ALU.add).then_inc(oh_ready, 1)

            def s3_place(st, ch):
                bank, before = wait_fill(st, "rk")
                wq = 1 - st.q
                rank = pa[bank][:, 0:NK * NE].rearrange("p (k e) -> p k e", k=NK)
                total = pa[bank][:, NK * NE:2 * NK * NE].rearrange("p (k e) -> p k e", k=NK)
                dve.wait_ge(p2_ready, st.u - NB)
                dve.tensor_scalar(gap, p2, 1.0, None, ALU.add)
                prev = count
                for k in range(NK):
                    ins = dve.tensor_tensor(base[:, k, :], prev[:, :] if k == 0 else base[:, k - 1, :], total[:, k, :], ALU.add)
                    ch.link(ins)
                dve.tensor_tensor(pos[:, 0, :], rank[:, 0, :], count[:, :], ALU.add)
                dve.tensor_tensor(pos[:, 1:NK, :], rank[:, 1:NK, :], base[:, 0:NK - 1, :], ALU.add).then_inc(a_free[bank], 1)
                dve.wait_ge(a_free[bank], before + 1)
                dve.tensor_copy(count[:, :], base[:, NK - 1, :])
                dve.tensor_tensor(pick[:, 0], pos, oh1, ALU.mult)
                dve.reciprocal(pw[:, :, 0], gap)
                ch.link(dve.tensor_tensor(pick[:, 1], pos, oh2, ALU.mult))
                dve.tensor_tensor(pw[:, :, 1], p2, pw[:, :, 0], ALU.mult)
                dve.tensor_reduce(pw[:, :, 2], pick[:, 0], AX.X, ALU.add)
                ch.link(dve.tensor_reduce(pw[:, :, 3], pick[:, 1], AX.X, ALU.add))
                for s in range(2):
                    ins = dve.tensor_copy(slot[:, wq, s * NK:(s + 1) * NK], pw[:, :, 2 + s])
                ins.then_inc(slot_ready, 1)
                dve.tensor_copy(route[:, bass.ds(NK * (st.u - (NB + 1)), NK), :], pw)
                ch.close()

            def body(st):
                s1, s3 = not st.last, st.s3
                c = [Chunk(st, k) for k in range(NK + 1)]
                if not st.first:
                    end_a(st)
                if s1:
                    ch1 = Chain(dve, c_dve2, S1_LINKS, st.u + 1)
                    dt_first(st)
                if not st.first:
                    end_b(st)
                if s1:
                    dt_last(st, ch1)
                    taps(st, "c4", ch1)
                chunk_b2(c[0])
                if st.first:
                    low_weights(1, late_w)
                if s1:
                    taps(st, "c0", ch1)
                chunk_a(c[1])
                if s1:
                    silu_x(st, "c4")
                g_low(c[0])
                if s3:
                    ch3 = s3_stats(st)
                chunk_mix(c[1])
                chunk_b1(c[1])
                if s1:
                    silu_x(st, "c0")
                    taps(st, "c1", ch1)
                if s1 and not s3:
                    taps(st, "c2", ch1)
                chunk_b2(c[1])
                if s1 and s3:
                    taps(st, "c2", ch1)
                if s1:
                    silu_x(st, "c1")
                chunk_a(c[2])
                if s3:
                    s3_apply(st)
                if s1:
                    silu_x(st, "c2")
                g_low(c[1])
                chunk_mix(c[2])
                chunk_b1(c[2])
                if s1:
                    taps(st, "c3", ch1)
                    ch1.close()
                if s1:
                    ln_stats(st.u + 2, st.h + 1, st.q)
                chunk_b2(c[2])
                if s1:
                    z_gate(st, 0)
                chunk_a(c[3])
                if s1:
                    silu_x(st, "c3")
                g_low(c[2])
                chunk_mix(c[3])
                chunk_b1(c[3])
                if s3:
                    s3_top(st, ch3)
                if s1:
                    z_gate(st, 1)
                if s1:
                    ln_apply(st.u + 2, st.q)
                chunk_b2(c[3])
                if s1:
                    z_gate(st, 2)
                    chunk_a(c[4])
                if s3:
                    s3_place(st, ch3)
                g_low(c[3])
                if s1:
                    chunk_mix(c[4])
                if s1:
                    u_lows(st)
                    z_gate(st, 3)

            def low_parts(n):
                dve.wait_ge(high0, n + 1)
                for a, b, scale in quarter(n):
                    ins = dve.scalar_tensor_tensor(w_split[:, 0, 1, a:b], w_raw[:, a:b], scale, w_split[:, 0, 0, a:b],
                                                   ALU.mult, ALU.subtract)
                if n == 3:
                    ins.then_inc(w_have, 1)

            def prologue(st):
                ch1 = Chain(dve, c_dve2, S1_LINKS, 0)
                for d in range(KD):
                    bank, before = st.fill(f"ln{d}")
                    u_low(0, 0, d, bank, before + 1)
                dt_first(st)
                ln_stats(1, 0, 1)
                dt_last(st, ch1)
                taps(st, "c4", ch1)
                ln_apply(1, 1)
                for c, then in zip(CONV_ORDER, CONV_ORDER[1:]):
                    taps(st, then, ch1)
                    silu_x(st, c)
                silu_x(st, CONV_ORDER[-1])
                ch1.close()
                for k in range(NK - 1):
                    z_gate(st, k)
                chunk_a(Chunk(st, NK))
                for d in range(KD):
                    bank, before = st.fill(f"ln{d}n")
                    u_low(1, 1, d, bank, before + 1)
                chunk_mix(Chunk(st, NK))
                z_gate(st, NK - 1)

            def epilogue(st):
                end_a(st)
                end_b(st)
                ch3 = s3_stats(st)
                low_parts(0)
                s3_apply(st)
                low_parts(1)
                low_parts(2)
                s3_top(st, ch3)
                low_parts(3)
                s3_place(st, ch3)

            S1_LINKS = 1 + NC * (TAPS - 2)
            dve.wait_ge(consts, N_CONSTS)
            ln_stats(0, 0, 0)
            ln_apply(0, 0)
            dve.wait_ge(params, 16 * N_PARAMS)
            dve.tensor_scalar(cw, cw, 0.5 / S1, None, ALU.mult)
            dve.tensor_scalar(cb, cb, 0.5, None, ALU.mult)
            dve.tensor_scalar(rmsw, rmsw, S2 / (2 * S1 * SG), None, ALU.mult).then_inc(c_prep, 1)
            dve.wait_ge(c_prep, 2)
            dve.tensor_scalar(aneg, aneg, -1.0, None, ALU.mult)
            for l in range(2):
                for c in range(NCT):
                    ins = dve.tensor_scalar(wout_raw[l][:, c, :], wout_raw[l][:, c, :], rmsw[:, l, c:c + 1], None, ALU.mult)
                ins.then_inc(c_prep, 1)

            def low_weights(l, done):
                dve.wait_ge(high_w, 2 * l + 1)
                dve.scalar_tensor_tensor(win[:, l, 1], win_raw[:, l], S1, win[:, l, 0], ALU.mult, ALU.subtract)
                dve.wait_ge(high_w, 2 * l + 2)
                dve.tensor_tensor(wout[:, l, 1], wout_raw[l], wout[:, l, 0], ALU.subtract).then_inc(done, 1)

            low_weights(0, prepared)
            dve.wait_ge(prepared, 1)
            schedule(dve, body, prologue, epilogue)

            at = [0]

            def step(ins):
                at[0] += 1
                ins.then_inc(c_plan, 1)
                dve.wait_ge(c_plan, at[0])

            def cells(ap, n=NJT):
                return ap.unsqueeze(2).to_broadcast([1, n, NE])

            jr, jd = jrow[0:1, :], jdum[0:1, :]
            row_f, e_f = plan_f[0:1, 0:NJT], plan_f[0:1, NJT:2 * NJT]
            par_f, len_f = plan_f[0:1, 2 * NJT:3 * NJT], plan_f[0:1, 3 * NJT:3 * NJT + NE]
            step(dve.tensor_scalar(j128, jrow[:, 0:NTILE], float(P), None, ALU.mult))
            step(dve.tensor_tensor(cnt, count[:, :], qbase[:, :], ALU.subtract))
            dve.tensor_copy(len_f, cnt[0:1, :])
            step(dve.tensor_tensor(tcmp, cnt.unsqueeze(2).to_broadcast([P, NE, NTILE]),
                                   j128.unsqueeze(1).to_broadcast([P, NE, NTILE]), ALU.is_gt))
            step(dve.tensor_reduce(nt, tcmp, AX.X, ALU.add))
            step(dve.tensor_copy(end[0:1, 0:1], nt[0:1, 0:1]))
            for e in range(1, NE):
                step(dve.tensor_tensor(end[0:1, e:e + 1], end[0:1, e - 1:e], nt[0:1, e:e + 1], ALU.add))
            step(dve.tensor_tensor(cmp_[0:1], cells(jr), end[0:1].unsqueeze(1).to_broadcast([1, NJT, NE]), ALU.is_ge))
            dve.tensor_reduce(e_f, cmp_[0:1, :, 0:NE - 1], AX.X, ALU.add)
            dve.tensor_scalar(usedj[0:1], cmp_[0:1, :, NE - 1], -1.0, 1.0, ALU.mult, ALU.add)
            step(dve.tensor_tensor(cmp_nt[0:1], cmp_[0:1], nt[0:1].unsqueeze(1).to_broadcast([1, NJT, NE]), ALU.mult))
            dve.tensor_reduce(stj[0:1], cmp_nt[0:1], AX.X, ALU.add)
            step(dve.tensor_tensor(cmp_[0:1], cmp_[0:1], sign[0:1, :].unsqueeze(1).to_broadcast([1, NJT, NE]), ALU.mult))
            step(dve.tensor_reduce(ej[0:1], cmp_[0:1, :, 0:NE - 1], AX.X, ALU.add))
            NG = NJT // WB
            par, packed = ej[0:1].rearrange("p (g r) -> p g r", r=WB), par_f[:, 0:NG]
            step(dve.tensor_copy(packed, par[:, :, 0]))
            for m in range(1, WB):
                step(dve.scalar_tensor_tensor(packed, par[:, :, m], float(1 << m), packed, ALU.mult, ALU.add))
            step(dve.scalar_tensor_tensor(packed[:, 1:NG], par[:, 0:NG - 1, WB - 1], float(1 << WB), packed[:, 1:NG],
                                          ALU.mult, ALU.add))
            step(dve.tensor_tensor(tmpj[0:1], jr, stj[0:1], ALU.subtract))
            step(dve.tensor_scalar(tmpj[0:1], tmpj[0:1], float(P), None, ALU.mult))
            step(dve.scalar_tensor_tensor(tmpj[0:1], e_f, float(QROWS), tmpj[0:1], ALU.mult, ALU.add))
            step(dve.tensor_tensor(tmpj[0:1], tmpj[0:1], jd, ALU.subtract))
            step(dve.tensor_tensor(tmpj[0:1], tmpj[0:1], usedj[0:1], ALU.mult))
            dve.tensor_copy(plan_f[0:1, 3 * NJT + NE:3 * NJT + 2 * NE], end[0:1, :])
            step(dve.tensor_tensor(usedj[0:1, 0:NJ], jrow[0:1, 0:NJ], end[0:1, NE - 2:NE - 1].to_broadcast([1, NJ]),
                                   ALU.is_lt))
            dve.tensor_reduce(plan_f[0:1, 3 * NJT + 2 * NE:], usedj[0:1, 0:NJ].rearrange("p (g r) -> p r g", r=WB),
                              AX.X, ALU.add)
            step(dve.tensor_tensor(row_f, tmpj[0:1], jd, ALU.add))
            dve.tensor_copy(plan_i[0:1, :], plan_f[0:1, :]).then_inc(plan_done, 1)
            step(dve.tensor_scalar(moved, nt[:, 0:NE - 1], float(P), -float(QROWS), ALU.mult, ALU.add))
            for s in range(2):
                step(dve.tensor_tensor(behind, route[:, :, 2 + s].unsqueeze(2).to_broadcast([P, NTILE, NE - 1]),
                                       qbase[:, 1:NE].unsqueeze(1).to_broadcast([P, NTILE, NE - 1]), ALU.is_ge))
                step(dve.tensor_tensor(behind, behind, moved.unsqueeze(1).to_broadcast([P, NTILE, NE - 1]), ALU.mult))
                step(dve.tensor_reduce(shift, behind, AX.X, ALU.add))
                step(dve.tensor_tensor(rows_u[:, :, s], route[:, :, 2 + s], shift, ALU.add))
            row1, row2 = rows_u[:, :, 0], rows_u[:, :, 1]
            dve.tensor_tensor(swap, row1, row2, ALU.is_gt)
            dve.tensor_tensor(keep, row2, row1, ALU.is_gt)
            dve.tensor_tensor(rows_lh[:, 0], row1, row2, ALU.min)
            step(dve.tensor_tensor(rows_lh[:, 1], row1, row2, ALU.max))
            dve.tensor_copy(slot_low, rows_lh[:, 0]).then_inc(low_rows, 1)
            for s, (first, second) in enumerate(((keep, swap), (swap, keep))):
                dve.tensor_tensor(w_part, first, route[:, :, 0], ALU.mult)
                step(dve.tensor_tensor(w_lh[:, :, s], second, route[:, :, 1], ALU.mult))
                step(dve.tensor_tensor(w_lh[:, :, s], w_lh[:, :, s], w_part, ALU.add))
            dve.sem_inc(low_rows, 1)

            dve.sem_inc(o_ready, 1)

            def rows_low(i, r):
                dve.wait_ge(xh_ready, WB * i + (r + 1))
                dve.tensor_tensor(xl[:, r % WB].rearrange("p d t -> p (d t)"), pt[:, 0:KD * P],
                                  xh[:, r % WB].rearrange("p d t -> p (d t)"), ALU.subtract).then_inc(x_done, 1)

            def gated(i, r):
                j = WB * i + r
                ex_ = dve.value_load(plan_i[0:1, bass.ds(WB * i + (r + NJT), 1)], min_val=0, max_val=NE - 1)
                for half in range(2):
                    dve.wait_ge(f_full[2 * half + 1], j + 1)
                    dve.wait_ge(silu_done[half], j + 1)
                    dve.sem_inc(hop, 1)
                    for f in range(4):
                        ff = 4 * half + f
                        ins = dve.scalar_tensor_tensor(glu[:, half, f * P:(f + 1) * P], VALUE[half][:, f * P:(f + 1) * P],
                                                       b1v[:, bass.ds(ex_, 1), ff], sg[:, half, f, :],
                                                       ALU.add, ALU.mult)
                    ins.then_inc(c_glu, 1)
                    dve.wait_ge(c_glu, 4 * j + 2 * half + 2)
                    high = acth[:, r, 4 * half:4 * half + 4].rearrange("p f t -> p (f t)")
                    dve.tensor_copy(high, glu[:, half]).then_inc(c_glu, 1)
                    dve.wait_ge(c_glu, 4 * j + 2 * half + 3)
                    dve.tensor_tensor(actl[:, r, 4 * half:4 * half + 4].rearrange("p f t -> p (f t)"), glu[:, half],
                                      high, ALU.subtract).then_inc(act_done, 1)

            def result(i, r, first):
                b = r % WB
                ex_ = dve.value_load(plan_i[0:1, bass.ds(WB * i + (r + NJT), 1)], min_val=0, max_val=NE - 1)
                dve.wait_ge(o_full, WB * i + (r + 1))
                if not first:
                    dve.wait_ge(ans_out[b], 16 * i)
                dve.sem_inc(hop, 1)
                dve.scalar_tensor_tensor(yt[:, b], py[:, 0:D], 1.0 / (S1 * S2),
                                         b2a[:, bass.ds(ex_, 1), :].rearrange("p o d -> p (o d)"),
                                         ALU.mult, ALU.add).then_inc(o_ready, 1)

            rows_low(0, 0)
            dve.wait_ge(bias_in, 32)
            dve.tensor_scalar(b1v, b1a[:, :, 0:NF], S1, None, ALU.mult).then_inc(c_glu, 1)
            dve.wait_ge(c_glu, 1)
            for r in range(WB):
                gated(0, r)
                rows_low(0, r + 1)
                if r > 0:
                    result(0, r - 1, True)
            gated(1, 0)
            rows_low(1, 1)
            result(0, WB - 1, True)
            for r in range(1, WB):
                gated(1, r)
                rows_low(1, r + 1)
                result(1, r - 1, False)
            with dve.Fori(2, NJ // WB) as i:
                for r in range(WB):
                    gated(i, r)
                    rows_low(i, r + 1)
                    result(i - 1 if r == 0 else i, (r - 1) % WB, False)
            result(NJ // WB - 1, WB - 1, False)

            def slots(i, q):
                dve.tensor_copy(slot_c[:, q], rows_lh[:, 1, bass.ds(LG * (2 * i + q), LG)]).then_inc(idx_ready, 1)

            def finish(i, q, ahead):
                ch = Chain(dve, c_fin, 4, 2 * i + q)
                ch.link(dve.tensor_copy(wv[:, q], w_lh[:, bass.ds(LG * (2 * i + q), LG), :]))
                dve.wait_ge(got[q], 16 * LG * (i + 1))
                dve.sem_inc(hop, 1)
                if ahead:
                    slots(i + 1, q)
                for k in range(LG):
                    low = got_low[:, bass.ds(LG * (2 * i + q) + k, 1), :].rearrange("p o d -> p (o d)")
                    ins = dve.scalar_tensor_tensor(fsum[:, q, k], got_high[:, q, k], wv[:, q, k, 1:2], low,
                                                   ALU.mult, ALU.add)
                ins.then_inc(f_sum, 1)
                dve.wait_ge(f_sum, 2 * i + (q + 1))
                for k in range(LG):
                    ins = dve.bn_stats(fst[:, q, k], fsum[:, q, k])
                ch.link(ins)
                dve.sem_inc(hop, 1)
                for k in range(LG):
                    ins = dve.bn_aggr(fmv[:, q, k], fst[:, q, k])
                ch.link(ins)
                dve.tensor_scalar(fve[:, q], fmv[:, q, :, 1], EPS, None, ALU.add).then_inc(f_var, 1)
                dve.wait_ge(f_rs, 2 * i + (q + 1))
                ch.link(dve.reciprocal(frs[:, q], fsd[:, q]))
                dve.scalar_tensor_tensor(fnb[:, q], fmv[:, q, :, 0], -1.0, frs[:, q], ALU.mult, ALU.mult
                                         ).then_inc(f_scale, 1)
                ch.close()

            dve.wait_ge(low_sum, 1)
            for q in range(2):
                slots(0, q)
            for q in range(2):
                finish(0, q, True)
            with dve.Fori(1, NB // 2 - 1) as i:
                for q in range(2):
                    finish(i, q, True)
            for q in range(2):
                finish(NB // 2 - 1, q, False)

        @block.gpsimd
        def _(pool):
            own = [0]

            def next_(ins):
                own[0] += 1
                ins.then_inc(c_pool, 1)
                pool.wait_ge(c_pool, own[0])

            next_(pool.memset(zeros[:, :], 0.0))
            for s in range(2):
                row = DUMMY + s * P
                pool.dma_start(queue[row:row + P, :], zeros[:, :]).then_inc(scattered[s], 16)
            next_(pool.memset(ones[:, :], 1.0))
            pool.memset(half_neg[:, :], -0.5)
            pool.iota(sign_i[:, :], [[0, NE // 2], [-2, 2]], base=1, channel_multiplier=0)
            pool.iota(jrow_i[:, :], [[1, NJT]], base=0, channel_multiplier=0)
            next_(pool.iota(jdum_i[:, :], [[0, NJT // WB], [P, WB]], base=DUMMY, channel_multiplier=0))
            pool.tensor_copy(sign[:, :], sign_i[:, :])
            pool.tensor_copy(jrow[:, :], jrow_i[:, :])
            next_(pool.tensor_copy(jdum[:, :], jdum_i[:, :]))
            pool.tensor_copy(iota_e[:, :], jrow[:, 0:NE])
            pool.tensor_scalar(qbase[:, :], jrow[:, 0:NE], float(QROWS), 0.0, ALU.mult, ALU.add)
            pool.tensor_scalar(count[:, :], jrow[:, 0:NE], float(QROWS), 0.0, ALU.mult, ALU.add)
            pool.affine_select(out=tri_le[:, :], in_=ones[:, :], compare_op=ALU.is_ge, fill=0.0, base=0,
                               pattern=[[1, P]], channel_multiplier=-1)
            pool.affine_select(out=tri_lt[:, :], in_=ones[:, :], compare_op=ALU.is_gt, fill=0.0, base=0,
                               pattern=[[1, P]], channel_multiplier=-1)
            pool.affine_select(out=tri_gt[:, :], in_=ones[:, :], compare_op=ALU.is_gt, fill=0.0, base=0,
                               pattern=[[-1, P]], channel_multiplier=1)
            next_(pool.affine_select(out=ident[:, :], in_=ones[:, :], compare_op=ALU.is_equal, fill=0.0, base=0,
                                     pattern=[[-1, P]], channel_multiplier=1))
            pool.sem_inc(consts, 1)

            def by_head(ap):
                return ap.unsqueeze(2).to_broadcast([ap.shape[0], NH, HD])

            def load_weights(e):
                for n in range(4):
                    if n > 0 and e > 0:
                        pool.wait_ge(w_raw_in, 16 * (4 * e + n))
                    a, b = n * WEX // 4, (n + 1) * WEX // 4
                    pool.dma_start(w_raw[:, a:b], w_exp[e, :, a:b]).then_inc(w_raw_in, 16)

            def split(e):
                p = e % 2
                for n in range(4):
                    for a, b, scale in quarter(n):
                        raw, high, low = w_raw[:, a:b], w_split[:, p, 0, a:b], w_split[:, p, 1, a:b]
                        pool.tensor_scalar(high, raw, scale, 0.0, ALU.mult, ALU.add)
                        next_(pool.tensor_scalar(raw, raw, scale, 0.0, ALU.mult, ALU.add))
                        ins = pool.tensor_tensor(low, raw, high, ALU.subtract)
                next_(ins)
                pool.sem_inc(w_have, 1)

            def rsqrt_ln(w):
                pool.wait_ge(ln_var, w + 1)
                pool.tensor_tensor(rs, ve, half_neg[:, :], ALU.pow).then_inc(ln_rs, 1)

            def end(st):
                pool.wait_ge(sve_ready, st.u)
                pool.tensor_tensor(srs, sve, half_neg[:, :], ALU.pow).then_inc(srs_ready, 1)

            def add_x(st):
                wq = 1 - st.q
                pool.wait_ge(h_ready, st.u)
                pool.tensor_tensor(hres[:, wq], ob[:, wq], hres[:, wq], ALU.add).then_inc(hx_ready, 1)

            def rsqrt_x1(st):
                pool.wait_ge(r_var, st.u - NB)
                pool.tensor_tensor(rrs, rve, half_neg[:, :], ALU.pow).then_inc(r_rs, 1)

            def scatter(m, mq, first, end_):
                if first == 0:
                    pool.wait_ge(slot_ready, m + 1)
                    pool.sem_inc(hop, 1)
                for n in range(first, end_):
                    pool.indirect_dma_start(queue, bass.IndirectOffsetOnAxis(ap=slot[:, mq, n:n + 1], axis=0),
                                            x1b[:, mq, n % NK, :], None).then_inc(scattered[mq], 16)

            def scatter_before(st, first, end_):
                if st.s3 and not (isinstance(st.u, int) and st.u == NB + 1):
                    scatter(st.u - NB - 2, st.q, first, end_)

            def operands(c):
                q, n, k, kq, u6 = c.q, c.n, c.k, c.kq, c.u6
                pool.wait_ge(pt_free, c.use("a") + 1)
                at_least(pool, y_full, n - 1)
                pool.tensor_tensor(dtx[:, kq], xs[:, kq], by_head(dt_s[:, q, k]), ALU.mult).then_inc(dtx_ready, 1)
                if k < NK - 1:
                    pool.wait_ge(wdt_ready, n + 1)
                    at_least(pool, z_full, (u6 + 1) if k == 2 else (u6 - 1 - 2 * k))
                    pool.tensor_tensor(xw[:, kq], xs[:, kq], by_head(wdt[:, kq]), ALU.mult).then_inc(xw_ready, 1)
                at_least(pool, y_free, n - 1)
                pool.tensor_tensor(xd[:, kq], xs[:, kq], by_head(dsk[:, c.layer]), ALU.mult).then_inc(xd_ready, 1)
                if k in (1, 2):
                    pool.wait_ge(z_free, u6 + 2 * k - 1)
                    pool.tensor_tensor(state_d[0:DS], state[0:DS, (k - 1) % 2], by_head(ex[0:DS, kq, 2]),
                                       ALU.mult).then_inc(sd_ready, 1)

            def add_xd(c):
                pool.wait_ge(z_free, c.u6 + 2 * c.k)
                pool.wait_ge(xd_ready, c.n + 1)
                pool.tensor_tensor(y1[:, c.kq], y1[:, c.kq], xd[:, c.kq], ALU.add).then_inc(ysum_ready, 1)

            def gated(c):
                n, k, kq = c.n, c.k, c.kq
                pool.wait_ge(y_free, n + 1)
                at_least(pool, ss_ready, n - 1)
                before = {0: -1, 1: 1, 2: 3, 3: 5}[k]
                if isinstance(c.u, int) and c.u == 0 and k < 2:
                    before = 0
                at_least(pool, pt_free, 8 * c.u + before if before or k >= 2 else 0)
                pool.tensor_tensor(g[:, kq], y2[:, kq], zs[:, c.q, k].rearrange("p (h d) -> p h d", h=NH),
                                   ALU.mult).then_inc(g_ready, 1)

            def body(st):
                c = [Chunk(st, k) for k in range(NK + 1)]
                if not st.first:
                    end(st)
                if st.last:
                    for s in range(2):
                        pool.wait_ge(a_free[s], LAST_HB)
                    load_weights(0)
                gated(c[0])
                operands(c[1])
                if not st.first and not st.s3:
                    add_x(st)
                add_xd(c[1])
                if st.s3:
                    rsqrt_x1(st)
                scatter_before(st, 0, 2)
                gated(c[1])
                operands(c[2])
                add_xd(c[2])
                if not st.last:
                    rsqrt_ln(st.u + 2)
                scatter_before(st, 2, 4)
                gated(c[2])
                operands(c[3])
                add_xd(c[3])
                scatter_before(st, 4, 6)
                gated(c[3])
                if not st.last:
                    operands(c[4])
                scatter_before(st, 6, 8)

            def prologue(st):
                rsqrt_ln(1)
                operands(Chunk(st, NK))

            def epilogue(st):
                end(st)
                scatter(NB - 2, 0, 0, 4)
                rsqrt_x1(st)
                scatter(NB - 2, 0, 4, 2 * NK)
                scatter(NB - 1, 1, 0, 2 * NK)

            rsqrt_ln(0)
            schedule(pool, body, prologue, epilogue)

            for e in range(1, NE):
                if e == 1:
                    pool.wait_ge(plan_done, 1)
                    for s in range(2):
                        pool.wait_ge(scattered[s], 16 * 2 * NK * (NB // 2) + 16)
                        pool.wait_ge(stored[s], 16 * NB + 16)
                    for b in range(WB):
                        pool.wait_ge(xq_in[b], 16)
                load_weights(e)
                if e >= 2:
                    end_e = pool.value_load(plan_i[0:1, 3 * NJT + NE + e - 2:3 * NJT + NE + e - 1], min_val=0, max_val=NJ)
                    pool.wait_ge(o_ready, end_e + 1)
                    pool.sem_inc(hop, 1)
                pool.wait_ge(w_raw_in, 64 * (e + 1))
                split(e)

            pool.wait_ge(low_rows, 1)
            for s in range(WB):
                at = 3 * NJT + 2 * NE + s
                tiles = pool.value_load(plan_i[0:1, at:at + 1], min_val=NTILE // WB, max_val=NJ // WB)
                pool.wait_ge(ans_out[s], 16 * tiles)
                pool.sem_inc(hop, 1)
            for b in range(NB):
                pool.dma_start(x1_all[:, b * NK:(b + 1) * NK], x1_rows[b * T:(b + 1) * T, :].rearrange(
                    "(k p) d -> p k d", p=P)).then_inc(x1_back, 16)
            for t in range(NTILE):
                pool.indirect_dma_start(got_low[:, t, :], None, answer,
                                        bass.IndirectOffsetOnAxis(ap=slot_low[:, t:t + 1], axis=0)
                                        ).then_inc(low_got, 16)
            pool.wait_ge(low_rows, 2)
            pool.wait_ge(low_got, 16 * NTILE)
            next_(pool.tensor_tensor(got_low, got_low, w_lh[:, :, 0:1].to_broadcast([P, NTILE, D]), ALU.mult))
            pool.wait_ge(x1_back, 16 * NB)
            pool.tensor_tensor(got_low, got_low, x1_all, ALU.add).then_inc(low_sum, 1)

            for s in range(WB):
                pool.wait_ge(ans_out[s], 16 * (NJ // WB))

            def gather(i, q, first):
                pool.wait_ge(idx_ready, 2 * i + (q + 1))
                if not first:
                    pool.wait_ge(f_sum, 2 * i + (q - 1))
                pool.sem_inc(hop, 1)
                for k in range(LG):
                    pool.indirect_dma_start(got_high[:, q, k, :], None, answer,
                                            bass.IndirectOffsetOnAxis(ap=slot_c[:, q, k:k + 1], axis=0)
                                            ).then_inc(got[q], 16)

            for q in range(2):
                gather(0, q, True)
            with pool.Fori(1, NB // 2) as i:
                for q in range(2):
                    gather(i, q, False)


def kernel(**inputs):
    import numpy as _np
    import concourse.bacc as _bacc
    from concourse import mybir as _mybir
    from concourse.bass_utils import run_bass_kernel_spmd as _run

    def get(name):
        return _np.asarray(inputs["L0_" + name])

    def columns(a, tiles):
        a = a.reshape((a.shape[0], tiles, P) + a.shape[2:])
        return _np.moveaxis(a, 2, 0)

    def by_partition(a, tiles):
        return a.reshape(NE, tiles, P, -1).transpose(0, 2, 1, 3).reshape(NE, P, -1)

    laid = {
        "x": get("attn_x"),
        "w_in": get("attn_in_proj_w").transpose(0, 2, 1),
        "conv_w": columns(get("attn_conv_w"), NC),
        "conv_b": columns(get("attn_conv_b"), NC),
        "ln_w": columns(get("attn_ln_w"), KD),
        "ln_b": columns(get("attn_ln_b"), KD),
        "dt_bias": get("attn_dt_bias"),
        "a_log": get("attn_A_log"),
        "d_skip": get("attn_D"),
        "rms_w": columns(get("attn_rms_w"), NCT),
        "w_out": get("attn_out_proj_w").transpose(0, 2, 1),
        "gate_w": get("ffn_gate_w"),
        "gate_b": get("ffn_gate_b"),
        "w_exp": _np.concatenate([by_partition(get("ffn_w1"), KD), by_partition(get("ffn_w2"), NF)], axis=2),
        "b1": get("ffn_b1").reshape(NE, 2 * NF, P).transpose(2, 0, 1),
        "b2": get("ffn_b2"),
    }
    nc = _bacc.Bacc("TRN2", target_bir_lowering=False, num_devices=1)
    arrays, args = {}, []
    for name, a in laid.items():
        a = _np.ascontiguousarray(a)
        arrays[f"in_{name}"] = a
        args.append(nc.dram_tensor(f"in_{name}", a.shape, _mybir.dt.from_np(a.dtype), kind="ExternalInput").ap())
    args.append(nc.dram_tensor("out_0", (NTOK, D), F32, kind="ExternalOutput").ap())
    build(nc, *args)
    r = _run(nc, [arrays], core_ids=[0])
    return r.results[0]["out_0"].reshape(NB, T, D)
```
